# Optimizing a Trainium2 kernel written in Bass

```python
import numpy as np
import jax
import jax.numpy as jnp

def _softmax(x, axis=-1):
    return jax.nn.softmax(x, axis=axis)

def _gelu(x):
    return jax.nn.gelu(x, approximate=True)

def _silu(x):
    return jax.nn.silu(x)

def _sigmoid(x):
    return jax.nn.sigmoid(x)

def _layernorm(x, axis=-1, eps=1e-05):
    m = jnp.mean(x, axis=axis, keepdims=True)
    v = jnp.var(x, axis=axis, keepdims=True)
    return (x - m) / jnp.sqrt(v + eps)

def _scatter_add(tgt, idx, src, axis=0):
    return tgt.at[idx].add(src)

def _segment_sum(src, seg, n):
    return jax.ops.segment_sum(src, seg, n)
kernel_name = 'mk_hybrid_d2_jaxref_r8_e91162'

def setup_inputs(seed: int=0):
    np.random.seed(seed)
    _w = jnp.asarray

    def _L0_attn_a_setup():
        import jax, jax.numpy as jnp
        import numpy as np
        N_HEAD = 16
        NEG_INF = jnp.finfo(jnp.float32).min
        key = jax.random.key(seed)
        k1, k2, k3, k4 = jax.random.split(key, 4)
        B, T, C = (4, 256, 128)
        x = jax.random.normal(k1, (B, T, C), dtype=jnp.float32)
        w_attn = jax.random.normal(k2, (C, 3 * C), dtype=jnp.float32) * C ** (-0.5)
        w_proj = jax.random.normal(k3, (C, C), dtype=jnp.float32) * C ** (-0.5)
        decay_raw = jax.random.normal(k4, (N_HEAD,), dtype=jnp.float32)
        return {'x': x, 'w_attn': w_attn, 'w_proj': w_proj, 'decay_raw': decay_raw}
    _L0_attn_a_in = _L0_attn_a_setup()

    def _L0_attn_b_setup():
        import jax, jax.numpy as jnp
        import numpy as np
        B, T, D, H, LORA = (4, 128, 128, 16, 64)
        HD = D // H
        BLOCK_ID, N_BLOCKS = (6, 12)

        def _ln(x, w, b, eps=1e-05):
            m = x.mean(-1, keepdims=True)
            v = ((x - m) ** 2).mean(-1, keepdims=True)
            return (x - m) * jax.lax.rsqrt(v + eps) * w + b

        def _lora(z, a, b, l):
            return l + jnp.tanh(z @ a.T) @ b.T

        def _reference_tuple_inner(x, xw, rW, kW, vW, gW, r_la, r_lb, r_ll, k_la, k_lb, k_ll, v_la, v_lb, v_ll, g_la, g_lb, g_ll, d_la, d_lb, d_ll, ln_w, ln_b, oW, init_state, u):
            b, t, d = x.shape
            h = init_state.shape[0]
            hd = d // h
            xx = jnp.concatenate([jnp.zeros_like(x[:, :1]), x[:, :-1]], axis=1)
            dx = xx - x
            lerpx = x + dx * xw
            r = (x + dx * _lora(lerpx, r_la, r_lb, r_ll)) @ rW.T
            k = (x + dx * _lora(lerpx, k_la, k_lb, k_ll)) @ kW.T
            v = (x + dx * _lora(lerpx, v_la, v_lb, v_ll)) @ vW.T
            g = (x + dx * _lora(lerpx, g_la, g_lb, g_ll)) @ gW.T
            w = jnp.exp(-jnp.exp(_lora(x + dx * _lora(lerpx, d_la, d_lb, d_ll), d_la, d_lb, d_ll)))
            split = lambda z: z.reshape(b, t, h, hd).transpose(1, 0, 2, 3)
            rs, ws, ks, vs = (split(r), split(w), split(k), split(v))
            uh = u.reshape(h, hd)
            st0 = jnp.broadcast_to(init_state, (b, h, hd, hd))

            def step(st, inp):
                rt, wt, kt, vt = inp
                kv = jnp.einsum('bhi,bhj->bhij', kt, vt)
                y = jnp.einsum('bhi,bhij->bhj', rt, st + uh[None, :, :, None] * kv)
                return (wt[..., None] * st + kv, y)
            st1, ys = jax.lax.scan(step, st0, (rs, ws, ks, vs))
            o = jax.nn.silu(g.reshape(b, t, h, hd)) * _ln(ys.transpose(1, 0, 2, 3), ln_w, ln_b)
            return (o.reshape(b, t, d) @ oW.T, st1)
        key = jax.random.key(seed)
        ks = iter(jax.random.split(key, 64))
        rn = lambda shape, s: jax.random.normal(next(ks), shape, jnp.float32) * s
        inp = {}
        inp['x'] = rn((B, T, D), 1.0)
        r1 = 1.0 - BLOCK_ID / N_BLOCKS
        i = np.arange(D)
        inp['xw'] = jnp.asarray(1.0 - (i / D) ** r1, jnp.float32)
        for nm in ('rW', 'kW', 'vW', 'gW'):
            inp[nm] = rn((D, D), 0.02)
        for p in ('r', 'k', 'v', 'g', 'd'):
            inp[p + '_la'] = rn((LORA, D), 0.001)
            inp[p + '_lb'] = rn((D, LORA), 0.001)
            inp[p + '_ll'] = rn((D,), 1.0)
        inp['ln_w'] = jnp.full((HD,), ((1 + BLOCK_ID) / N_BLOCKS) ** 0.7, jnp.float32)
        inp['ln_b'] = jnp.zeros((HD,), jnp.float32)
        inp['oW'] = rn((D, D), 0.02)
        inp['init_state'] = rn((H, HD, HD), 1.0)
        r0 = BLOCK_ID / (N_BLOCKS - 1)
        ih = i % HD
        inp['u'] = jnp.asarray(r0 * (1 - ih / (D - 1)) + np.remainder(0.1 * (ih + 1), 3.0), jnp.float32)
        return inp
    _L0_attn_b_in = _L0_attn_b_setup()

    def _L0_ffn_setup():
        import jax, jax.numpy as jnp
        import numpy as np
        import math
        D_MODEL = 128
        D_FF = 512
        NUM_EXPERTS = 8
        NUM_SHARED = 1
        E_ROUTED = NUM_EXPERTS - NUM_SHARED
        TOP_K = 2
        CAP_FACTOR = 1.25
        B, S = (4, 256)
        T = B * S
        CAPACITY = math.ceil(CAP_FACTOR * T * TOP_K / E_ROUTED)
        SHARED_SCALE = 1.0

        def _layernorm(x, g, b, eps=1e-05):
            mu = jnp.mean(x, axis=-1, keepdims=True)
            var = jnp.mean((x - mu) ** 2, axis=-1, keepdims=True)
            return (x - mu) * jax.lax.rsqrt(var + eps) * g + b
        key = jax.random.key(seed)
        ks = jax.random.split(key, 10)
        s = 0.02
        return {'x': jax.random.normal(ks[0], (B, S, D_MODEL), dtype=jnp.float32), 'ln_g': jnp.ones((D_MODEL,), jnp.float32), 'ln_b': jnp.zeros((D_MODEL,), jnp.float32), 'Wr': jax.random.normal(ks[1], (D_MODEL, E_ROUTED), jnp.float32) * s, 'W1': jax.random.normal(ks[2], (E_ROUTED, D_MODEL, D_FF), jnp.float32) * s, 'W3': jax.random.normal(ks[3], (E_ROUTED, D_MODEL, D_FF), jnp.float32) * s, 'W2': jax.random.normal(ks[4], (E_ROUTED, D_FF, D_MODEL), jnp.float32) * s, 'W1s': jax.random.normal(ks[5], (D_MODEL, D_FF), jnp.float32) * s, 'W3s': jax.random.normal(ks[6], (D_MODEL, D_FF), jnp.float32) * s, 'W2s': jax.random.normal(ks[7], (D_FF, D_MODEL), jnp.float32) * s}
    _L0_ffn_in = _L0_ffn_setup()

    def _L1_attn_a_setup():
        import jax, jax.numpy as jnp
        import numpy as np
        DIM = 128
        NUM_HEADS = 16
        DIM_HEAD = 64
        INNER = NUM_HEADS * DIM_HEAD

        def rotate_half(t):
            x1, x2 = jnp.split(t, 2, axis=-1)
            return jnp.concatenate([-x2, x1], axis=-1)

        def rope_pos(n, d, dtype=jnp.float32):
            inv_freq = 1.0 / 10000.0 ** (jnp.arange(0, d, 2, dtype=jnp.float32) / d)
            freqs = jnp.arange(n, dtype=jnp.float32)[:, None] * inv_freq[None, :]
            return jnp.concatenate([freqs, freqs], axis=-1).astype(dtype)

        def apply_rope(pos, t):
            return t * jnp.cos(pos) + rotate_half(t) * jnp.sin(pos)
        key = jax.random.key(seed)
        k1, k2, k3, k4 = jax.random.split(key, 4)
        b, n = (2, 256)
        x = jax.random.normal(k1, (b, n, DIM), dtype=jnp.float32)
        s = DIM ** (-0.5)
        Wq = jax.random.normal(k2, (DIM, INNER), dtype=jnp.float32) * s
        Wkv = jax.random.normal(k3, (DIM, 2 * DIM_HEAD), dtype=jnp.float32) * s
        Wo = jax.random.normal(k4, (INNER, DIM), dtype=jnp.float32) * INNER ** (-0.5)
        return {'x': x, 'Wq': Wq, 'Wkv': Wkv, 'Wo': Wo}
    _L1_attn_a_in = _L1_attn_a_setup()

    def _L1_attn_b_setup():
        import jax, jax.numpy as jnp
        import numpy as np
        NUM_HEADS = 8
        SCALE_BASE = 512.0
        GN_EPS = 1e-05

        def rotate_every_two(x):
            x1 = x[..., ::2]
            x2 = x[..., 1::2]
            return jnp.stack([-x2, x1], axis=-1).reshape(x.shape)

        def xpos_apply(x, downscale):
            L, D = (x.shape[1], x.shape[2])
            half = D // 2
            scale_vec = (jnp.arange(0, D, 2, dtype=jnp.float32) + 0.4 * D) / (1.4 * D)
            pos = jnp.arange(L, dtype=jnp.float32)
            scale = scale_vec[None, :] ** (pos[:, None] / SCALE_BASE)
            inv_freq = 1.0 / 10000.0 ** (jnp.arange(half, dtype=jnp.float32) / half)
            sinusoid = pos[:, None] * inv_freq[None, :]
            sin, cos = (jnp.sin(sinusoid), jnp.cos(sinusoid))
            if downscale:
                scale = 1.0 / scale
            sin_s = jnp.repeat(sin * scale, 2, axis=-1)
            cos_s = jnp.repeat(cos * scale, 2, axis=-1)
            return x * cos_s + rotate_every_two(x) * sin_s

        def decay_mask_fn(T, num_heads):
            s, e = (np.log(1.0 / 32.0), np.log(1.0 / 512.0))
            gamma = 1.0 - jnp.exp(jnp.linspace(s, e, num_heads).astype(jnp.float32))
            log_decay = jnp.log(gamma)
            idx = jnp.arange(T)
            expo = (idx[:, None] - idx[None, :]).astype(jnp.float32)
            tri = idx[:, None] >= idx[None, :]
            expo_safe = jnp.where(tri, expo, 0.0)
            mask = jnp.exp(log_decay[:, None, None] * expo_safe) * tri
            scale = jnp.sqrt(mask.sum(axis=-1, keepdims=True))
            return mask / scale

        def _reference_tuple_inner(hidden_states, w_qkv, b_qkv, w_g, b_g, w_p, b_p):
            B, T, E = hidden_states.shape
            H = NUM_HEADS
            V = 2 * E
            dk, dv = (E // H, V // H)
            qkv = hidden_states @ w_qkv + b_qkv
            q, k, v = (qkv[..., :E], qkv[..., E:2 * E], qkv[..., 2 * E:])
            q = xpos_apply(q, downscale=False)
            k = xpos_apply(k, downscale=True)
            q = q.reshape(B, T, H, dk).transpose(0, 2, 1, 3)
            k = k.reshape(B, T, H, dk).transpose(0, 2, 1, 3)
            v = v.reshape(B, T, H, dv).transpose(0, 2, 1, 3)
            mask = decay_mask_fn(T, H)
            retention = jnp.einsum('bhid,bhjd->bhij', q, k) * dk ** (-0.5)
            retention = retention * mask[None]
            out = jnp.einsum('bhij,bhjv->bhiv', retention, v)
            curr_kv = jnp.einsum('hj,bhjk,bhjv->bhkv', mask[:, -1, :], k, v)
            retention_out = out.transpose(0, 2, 1, 3).reshape(B, T, V)
            g = retention_out.reshape(B * T, H, dv)
            mu = g.mean(axis=-1, keepdims=True)
            var = ((g - mu) ** 2).mean(axis=-1, keepdims=True)
            normed = ((g - mu) / jnp.sqrt(var + GN_EPS)).reshape(B, T, V)
            gated = jax.nn.silu(hidden_states @ w_g + b_g) * normed
            proj = gated @ w_p + b_p
            return (proj, curr_kv)
        key = jax.random.key(seed)
        ks = jax.random.split(key, 4)
        B, T, E = (2, 256, 128)
        V = 2 * E
        return {'hidden_states': jax.random.normal(ks[0], (B, T, E), dtype=jnp.float32), 'w_qkv': jax.random.normal(ks[1], (E, 2 * E + V), dtype=jnp.float32) * 0.02, 'b_qkv': jnp.zeros((2 * E + V,), dtype=jnp.float32), 'w_g': jax.random.normal(ks[2], (E, V), dtype=jnp.float32) * 0.02, 'b_g': jnp.zeros((V,), dtype=jnp.float32), 'w_p': jax.random.normal(ks[3], (V, E), dtype=jnp.float32) * 0.02, 'b_p': jnp.zeros((E,), dtype=jnp.float32)}
    _L1_attn_b_in = _L1_attn_b_setup()

    def _L1_ffn_setup():
        import jax, jax.numpy as jnp
        import numpy as np
        B, S, H = (2, 512, 128)
        E, K, I = (8, 2, 176)
        key = jax.random.key(seed)
        ks = jax.random.split(key, 9)
        sc = 0.02
        return {'hidden_states': jax.random.normal(ks[0], (B, S, H), jnp.float32), 'gate_w': jax.random.normal(ks[1], (E, H), jnp.float32) * sc, 'w_gate': jax.random.normal(ks[2], (E, H, I), jnp.float32) * sc, 'w_up': jax.random.normal(ks[3], (E, H, I), jnp.float32) * sc, 'w_down': jax.random.normal(ks[4], (E, I, H), jnp.float32) * sc, 'sw_gate': jax.random.normal(ks[5], (H, I), jnp.float32) * sc, 'sw_up': jax.random.normal(ks[6], (H, I), jnp.float32) * sc, 'sw_down': jax.random.normal(ks[7], (I, H), jnp.float32) * sc, 'shared_gate_w': jax.random.normal(ks[8], (1, H), jnp.float32) * sc}
    _L1_ffn_in = _L1_ffn_setup()
    _d = {'L0_attn_a_x': _L0_attn_a_in['x'], 'L0_attn_a_w_attn': _L0_attn_a_in['w_attn'], 'L0_attn_a_w_proj': _L0_attn_a_in['w_proj'], 'L0_attn_a_decay_raw': _L0_attn_a_in['decay_raw'], 'L0_attn_b_xw': _L0_attn_b_in['xw'], 'L0_attn_b_rW': _L0_attn_b_in['rW'], 'L0_attn_b_kW': _L0_attn_b_in['kW'], 'L0_attn_b_vW': _L0_attn_b_in['vW'], 'L0_attn_b_gW': _L0_attn_b_in['gW'], 'L0_attn_b_r_la': _L0_attn_b_in['r_la'], 'L0_attn_b_r_lb': _L0_attn_b_in['r_lb'], 'L0_attn_b_r_ll': _L0_attn_b_in['r_ll'], 'L0_attn_b_k_la': _L0_attn_b_in['k_la'], 'L0_attn_b_k_lb': _L0_attn_b_in['k_lb'], 'L0_attn_b_k_ll': _L0_attn_b_in['k_ll'], 'L0_attn_b_v_la': _L0_attn_b_in['v_la'], 'L0_attn_b_v_lb': _L0_attn_b_in['v_lb'], 'L0_attn_b_v_ll': _L0_attn_b_in['v_ll'], 'L0_attn_b_g_la': _L0_attn_b_in['g_la'], 'L0_attn_b_g_lb': _L0_attn_b_in['g_lb'], 'L0_attn_b_g_ll': _L0_attn_b_in['g_ll'], 'L0_attn_b_d_la': _L0_attn_b_in['d_la'], 'L0_attn_b_d_lb': _L0_attn_b_in['d_lb'], 'L0_attn_b_d_ll': _L0_attn_b_in['d_ll'], 'L0_attn_b_ln_w': _L0_attn_b_in['ln_w'], 'L0_attn_b_ln_b': _L0_attn_b_in['ln_b'], 'L0_attn_b_oW': _L0_attn_b_in['oW'], 'L0_attn_b_init_state': _L0_attn_b_in['init_state'], 'L0_attn_b_u': _L0_attn_b_in['u'], 'L0_ffn_ln_g': _L0_ffn_in['ln_g'], 'L0_ffn_ln_b': _L0_ffn_in['ln_b'], 'L0_ffn_Wr': _L0_ffn_in['Wr'], 'L0_ffn_W1': _L0_ffn_in['W1'], 'L0_ffn_W3': _L0_ffn_in['W3'], 'L0_ffn_W2': _L0_ffn_in['W2'], 'L0_ffn_W1s': _L0_ffn_in['W1s'], 'L0_ffn_W3s': _L0_ffn_in['W3s'], 'L0_ffn_W2s': _L0_ffn_in['W2s'], 'L1_attn_a_Wq': _L1_attn_a_in['Wq'], 'L1_attn_a_Wkv': _L1_attn_a_in['Wkv'], 'L1_attn_a_Wo': _L1_attn_a_in['Wo'], 'L1_attn_b_w_qkv': _L1_attn_b_in['w_qkv'], 'L1_attn_b_b_qkv': _L1_attn_b_in['b_qkv'], 'L1_attn_b_w_g': _L1_attn_b_in['w_g'], 'L1_attn_b_b_g': _L1_attn_b_in['b_g'], 'L1_attn_b_w_p': _L1_attn_b_in['w_p'], 'L1_attn_b_b_p': _L1_attn_b_in['b_p'], 'L1_ffn_gate_w': _L1_ffn_in['gate_w'], 'L1_ffn_w_gate': _L1_ffn_in['w_gate'], 'L1_ffn_w_up': _L1_ffn_in['w_up'], 'L1_ffn_w_down': _L1_ffn_in['w_down'], 'L1_ffn_sw_gate': _L1_ffn_in['sw_gate'], 'L1_ffn_sw_up': _L1_ffn_in['sw_up'], 'L1_ffn_sw_down': _L1_ffn_in['sw_down'], 'L1_ffn_shared_gate_w': _L1_ffn_in['shared_gate_w']}
    _x0 = _d['L0_attn_a_x']
    _d['L0_attn_a_x'] = jax.random.normal(jax.random.fold_in(jax.random.key(seed), 1), (4, 512, 128), dtype=_x0.dtype)
    del _x0
    return _d

def reference(L0_attn_a_x, L0_attn_a_w_attn, L0_attn_a_w_proj, L0_attn_a_decay_raw, L0_attn_b_xw, L0_attn_b_rW, L0_attn_b_kW, L0_attn_b_vW, L0_attn_b_gW, L0_attn_b_r_la, L0_attn_b_r_lb, L0_attn_b_r_ll, L0_attn_b_k_la, L0_attn_b_k_lb, L0_attn_b_k_ll, L0_attn_b_v_la, L0_attn_b_v_lb, L0_attn_b_v_ll, L0_attn_b_g_la, L0_attn_b_g_lb, L0_attn_b_g_ll, L0_attn_b_d_la, L0_attn_b_d_lb, L0_attn_b_d_ll, L0_attn_b_ln_w, L0_attn_b_ln_b, L0_attn_b_oW, L0_attn_b_init_state, L0_attn_b_u, L0_ffn_ln_g, L0_ffn_ln_b, L0_ffn_Wr, L0_ffn_W1, L0_ffn_W3, L0_ffn_W2, L0_ffn_W1s, L0_ffn_W3s, L0_ffn_W2s, L1_attn_a_Wq, L1_attn_a_Wkv, L1_attn_a_Wo, L1_attn_b_w_qkv, L1_attn_b_b_qkv, L1_attn_b_w_g, L1_attn_b_b_g, L1_attn_b_w_p, L1_attn_b_b_p, L1_ffn_gate_w, L1_ffn_w_gate, L1_ffn_w_up, L1_ffn_w_down, L1_ffn_sw_gate, L1_ffn_sw_up, L1_ffn_sw_down, L1_ffn_shared_gate_w):

    def _L0_attn_a_ref(x, w_attn, w_proj, decay_raw):
        import jax, jax.numpy as jnp
        import numpy as np
        N_HEAD = 16
        NEG_INF = jnp.finfo(jnp.float32).min
        B, T, C = x.shape
        H = N_HEAD
        D = C // H
        qkv = x @ w_attn
        q, k, v = jnp.split(qkv, 3, axis=-1)
        q = q.reshape(B, T, H, D).transpose(0, 2, 1, 3)
        k = k.reshape(B, T, H, D).transpose(0, 2, 1, 3)
        v = v.reshape(B, T, H, D).transpose(0, 2, 1, 3)
        idx = jnp.arange(T)
        causal = jnp.where(idx[None, :] > idx[:, None], NEG_INF, 0.0).astype(jnp.float32)
        decay = jax.nn.softplus(decay_raw)
        dist = jnp.maximum(idx[:, None] - idx[None, :], 0).astype(jnp.float32)
        log1p_dist = jnp.log1p(dist)
        logw = -jnp.log1p(decay[:, None, None] * log1p_dist)
        attn_mask = causal[None, :, :] + logw
        scores = jnp.einsum('bhqd,bhkd->bhqk', q, k) * (1.0 / jnp.sqrt(jnp.float32(D)))
        scores = scores + attn_mask[None]
        att = jax.nn.softmax(scores, axis=-1)
        y = jnp.einsum('bhqk,bhkd->bhqd', att, v)
        y = y.transpose(0, 2, 1, 3).reshape(B, T, C)
        return y @ w_proj

    def _L0_attn_b_ref(x, xw, rW, kW, vW, gW, r_la, r_lb, r_ll, k_la, k_lb, k_ll, v_la, v_lb, v_ll, g_la, g_lb, g_ll, d_la, d_lb, d_ll, ln_w, ln_b, oW, init_state, u):
        import jax, jax.numpy as jnp
        import numpy as np
        B, T, D, H, LORA = (4, 128, 128, 16, 64)
        HD = D // H
        BLOCK_ID, N_BLOCKS = (6, 12)

        def _ln(x, w, b, eps=1e-05):
            m = x.mean(-1, keepdims=True)
            v = ((x - m) ** 2).mean(-1, keepdims=True)
            return (x - m) * jax.lax.rsqrt(v + eps) * w + b

        def _lora(z, a, b, l):
            return l + jnp.tanh(z @ a.T) @ b.T

        def _reference_tuple_inner(x, xw, rW, kW, vW, gW, r_la, r_lb, r_ll, k_la, k_lb, k_ll, v_la, v_lb, v_ll, g_la, g_lb, g_ll, d_la, d_lb, d_ll, ln_w, ln_b, oW, init_state, u):
            b, t, d = x.shape
            h = init_state.shape[0]
            hd = d // h
            xx = jnp.concatenate([jnp.zeros_like(x[:, :1]), x[:, :-1]], axis=1)
            dx = xx - x
            lerpx = x + dx * xw
            r = (x + dx * _lora(lerpx, r_la, r_lb, r_ll)) @ rW.T
            k = (x + dx * _lora(lerpx, k_la, k_lb, k_ll)) @ kW.T
            v = (x + dx * _lora(lerpx, v_la, v_lb, v_ll)) @ vW.T
            g = (x + dx * _lora(lerpx, g_la, g_lb, g_ll)) @ gW.T
            w = jnp.exp(-jnp.exp(_lora(x + dx * _lora(lerpx, d_la, d_lb, d_ll), d_la, d_lb, d_ll)))
            split = lambda z: z.reshape(b, t, h, hd).transpose(1, 0, 2, 3)
            rs, ws, ks, vs = (split(r), split(w), split(k), split(v))
            uh = u.reshape(h, hd)
            st0 = jnp.broadcast_to(init_state, (b, h, hd, hd))

            def step(st, inp):
                rt, wt, kt, vt = inp
                kv = jnp.einsum('bhi,bhj->bhij', kt, vt)
                y = jnp.einsum('bhi,bhij->bhj', rt, st + uh[None, :, :, None] * kv)
                return (wt[..., None] * st + kv, y)
            st1, ys = jax.lax.scan(step, st0, (rs, ws, ks, vs))
            o = jax.nn.silu(g.reshape(b, t, h, hd)) * _ln(ys.transpose(1, 0, 2, 3), ln_w, ln_b)
            return (o.reshape(b, t, d) @ oW.T, st1)
        return _reference_tuple_inner(x, xw, rW, kW, vW, gW, r_la, r_lb, r_ll, k_la, k_lb, k_ll, v_la, v_lb, v_ll, g_la, g_lb, g_ll, d_la, d_lb, d_ll, ln_w, ln_b, oW, init_state, u)[0]

    def _L0_ffn_ref(x, ln_g, ln_b, Wr, W1, W3, W2, W1s, W3s, W2s):
        import jax, jax.numpy as jnp
        import numpy as np
        import math
        D_MODEL = 128
        D_FF = 512
        NUM_EXPERTS = 8
        NUM_SHARED = 1
        E_ROUTED = NUM_EXPERTS - NUM_SHARED
        TOP_K = 2
        CAP_FACTOR = 1.25
        B, S = (4, 256)
        T = B * S
        CAPACITY = math.ceil(CAP_FACTOR * T * TOP_K / E_ROUTED)
        SHARED_SCALE = 1.0

        def _layernorm(x, g, b, eps=1e-05):
            mu = jnp.mean(x, axis=-1, keepdims=True)
            var = jnp.mean((x - mu) ** 2, axis=-1, keepdims=True)
            return (x - mu) * jax.lax.rsqrt(var + eps) * g + b
        Bx, Sx, D = x.shape
        Tn = Bx * Sx
        h = _layernorm(x, ln_g, ln_b).reshape(Tn, D)
        logits = h @ Wr
        top_vals, top_idx = jax.lax.top_k(logits, TOP_K)
        gates = jax.nn.softmax(top_vals, axis=-1)
        idx = top_idx.T.reshape(-1)
        gat = gates.T.reshape(-1)
        tok = jnp.tile(jnp.arange(Tn), TOP_K)
        onehot = jax.nn.one_hot(idx, E_ROUTED, dtype=jnp.int32)
        pos = jnp.sum(jnp.cumsum(onehot, axis=0) * onehot, axis=-1) - 1
        keep = pos < CAPACITY
        pos_c = jnp.where(keep, pos, CAPACITY)
        xe = jnp.zeros((E_ROUTED, CAPACITY, D), h.dtype).at[idx, pos_c].set(h[tok], mode='drop')
        a = jnp.einsum('ecd,edf->ecf', xe, W1)
        b = jnp.einsum('ecd,edf->ecf', xe, W3)
        ye = jnp.einsum('ecf,efd->ecd', jax.nn.silu(a) * b, W2)
        out_slots = ye[jnp.clip(idx, 0, E_ROUTED - 1), jnp.clip(pos_c, 0, CAPACITY - 1)]
        out_slots = out_slots * (gat * keep.astype(gat.dtype))[:, None]
        routed = jnp.zeros((Tn, D), h.dtype).at[tok].add(out_slots)
        shared = jax.nn.silu(h @ W1s) * (h @ W3s) @ W2s
        out = routed + SHARED_SCALE * shared
        return out.reshape(Bx, Sx, D)

    def _L1_attn_a_ref(x, Wq, Wkv, Wo):
        import jax, jax.numpy as jnp
        import numpy as np
        DIM = 128
        NUM_HEADS = 16
        DIM_HEAD = 64
        INNER = NUM_HEADS * DIM_HEAD

        def rotate_half(t):
            x1, x2 = jnp.split(t, 2, axis=-1)
            return jnp.concatenate([-x2, x1], axis=-1)

        def rope_pos(n, d, dtype=jnp.float32):
            inv_freq = 1.0 / 10000.0 ** (jnp.arange(0, d, 2, dtype=jnp.float32) / d)
            freqs = jnp.arange(n, dtype=jnp.float32)[:, None] * inv_freq[None, :]
            return jnp.concatenate([freqs, freqs], axis=-1).astype(dtype)

        def apply_rope(pos, t):
            return t * jnp.cos(pos) + rotate_half(t) * jnp.sin(pos)
        b, n, _ = x.shape
        scale = DIM_HEAD ** (-0.5)
        q = x @ Wq
        kv = x @ Wkv
        k, v = jnp.split(kv, 2, axis=-1)
        q = q.reshape(b, n, NUM_HEADS, DIM_HEAD).transpose(0, 2, 1, 3)
        pos = rope_pos(n, DIM_HEAD, x.dtype)
        q = apply_rope(pos, q)
        k = apply_rope(pos, k)
        q = q * scale
        sim = jnp.einsum('bhid,bjd->bhij', q, k)
        causal = jnp.triu(jnp.ones((n, n), dtype=bool), k=1)
        neg = -jnp.finfo(sim.dtype).max
        sim = jnp.where(causal, neg, sim)
        sim = sim - jnp.max(sim, axis=-1, keepdims=True)
        attn = jax.nn.softmax(sim, axis=-1)
        out = jnp.einsum('bhij,bjd->bhid', attn, v)
        out = out.transpose(0, 2, 1, 3).reshape(b, n, INNER)
        return out @ Wo

    def _L1_attn_b_ref(hidden_states, w_qkv, b_qkv, w_g, b_g, w_p, b_p):
        import jax, jax.numpy as jnp
        import numpy as np
        NUM_HEADS = 8
        SCALE_BASE = 512.0
        GN_EPS = 1e-05

        def rotate_every_two(x):
            x1 = x[..., ::2]
            x2 = x[..., 1::2]
            return jnp.stack([-x2, x1], axis=-1).reshape(x.shape)

        def xpos_apply(x, downscale):
            L, D = (x.shape[1], x.shape[2])
            half = D // 2
            scale_vec = (jnp.arange(0, D, 2, dtype=jnp.float32) + 0.4 * D) / (1.4 * D)
            pos = jnp.arange(L, dtype=jnp.float32)
            scale = scale_vec[None, :] ** (pos[:, None] / SCALE_BASE)
            inv_freq = 1.0 / 10000.0 ** (jnp.arange(half, dtype=jnp.float32) / half)
            sinusoid = pos[:, None] * inv_freq[None, :]
            sin, cos = (jnp.sin(sinusoid), jnp.cos(sinusoid))
            if downscale:
                scale = 1.0 / scale
            sin_s = jnp.repeat(sin * scale, 2, axis=-1)
            cos_s = jnp.repeat(cos * scale, 2, axis=-1)
            return x * cos_s + rotate_every_two(x) * sin_s

        def decay_mask_fn(T, num_heads):
            s, e = (np.log(1.0 / 32.0), np.log(1.0 / 512.0))
            gamma = 1.0 - jnp.exp(jnp.linspace(s, e, num_heads).astype(jnp.float32))
            log_decay = jnp.log(gamma)
            idx = jnp.arange(T)
            expo = (idx[:, None] - idx[None, :]).astype(jnp.float32)
            tri = idx[:, None] >= idx[None, :]
            expo_safe = jnp.where(tri, expo, 0.0)
            mask = jnp.exp(log_decay[:, None, None] * expo_safe) * tri
            scale = jnp.sqrt(mask.sum(axis=-1, keepdims=True))
            return mask / scale

        def _reference_tuple_inner(hidden_states, w_qkv, b_qkv, w_g, b_g, w_p, b_p):
            B, T, E = hidden_states.shape
            H = NUM_HEADS
            V = 2 * E
            dk, dv = (E // H, V // H)
            qkv = hidden_states @ w_qkv + b_qkv
            q, k, v = (qkv[..., :E], qkv[..., E:2 * E], qkv[..., 2 * E:])
            q = xpos_apply(q, downscale=False)
            k = xpos_apply(k, downscale=True)
            q = q.reshape(B, T, H, dk).transpose(0, 2, 1, 3)
            k = k.reshape(B, T, H, dk).transpose(0, 2, 1, 3)
            v = v.reshape(B, T, H, dv).transpose(0, 2, 1, 3)
            mask = decay_mask_fn(T, H)
            retention = jnp.einsum('bhid,bhjd->bhij', q, k) * dk ** (-0.5)
            retention = retention * mask[None]
            out = jnp.einsum('bhij,bhjv->bhiv', retention, v)
            curr_kv = jnp.einsum('hj,bhjk,bhjv->bhkv', mask[:, -1, :], k, v)
            retention_out = out.transpose(0, 2, 1, 3).reshape(B, T, V)
            g = retention_out.reshape(B * T, H, dv)
            mu = g.mean(axis=-1, keepdims=True)
            var = ((g - mu) ** 2).mean(axis=-1, keepdims=True)
            normed = ((g - mu) / jnp.sqrt(var + GN_EPS)).reshape(B, T, V)
            gated = jax.nn.silu(hidden_states @ w_g + b_g) * normed
            proj = gated @ w_p + b_p
            return (proj, curr_kv)
        return _reference_tuple_inner(hidden_states, w_qkv, b_qkv, w_g, b_g, w_p, b_p)[0]

    def _L1_ffn_ref(hidden_states, gate_w, w_gate, w_up, w_down, sw_gate, sw_up, sw_down, shared_gate_w):
        import jax, jax.numpy as jnp
        import numpy as np
        B, S, H = (2, 512, 128)
        E, K, I = (8, 2, 176)
        b, s, h = hidden_states.shape
        x = hidden_states.reshape(-1, h)
        logits = jnp.einsum('th,eh->te', x, gate_w)
        probs = jax.nn.softmax(logits.astype(jnp.float32), axis=-1)
        topk_w, topk_i = jax.lax.top_k(probs, K)
        topk_w = topk_w / jnp.sum(topk_w, axis=-1, keepdims=True)
        combine = jnp.sum(jax.nn.one_hot(topk_i, E, dtype=topk_w.dtype) * topk_w[..., None], axis=1)
        combine = combine.astype(x.dtype)
        g = jnp.einsum('th,ehi->eti', x, w_gate)
        u = jnp.einsum('th,ehi->eti', x, w_up)
        eo = jnp.einsum('eti,eih->eth', jax.nn.silu(g) * u, w_down)
        out = jnp.einsum('te,eth->th', combine, eo)
        sg = jax.nn.sigmoid(jnp.einsum('th,oh->to', x, shared_gate_w))
        so = jax.nn.silu(x @ sw_gate) * (x @ sw_up) @ sw_down
        out = out + sg * so
        return out.reshape(b, s, h)
    x = L0_attn_a_x
    x = x + _L0_attn_a_ref(_layernorm(x, axis=-1), L0_attn_a_w_attn, L0_attn_a_w_proj, L0_attn_a_decay_raw)
    x = x + _L0_ffn_ref(_layernorm(x, axis=-1), L0_ffn_ln_g, L0_ffn_ln_b, L0_ffn_Wr, L0_ffn_W1, L0_ffn_W3, L0_ffn_W2, L0_ffn_W1s, L0_ffn_W3s, L0_ffn_W2s)
    x = x + _L0_attn_b_ref(_layernorm(x, axis=-1), L0_attn_b_xw, L0_attn_b_rW, L0_attn_b_kW, L0_attn_b_vW, L0_attn_b_gW, L0_attn_b_r_la, L0_attn_b_r_lb, L0_attn_b_r_ll, L0_attn_b_k_la, L0_attn_b_k_lb, L0_attn_b_k_ll, L0_attn_b_v_la, L0_attn_b_v_lb, L0_attn_b_v_ll, L0_attn_b_g_la, L0_attn_b_g_lb, L0_attn_b_g_ll, L0_attn_b_d_la, L0_attn_b_d_lb, L0_attn_b_d_ll, L0_attn_b_ln_w, L0_attn_b_ln_b, L0_attn_b_oW, L0_attn_b_init_state, L0_attn_b_u)
    x = x + _L0_ffn_ref(_layernorm(x, axis=-1), L0_ffn_ln_g, L0_ffn_ln_b, L0_ffn_Wr, L0_ffn_W1, L0_ffn_W3, L0_ffn_W2, L0_ffn_W1s, L0_ffn_W3s, L0_ffn_W2s)
    x = x + _L1_attn_a_ref(_layernorm(x, axis=-1), L1_attn_a_Wq, L1_attn_a_Wkv, L1_attn_a_Wo)
    x = x + _L1_ffn_ref(_layernorm(x, axis=-1), L1_ffn_gate_w, L1_ffn_w_gate, L1_ffn_w_up, L1_ffn_w_down, L1_ffn_sw_gate, L1_ffn_sw_up, L1_ffn_sw_down, L1_ffn_shared_gate_w)
    x = x + _L1_attn_b_ref(_layernorm(x, axis=-1), L1_attn_b_w_qkv, L1_attn_b_b_qkv, L1_attn_b_w_g, L1_attn_b_b_g, L1_attn_b_w_p, L1_attn_b_b_p)
    x = x + _L1_ffn_ref(_layernorm(x, axis=-1), L1_ffn_gate_w, L1_ffn_w_gate, L1_ffn_w_up, L1_ffn_w_down, L1_ffn_sw_gate, L1_ffn_sw_up, L1_ffn_sw_down, L1_ffn_shared_gate_w)
    return x

_drawn_inputs = setup_inputs


def setup_inputs(seed=0):
    import zlib

    import numpy as np

    out = dict(_drawn_inputs(seed))
    spreads = {'L0_attn_b_ln_w': (0.6857119798660278, 0.6),
     'L0_attn_b_ln_b': (0.0, 0.8),
     'L0_ffn_ln_g': (1.0, 0.6),
     'L0_ffn_ln_b': (0.0, 0.8),
     'L1_attn_b_b_qkv': (0.0, 0.1),
     'L1_attn_b_b_g': (0.0, 0.559),
     'L1_attn_b_b_p': (0.0, 0.1)}
    factors = {'L0_attn_b_xw': 8.0,
     'L0_attn_b_r_la': 28.032,
     'L0_attn_b_r_lb': 8.0,
     'L0_attn_b_k_la': 23.592,
     'L0_attn_b_k_lb': 25.012,
     'L0_attn_b_v_la': 43.46,
     'L0_attn_b_v_lb': 43.779,
     'L0_attn_b_g_la': 8.0,
     'L0_attn_b_g_lb': 23.575,
     'L0_attn_b_d_la': 64.0,
     'L0_attn_b_d_lb': 64.0,
     'L0_attn_b_d_ll': 4.434,
     'L0_attn_b_init_state': 8.0,
     'L0_attn_b_u': 8.0,
     'L0_ffn_Wr': 4.113,
     'L0_ffn_W1': 3.75,
     'L0_ffn_W3': 3.716,
     'L0_ffn_W2': 3.714,
     'L1_ffn_gate_w': 7.05,
     'L1_ffn_w_gate': 6.153,
     'L1_ffn_w_up': 6.105,
     'L1_ffn_w_down': 6.099,
     'L1_ffn_sw_gate': 8.0,
     'L1_ffn_sw_up': 8.0,
     'L1_ffn_sw_down': 8.0,
     'L1_ffn_shared_gate_w': 8.0,
     'L1_attn_b_w_g': 2.797}
    for name, (base, spread) in spreads.items():
        noise = np.random.default_rng([zlib.crc32(name.encode()), seed]).standard_normal(out[name].shape)
        drawn = base * np.exp(spread * noise) if base else spread * noise
        out[name] = jnp.asarray(drawn.astype(out[name].dtype))
    for name, factor in factors.items():
        out[name] = (out[name] * factor).astype(out[name].dtype)
    return out
```

```python
from contextlib import ExitStack

import concourse.bass as bass
from concourse import mybir

F32 = mybir.dt.float32
BF16 = mybir.dt.bfloat16
ALU = mybir.AluOpType
ACT = mybir.ActivationFunctionType
AX = mybir.AxisListType

P = 128
B, T = 4, 512
TPB = T // P
NT = B * TPB
EPS = 1e-5
LEAD = 8
LAYERS = (1, 2, 3, 4, 5, 6, 7, 8)

A_HEADS, A_HD = 16, 8
W_HEADS, W_HD, LORA = 16, 8, 64
FF0_EXPERTS, FF0_DIM = 7, 512
FF0_CAPACITY = -(-5 * (B * T // 2) * 2 // (4 * FF0_EXPERTS))
M_HEADS, M_HD = 16, 64
FF1_EXPERTS, FF1_DIM = 8, 176
R_HEADS, R_DK, R_DV = 8, 16, 32
MASKED = -1e30


class Room:

    def __init__(self, nc, ctx):
        self.nc, self.ctx = nc, ctx

    def sb(self, name, shape, dt=F32):
        return self.ctx.enter_context(self.nc.sbuf_tensor(name, shape, dt, allow_name_mangling=True))

    def ps(self, name, shape, dt=F32):
        return self.ctx.enter_context(self.nc.psum_tensor(name, shape, dt, allow_name_mangling=True))


class Signal:

    def __init__(self, nc, ctx, name):
        self.sem = ctx.enter_context(nc.semaphore(name))
        self.base = LEAD

    def at(self, n):
        return self.base + n

    def passed(self, n):
        self.base += n


class Steps:

    def __init__(self, engine, signal):
        self.engine, self.own_count, self.n = engine, signal, 0
        self.turn, self.per = None, 0

    def link(self, ins):
        self.n += 1
        ins.then_inc(self.own_count.sem, 1)
        n = self.n if self.turn is None else self.turn * self.per + self.n
        self.engine.wait_ge(self.own_count.sem, self.own_count.base + n)

    def enter(self, turn, per):
        self.turn, self.per, self.entered = turn, per, self.n

    def leave(self, turns):
        assert self.n - self.entered == self.per, (self.n - self.entered, self.per)
        self.n = self.entered + self.per * turns
        self.turn = None

    def close(self):
        self.own_count.passed(self.n)


def stand_alone(engine, signal):
    engine.sem_inc(signal.sem, 1)


def norm_transpose(nc, S, X, xnT, ident, twice=False, gain=None, shift=None):
    rounds = 2 if twice else 1
    with ExitStack() as ctx:
        room = Room(nc, ctx)
        xn = room.sb("xn", [P, NT, P], F32)
        stats = room.sb("stats", [P, TPB, 6], F32)
        mv = room.sb("mv", [P, TPB, 2], F32)
        ve = room.sb("ve", [P, TPB], F32)
        sd = room.sb("sd", [P, TPB], F32)
        rs = room.sb("rs", [P, TPB], F32)
        tp = room.ps("tp", [P, B, T], F32)
        var_ready, std_ready, norm_ready, turned = S["var"], S["std"], S["norm"], S["turned"]
        block = ctx.enter_context(nc.Block())

        @block.vector
        def _(dve):
            own = Steps(dve, S["dve"])
            for r in range(rounds):
                src = X if r == 0 else xn
                if r:
                    dve.wait_ge(norm_ready.sem, norm_ready.at(r * B))
                for b in range(B):
                    for t in range(TPB):
                        ins = nc.vector.bn_stats(stats[:, t, :], src[:, b * TPB + t, :])
                    own.link(ins)
                    for t in range(TPB):
                        ins = nc.vector.bn_aggr(mv[:, t, :], stats[:, t, :])
                    own.link(ins)
                    nc.vector.tensor_scalar(ve[:, :], mv[:, :, 1], EPS, None, ALU.add).then_inc(var_ready.sem, 1)
                    dve.wait_ge(std_ready.sem, std_ready.at(r * B + b + 1))
                    own.link(nc.vector.reciprocal(rs[:, :], sd[:, :]))
                    for t in range(TPB):
                        ins = nc.vector.tensor_scalar(xn[:, b * TPB + t, :], src[:, b * TPB + t, :],
                                                      mv[:, t, 0:1], rs[:, t:t + 1], ALU.subtract, ALU.mult)
                    ins.then_inc(norm_ready.sem, 1)
            own.close()

        @block.scalar
        def _(act):
            for r in range(rounds):
                for b in range(B):
                    act.wait_ge(var_ready.sem, var_ready.at(r * B + b + 1))
                    nc.scalar.activation(sd[:, :], ve[:, :], ACT.Sqrt).then_inc(std_ready.sem, 1)
            for b in range(B):
                act.wait_ge(turned.sem, turned.at(b + 1))
                dst = xnT[:, b * T:(b + 1) * T]
                if gain is None:
                    nc.scalar.activation(dst, tp[:, b, :], ACT.Copy)
                else:
                    nc.scalar.activation(dst, tp[:, b, :], ACT.Identity, bias=shift, scale=gain)

        @block.tensor
        def _(pe):
            for b in range(B):
                pe.wait_ge(norm_ready.sem, norm_ready.at((rounds - 1) * B + b + 1))
                for t in range(TPB):
                    ins = nc.tensor.transpose(tp[:, b, t * P:(t + 1) * P], xn[:, b * TPB + t, :], ident[:, :])
                ins.then_inc(turned.sem, 1)

    for s in (var_ready, std_ready, norm_ready):
        s.passed(rounds * B)
    turned.passed(B)


def project_add(nc, S, X, Y, W, ident, KT, bias_row=None, ones_row=None):
    with ExitStack() as ctx:
        room = Room(nc, ctx)
        yT = room.sb("yT", [P, 2, KT * P], F32)
        tp = room.ps("tp", [P, 2, max(KT * P, 512)], F32)
        op = room.ps("op", [P, 2, 512], F32)
        turned, copied, ready, added = S["turned"], S["copied"], S["pready"], S["padded"]
        block = ctx.enter_context(nc.Block())

        @block.tensor
        def _(pe):
            def transposes(n):
                if n >= 2:
                    pe.wait_ge(copied.sem, copied.at(n - 1))
                for k in range(KT):
                    ins = nc.tensor.transpose(tp[:, n % 2, k * P:(k + 1) * P], Y[:, n, k * P:(k + 1) * P], ident[:, :])
                ins.then_inc(turned.sem, 1)

            transposes(0)
            for n in range(NT):
                if n + 1 < NT:
                    transposes(n + 1)
                pe.wait_ge(copied.sem, copied.at(n + 1))
                if n >= 2:
                    pe.wait_ge(added.sem, added.at(n - 1))
                for k in range(KT):
                    ins = nc.tensor.matmul(op[:, n % 2, 0:P], yT[:, n % 2, k * P:(k + 1) * P], W[:, k, :],
                                           start=(k == 0), stop=(k == KT - 1 and bias_row is None))
                if bias_row is not None:
                    ins = nc.tensor.matmul(op[:, n % 2, 0:P], ones_row, bias_row, start=False, stop=True)
                ins.then_inc(ready.sem, 1)

        @block.scalar
        def _(act):
            for n in range(NT):
                act.wait_ge(turned.sem, turned.at(n + 1))
                if n >= 2:
                    act.wait_ge(ready.sem, ready.at(n - 1))
                for half in range(-(-KT * P // 512)):
                    lo, hi = half * 512, min(KT * P, half * 512 + 512)
                    ins = nc.scalar.activation(yT[:, n % 2, lo:hi], tp[:, n % 2, lo:hi], ACT.Copy)
                ins.then_inc(copied.sem, 1)

        @block.vector
        def _(dve):
            for n in range(NT):
                dve.wait_ge(ready.sem, ready.at(n + 1))
                nc.vector.tensor_tensor(X[:, n, :], X[:, n, :], op[:, n % 2, 0:P], ALU.add).then_inc(added.sem, 1)

    for s in (turned, copied, ready, added):
        s.passed(NT)


def split3(own, nc, value, rest, hi, mid, lo):
    own.link(nc.vector.tensor_copy(hi, value))
    own.link(nc.vector.tensor_tensor(rest, value, hi, ALU.subtract))
    own.link(nc.vector.tensor_copy(mid, rest))
    return nc.vector.tensor_tensor(lo, rest, mid, ALU.subtract)


def route(nc, S, xnT, Wr, E, extra, capacity, gateT, C):
    EX = E + 1
    with ExitStack() as ctx:
        room = Room(nc, ctx)
        lg, l2 = room.sb("lg", [P, NT, 8]), room.sb("l2", [P, NT, 8])
        cand, m1 = room.sb("cand", [P, NT, 8]), room.sb("m1", [P, NT])
        v1, v2, ex, den, sg = room.sb("v1", [P, NT]), room.sb("v2", [P, NT]), room.sb("ex", [P, NT]), room.sb("den", [P, NT]), room.sb("sg", [P, NT])
        o = room.sb("o", [P, 2 * NT, 8])
        g = room.sb("g", [P, 2 * NT])
        ob = room.sb("ob", [P, 2 * NT, 8], BF16)
        run_a, run_b, pos = room.sb("run_a", [P, 2 * NT, 8]), room.sb("run_b", [P, 2 * NT, 8]), room.sb("pos", [P, 2 * NT, 8])
        comb = room.sb("comb", [P, NT, 9])
        rest = room.sb("rest", [P, NT, 9])
        parts = room.sb("parts", [P, NT, 96], BF16)
        lp = room.ps("lp", [P, 512], F32)
        cp = room.ps("cp", [P, 2, 512], F32)
        gp = room.ps("gp", [P, NT, P], BF16)
        logits = lp[:, 0:NT * 16].rearrange("p (n e) -> p n e", e=16)
        up_to = cp[:, 0, 0:2 * NT * 8].rearrange("p (n e) -> p n e", e=8)
        total = cp[:, 1, 0:2 * NT * 8].rearrange("p (n e) -> p n e", e=8)
        have, expd, chosen, counted, parted, turned = S["have"], S["expd"], S["chosen"], S["counted"], S["parted"], S["turned"]
        block = ctx.enter_context(nc.Block())

        @block.tensor
        def _(pe):
            ncol = EX if extra else E
            for n in range(NT):
                ins = nc.tensor.matmul(logits[:, n, 0:ncol], xnT[:, n * P:(n + 1) * P], Wr[:, 0:ncol], start=True, stop=True)
            ins.then_inc(have.sem, 1)
            if capacity:
                pe.wait_ge(chosen.sem, chosen.at(1))
                flat = ob[:, :, :].rearrange("p n e -> p (n e)")
                nc.tensor.matmul(cp[:, 0, 0:2 * NT * 8], C["upto"][:, :], flat, start=True, stop=True)
                nc.tensor.matmul(cp[:, 1, 0:2 * NT * 8], C["ones"][:, :], flat, start=True, stop=True).then_inc(counted.sem, 1)
            pe.wait_ge(parted.sem, parted.at(1))
            for n in range(NT):
                ins = nc.tensor.transpose(gp[0:96, n, :], parts[:, n, :], C["identb"][:, :])
            ins.then_inc(turned.sem, 1)

        @block.scalar
        def _(act):
            act.wait_ge(expd.sem, expd.at(1))
            nc.scalar.activation(ex[:, :], ex[:, :], ACT.Exp)
            if extra:
                nc.scalar.activation(sg[:, :], sg[:, :], ACT.Exp, scale=-1.0)
            nc.scalar.activation(m1[:, 0:1], m1[:, 0:1], ACT.Copy).then_inc(expd.sem, 1)
            act.wait_ge(turned.sem, turned.at(1))
            for h in range(2):
                nc.scalar.activation(gateT[:, h * 1024:(h + 1) * 1024],
                                     gp[0:96, h * 8:(h + 1) * 8, :].rearrange("p n t -> p (n t)"), ACT.Copy)

        @block.vector
        def _(dve):
            own = Steps(dve, S["dve"])
            link = own.link

            def bc(a, w=8):
                return a.unsqueeze(2).broadcast_to([P, a.shape[1], w])

            rank = C["rank"][:, 0:8].unsqueeze(1).broadcast_to([P, NT, 8])
            nc.vector.memset(parts[:, :, :], 0.0)
            nc.vector.memset(comb[:, :, :], 1.0)
            link(nc.vector.memset(lg[:, :, :], -3e38))
            dve.wait_ge(have.sem, have.at(1))
            link(nc.vector.tensor_copy(lg[:, :, 0:E], logits[:, :, 0:E]))
            if extra:
                link(nc.vector.tensor_copy(sg[:, :], logits[:, :, E]))
            for k, (src, v) in enumerate(((lg, v1), (l2, v2))):
                link(nc.vector.tensor_reduce(v[:, :], src[:, :, :], AX.X, ALU.max))
                link(nc.vector.tensor_tensor(cand[:, :, :], src[:, :, :], bc(v[:, :]), ALU.is_equal))
                link(nc.vector.tensor_tensor(cand[:, :, :], cand[:, :, :], rank, ALU.mult))
                link(nc.vector.tensor_reduce(m1[:, :], cand[:, :, :], AX.X, ALU.max))
                link(nc.vector.tensor_tensor(o[:, k * NT:(k + 1) * NT, :], cand[:, :, :], bc(m1[:, :]), ALU.is_equal))
                if k == 0:
                    link(nc.vector.scalar_tensor_tensor(l2[:, :, :], o[:, 0:NT, :], MASKED, lg[:, :, :], ALU.mult, ALU.add))
            nc.vector.tensor_tensor(ex[:, :], v2[:, :], v1[:, :], ALU.subtract).then_inc(expd.sem, 1)
            if capacity:
                nc.vector.tensor_copy(ob[:, :, :], o[:, :, :]).then_inc(chosen.sem, 1)
                dve.wait_ge(counted.sem, counted.at(1))
                link(nc.vector.tensor_copy(run_a[:, :, :], total))
                a, b_ = run_a, run_b
                for sh in (1, 2, 4, 8, 16):
                    nc.vector.tensor_copy(b_[:, 0:sh, :], a[:, 0:sh, :])
                    link(nc.vector.tensor_tensor(b_[:, sh:, :], a[:, sh:, :], a[:, 0:2 * NT - sh, :], ALU.add))
                    a, b_ = b_, a
                link(nc.vector.tensor_tensor(pos[:, :, :], a[:, :, :], total, ALU.subtract))
                link(nc.vector.tensor_tensor(pos[:, :, :], pos[:, :, :], up_to, ALU.add))
                link(nc.vector.scalar_tensor_tensor(o[:, :, :], pos[:, :, :], capacity + 0.5, o[:, :, :], ALU.is_lt, ALU.mult))
            dve.wait_ge(expd.sem, expd.at(2))
            link(nc.vector.tensor_scalar(den[:, :], ex[:, :], 1.0, None, ALU.add))
            link(nc.vector.reciprocal(g[:, 0:NT], den[:, :]))
            link(nc.vector.tensor_tensor(g[:, NT:2 * NT], ex[:, :], g[:, 0:NT], ALU.mult))
            link(nc.vector.tensor_tensor(o[:, :, :], o[:, :, :], bc(g[:, :]), ALU.mult))
            link(nc.vector.tensor_tensor(comb[:, :, 0:E], o[:, 0:NT, 0:E], o[:, NT:2 * NT, 0:E], ALU.add))
            if extra:
                link(nc.vector.tensor_scalar(sg[:, :], sg[:, :], 1.0, None, ALU.add))
                link(nc.vector.reciprocal(comb[:, :, E], sg[:, :]))
            pv = [parts[:, :, 32 * i:32 * i + EX] for i in range(3)]
            split3(own, nc, comb[:, :, 0:EX], rest[:, :, 0:EX], *pv).then_inc(parted.sem, 1)
            own.close()

    for s in (have, parted, turned):
        s.passed(1)
    expd.passed(2)
    if capacity:
        chosen.passed(1)
        counted.passed(1)


def experts(nc, S, X, xnT, gateT, sel, Wg, Wu, Wd, FT, ident, loaded, loaded_at):
    with ExitStack() as ctx:
        room = Room(nc, ctx)
        sg = room.sb("sg", [P, 2, T], F32)
        su = room.sb("su", [P, 2, T], F32)
        hid = room.sb("hid", [P, 2, T], F32)
        oT = room.sb("oT", [P, T], F32)
        pa = room.ps("pa", [P, 2, T], F32)
        pu = room.ps("pu", [P, 2, T], F32)
        pg = room.ps("pg", [P, 2, T], F32)
        po = room.ps("po", [P, T], F32)
        py = room.ps("py", [P, T], F32)
        proj, silu, hidden, down, copied, turned, added = (
            S[k] for k in ("proj", "silu", "hidden", "down", "copied", "turned", "padded"))
        block = ctx.enter_context(nc.Block())

        @block.tensor
        def _(pe):
            pe.wait_ge(loaded, loaded_at)
            with pe.Fori(0, B) as c:
                tok = bass.ds(c * T, T)

                def down_product(f):
                    if f == 0:
                        pe.wait_ge(copied.sem, copied.at(c))
                    pe.wait_ge(hidden.sem, hidden.at(c * FT + f + 1))
                    ins = nc.tensor.matmul(po[:, :], Wd[:, f, :], hid[:, f % 2, :],
                                           start=(f == 0), stop=(f == FT - 1))
                    ins.then_inc(down.sem, 1)

                for f in range(FT):
                    if f != 1:
                        pe.wait_ge(hidden.sem, hidden.at(c * FT + max(f - 1, 0)))
                    cols = slice(f * P, f * P + P)
                    nc.tensor.matmul(pa[:, f % 2, :], Wg[:, cols], xnT[:, tok], start=True, stop=True)
                    nc.tensor.matmul(pu[:, f % 2, :], Wu[:, cols], xnT[:, tok], start=True, stop=True)
                    nc.tensor.matmul(pg[:, f % 2, :], sel[0:96, cols], gateT[0:96, tok],
                                     start=True, stop=True).then_inc(proj.sem, 1)
                    if f >= 1:
                        down_product(f - 1)
                down_product(FT - 1)
                pe.wait_ge(copied.sem, copied.at(c + 1))
                pe.wait_ge(added.sem, added.at(c))
                for t in range(TPB):
                    ins = nc.tensor.transpose(py[:, t * P:(t + 1) * P], oT[:, t * P:(t + 1) * P], ident[:, :])
                ins.then_inc(turned.sem, 1)

        @block.scalar
        def _(act):
            with act.Fori(0, B) as c:
                for f in range(FT):
                    act.wait_ge(proj.sem, proj.at(c * FT + f + 1))
                    nc.scalar.activation(sg[:, f % 2, :], pa[:, f % 2, :], ACT.Silu).then_inc(silu.sem, 1)
                act.wait_ge(down.sem, down.at(c * FT + FT))
                act.wait_ge(turned.sem, turned.at(c))
                nc.scalar.activation(oT[:, :], po[:, :], ACT.Copy).then_inc(copied.sem, 1)

        @block.vector
        def _(dve):
            own = Steps(dve, S["dve"])
            with dve.Fori(0, B) as c:
                own.enter(c, FT)
                for f in range(FT):
                    dve.wait_ge(silu.sem, silu.at(c * FT + f + 1))
                    own.link(nc.vector.tensor_tensor(su[:, f % 2, :], sg[:, f % 2, :], pu[:, f % 2, :], ALU.mult))
                    if f != 1:
                        dve.wait_ge(down.sem, down.at(c * FT + max(f - 1, 0)))
                    nc.vector.tensor_tensor(hid[:, f % 2, :], su[:, f % 2, :], pg[:, f % 2, :],
                                            ALU.mult).then_inc(hidden.sem, 1)
                dve.wait_ge(turned.sem, turned.at(c + 1))
                xs = X[:, bass.ds(c * TPB, TPB), :].rearrange("p n d -> p (n d)")
                nc.vector.tensor_tensor(xs, xs, py[:, :], ALU.add).then_inc(added.sem, 1)
            own.leave(B)
            own.close()

    for s in (proj, silu, hidden, down):
        s.passed(B * FT)
    for s in (copied, turned, added):
        s.passed(B)


def group_norm_gate(nc, S, Y, G, groups, width, gain=None, shift=None):
    GC = TPB * groups
    with ExitStack() as ctx:
        room = Room(nc, ctx)
        sq = room.sb("sq", [P, GC, width])
        total, mean, ve = room.sb("total", [P, GC]), room.sb("mean", [P, GC]), room.sb("ve", [P, GC])
        sd, rs = room.sb("sd", [P, GC]), room.sb("rs", [P, GC])
        centred, squared, var_ready, std_ready, gated = (S[k] for k in ("centred", "squared", "var", "std", "gated"))
        block = ctx.enter_context(nc.Block())

        @block.vector
        def _(dve):
            own = Steps(dve, S["dve"])

            def bc(a):
                return a.unsqueeze(2).broadcast_to([P, GC, width])

            for b in range(B):
                y = Y[:, b * TPB:(b + 1) * TPB, :].rearrange("p n (g w) -> p (n g) w", w=width)
                gate = G[:, b * TPB:(b + 1) * TPB, :].rearrange("p n (g w) -> p (n g) w", w=width)
                own.link(nc.vector.tensor_reduce(total[:, :], y, AX.X, ALU.add))
                own.link(nc.vector.tensor_scalar(mean[:, :], total[:, :], -1.0 / width, None, ALU.mult))
                nc.vector.tensor_tensor(y, y, bc(mean[:, :]), ALU.add).then_inc(centred.sem, 1)
                dve.wait_ge(squared.sem, squared.at(b + 1))
                own.link(nc.vector.tensor_reduce(total[:, :], sq[:, :, :], AX.X, ALU.add))
                nc.vector.tensor_scalar(ve[:, :], total[:, :], 1.0 / width, EPS, ALU.mult, ALU.add).then_inc(var_ready.sem, 1)
                dve.wait_ge(std_ready.sem, std_ready.at(b + 1))
                own.link(nc.vector.reciprocal(rs[:, :], sd[:, :]))
                own.link(nc.vector.tensor_tensor(y, y, bc(rs[:, :]), ALU.mult))
                if gain is not None:
                    own.link(nc.vector.tensor_tensor(y, y, gain.unsqueeze(1).broadcast_to([P, GC, width]), ALU.mult))
                    own.link(nc.vector.tensor_tensor(y, y, shift.unsqueeze(1).broadcast_to([P, GC, width]), ALU.add))
                if b == 0:
                    dve.wait_ge(gated.sem, gated.at(B))
                nc.vector.tensor_tensor(y, y, gate, ALU.mult)
            own.close()

        @block.scalar
        def _(act):
            for b in range(B):
                g = G[:, b * TPB:(b + 1) * TPB, :]
                nc.scalar.activation(g, g, ACT.Silu).then_inc(gated.sem, 1)
            for b in range(B):
                y = Y[:, b * TPB:(b + 1) * TPB, :].rearrange("p n (g w) -> p (n g) w", w=width)
                act.wait_ge(centred.sem, centred.at(b + 1))
                nc.scalar.activation(sq[:, :, :], y, ACT.Square).then_inc(squared.sem, 1)
                act.wait_ge(var_ready.sem, var_ready.at(b + 1))
                nc.scalar.activation(sd[:, :], ve[:, :], ACT.Sqrt).then_inc(std_ready.sem, 1)

    for s in (centred, squared, var_ready, std_ready, gated):
        s.passed(B)


def retention_project(nc, S, xnT, W, qT, kT, V, G):
    with ExitStack() as ctx:
        room = Room(nc, ctx)
        t1, t2 = room.sb("t1", [P, T]), room.sb("t2", [P, T])
        qk = room.ps("qk", [P, 4, T])
        vg = room.ps("vg", [P, 2, 2, 256])
        qk_ready, rotated, vg_ready, vg_copied = (S[k] for k in ("qk_ready", "rotated", "vg_ready", "vg_copied"))
        block = ctx.enter_context(nc.Block())

        @block.tensor
        def _(pe):
            for b in range(B):
                x = xnT[:, b * T:(b + 1) * T]
                if b >= 1:
                    pe.wait_ge(rotated.sem, rotated.at(b))
                for i in range(4):
                    ins = nc.tensor.matmul(qk[:, i, :], W["wqk"][:, i, :], x, start=True, stop=True)
                ins.then_inc(qk_ready.sem, 1)
                for t in range(TPB):
                    n = b * TPB + t
                    if n >= 2:
                        pe.wait_ge(vg_copied.sem, vg_copied.at(n - 1))
                    xt = xnT[:, n * P:(n + 1) * P]
                    for i, (w, bias) in enumerate((("wv", "bv"), ("wg", "bg"))):
                        nc.tensor.matmul(vg[:, n % 2, i, :], xt, W[w][:, :], start=True, stop=False)
                        ins = nc.tensor.matmul(vg[:, n % 2, i, :], W["one"][0:1, :], W[bias][0:1, :], start=False, stop=True)
                    ins.then_inc(vg_ready.sem, 1)

        @block.scalar
        def _(act):
            for n in range(NT):
                act.wait_ge(vg_ready.sem, vg_ready.at(n + 1))
                nc.scalar.activation(V[:, n, :], vg[:, n % 2, 0, :], ACT.Copy)
                nc.scalar.activation(G[:, n, :], vg[:, n % 2, 1, :], ACT.Copy).then_inc(vg_copied.sem, 1)

        @block.vector
        def _(dve):
            own = Steps(dve, S["dve"])
            for b in range(B):
                dve.wait_ge(qk_ready.sem, qk_ready.at(b + 1))
                for i, (dst, tab) in enumerate(((qT, "xq"), (kT, "xk"))):
                    nc.vector.scalar_tensor_tensor(t1[:, :], qk[:, 2 * i, :], W["bqk"][:, 2 * i:2 * i + 1],
                                                   W[tab + "_cos"][:, :], ALU.add, ALU.mult)
                    own.link(nc.vector.scalar_tensor_tensor(t2[:, :], qk[:, 2 * i + 1, :], W["bqk"][:, 2 * i + 1:2 * i + 2],
                                                            W[tab + "_sin"][:, :], ALU.add, ALU.mult))
                    own.link(nc.vector.tensor_tensor(dst[:, b, :], t1[:, :], t2[:, :], ALU.add))
                dve.sem_inc(rotated.sem, 1)
            own.close()

    qk_ready.passed(B)
    rotated.passed(B)
    vg_ready.passed(NT)
    vg_copied.passed(NT)


def retention_heads(nc, S, W, qT, kT, V, Y):
    U = R_HEADS * B
    start_of = [0, T, 2 * T - P, 3 * T - 3 * P]
    with ExitStack() as ctx:
        room = Room(nc, ctx)
        qh = room.sb("qh", [P, 2, T])
        decayed = room.sb("decayed", [P, 2, 10 * P])
        sc = room.ps("sc", [P, 4, T])
        ob = room.ps("ob", [P, 2, 512])
        picked, scored, decays, summed, copied = (S[k] for k in ("picked", "scored", "decays", "rsummed", "rcopied"))
        block = ctx.enter_context(nc.Block())

        @block.scalar
        def _(act):
            def pick(h, b, u):
                act.wait_ge(scored.sem, scored.at(TPB * (u - 1)))
                stand_alone(act, S["aside"])
                nc.scalar.activation(qh[:, b % 2, :], qT[:, b, :], ACT.Copy, scale=W["head_rows"][:, h]).then_inc(picked.sem, 1)

            def put(h, b, u):
                act.wait_ge(summed.sem, summed.at(u + 1))
                stand_alone(act, S["aside"])
                dst = Y[:, b * TPB:(b + 1) * TPB, h]
                nc.scalar.activation(dst, ob[:, b % 2, 0:TPB * R_DV].rearrange("p (n c) -> p n c", c=R_DV),
                                     ACT.Copy).then_inc(copied.sem, 1)

            with act.Fori(0, R_HEADS) as h:
                head = bass.ds(h, 1)
                cols = bass.ds(h * R_DV, R_DV)
                for b in range(B):
                    pick(head, b, h * B + b)
                    if b >= 1:
                        put(cols, b - 1, h * B + b - 1)
                put(cols, B - 1, h * B + B - 1)

        @block.tensor
        def _(pe):
            with pe.Fori(0, R_HEADS) as h:
                def scores(b):
                    u = h * B + b
                    pe.wait_ge(picked.sem, picked.at(u + 1))
                    for kj in range(TPB):
                        pe.wait_ge(decays.sem, decays.at((u - 1) * TPB + kj + 1))
                        w = T - kj * P
                        nc.tensor.matmul(sc[:, kj, 0:w], kT[:, b, kj * P:(kj + 1) * P], qh[:, b % 2, kj * P:T],
                                         start=True, stop=True).then_inc(scored.sem, 1)

                def values(b):
                    u = h * B + b
                    pe.wait_ge(decays.sem, decays.at((u + 1) * TPB))
                    pe.wait_ge(copied.sem, copied.at(u - 1))
                    for qi in range(TPB):
                        for kj in range(qi + 1):
                            at = start_of[kj] + (qi - kj) * P
                            ins = nc.tensor.matmul(ob[:, b % 2, qi * R_DV:(qi + 1) * R_DV], decayed[:, b % 2, at:at + P],
                                                   V[:, b * TPB + kj, bass.ds(h * R_DV, R_DV)],
                                                   start=(kj == 0), stop=(kj == qi))
                    ins.then_inc(summed.sem, 1)

                for b in range(B):
                    scores(b)
                    if b >= 1:
                        values(b - 1)
                values(B - 1)

        @block.vector
        def _(dve):
            with dve.Fori(0, R_HEADS) as h:
                for b in range(B):
                    u = h * B + b
                    dve.wait_ge(summed.sem, summed.at(u - 1))
                    for kj in range(TPB):
                        w = T - kj * P
                        dve.wait_ge(scored.sem, scored.at(u * TPB + kj + 1))
                        nc.vector.tensor_tensor(decayed[:, b % 2, start_of[kj]:start_of[kj] + w], sc[:, kj, 0:w],
                                                W["decays"][:, bass.ds(h, 1), 0:w].rearrange("p a c -> p (a c)"),
                                                ALU.mult).then_inc(decays.sem, 1)

    picked.passed(U)
    scored.passed(TPB * U)
    decays.passed(TPB * U)
    summed.passed(U)
    copied.passed(U)


def retention(nc, S, X, C, D, ident):
    with ExitStack() as ctx:
        room = Room(nc, ctx)
        qT, kT = room.sb("qT", [P, B, T]), room.sb("kT", [P, B, T])
        V, G = room.sb("V", [P, NT, 256]), room.sb("G", [P, NT, 256])
        W = {n: room.sb(n, s) for n, s in (
            ("wqk", [P, 4, P]), ("bqk", [P, 4]), ("wv", [P, 256]), ("bv", [1, 256]), ("wg", [P, 256]), ("bg", [1, 256]),
            ("wp", [P, 2, P]), ("bp", [1, P]), ("one", [1, P]), ("decays", [P, R_HEADS, T]), ("head_rows", [P, R_HEADS]),
            ("xq_cos", [P, T]), ("xq_sin", [P, T]), ("xk_cos", [P, T]), ("xk_sin", [P, T]))}
        big, made = S["big"], S["made"]
        with nc.Block() as block:
            @block.sync
            def _(sp):
                for n, key in (("wqk", "re_wqk"), ("bqk", "re_bqk"), ("wv", "re_wv"), ("bv", "re_bv"), ("wg", "re_wg"), ("bg", "re_bg"),
                               ("wp", "re_wp"), ("bp", "re_bp"), ("xq_cos", "xq_cos"), ("xq_sin", "xq_sin"), ("xk_cos", "xk_cos"),
                               ("xk_sin", "xk_sin"), ("head_rows", "head_rows"), ("decays", "decays")):
                    sp.dma_start(W[n][:, :] if len(W[n].shape) == 2 else W[n][:, :, :], D[key]).then_inc(big.sem, 16)

            @block.gpsimd
            def _(pool):
                nc.gpsimd.memset(W["one"][0:1, :], 1.0).then_inc(made.sem, 1)
                pool.wait_ge(made.sem, made.at(1))
        made.passed(1)
        with ExitStack() as inner:
            xnT = Room(nc, inner).sb("xnT", [P, B * T])
            norm_transpose(nc, S, X, xnT, ident)
            with nc.Block() as block:
                @block.sync
                def _(sp):
                    sp.wait_ge(big.sem, big.at(14 * 16))
            big.passed(14 * 16)
            retention_project(nc, S, xnT, W, qT, kT, V, G)
        Y = room.sb("Y", [P, NT, 256])
        retention_heads(nc, S, W, qT, kT, V, Y)
        group_norm_gate(nc, S, Y, G, R_HEADS, R_DV)
        project_add(nc, S, X, Y, W["wp"], ident, 2, W["bp"][0:1, :], W["one"][0:1, :])


def recurrent(nc, S, X, C, D, ident):
    R, K, V_, G_, DEC = range(5)
    XW, U = 5, 6
    with ExitStack() as ctx:
        room = Room(nc, ctx)
        Y, G = room.sb("Y", [P, NT, P]), room.sb("G", [P, NT, P])
        wo, ln = room.sb("wo", [P, 1, P]), room.sb("ln", [P, 2 * W_HD])
        big = S["big"]
        inner = ExitStack()
        iroom = Room(nc, inner)
        xnT = iroom.sb("xnT", [P, B * T])
        la, lb = iroom.sb("la", [P, 5, LORA]), iroom.sb("lb", [LORA, 5, P])
        cols, w = iroom.sb("cols", [P, 7]), iroom.sb("w", [P, 5, P])
        wvj, to_j = iroom.sb("wvj", [P, W_HD, P]), iroom.sb("to_j", [P, W_HD, P])
        same, init = iroom.sb("same", [P, P]), iroom.sb("init", [P, W_HD])
        loads = ((la, "rw_la"), (lb, "rw_lb"), (cols, "rw_cols"), (w, "rw_w"), (wvj, "rw_wvj"), (to_j, "head_to"), (same, "head_sum"),
                 (init, "rw_init"))
        with nc.Block() as block:
            @block.sync
            def _(sp):
                for dst, key in loads:
                    src = D[key]
                    d = dst[:, :] if len(dst.shape) == 2 else dst[:, :, :] if key != "rw_w" else dst[:, 0:5, :]
                    sp.dma_start(d, src).then_inc(big.sem, 16)
                sp.dma_start(wo[:, :, :], D["rw_w"][:, 4:5, :]).then_inc(big.sem, 16)
                sp.dma_start(ln[:, :], D["rw_ln"].broadcast_to([P, 2 * W_HD])).then_inc(big.sem, 16)
        n_loads = len(loads) + 2
        norm_transpose(nc, S, X, xnT, ident)

        dx, lerp = iroom.sb("dx", [P, T]), iroom.sb("lerp", [P, T])
        th, mix, part = iroom.sb("th", [LORA, 2, T]), iroom.sb("mix", [P, 5, T]), iroom.sb("part", [P, T])
        rkv, e1, dec = iroom.sb("rkv", [P, 3, T]), iroom.sb("e1", [P, T]), iroom.sb("dec", [P, T])
        kv, st, pr = iroom.sb("kv", [P, T]), iroom.sb("st", [P, 2, T + 1]), iroom.sb("pr", [P, 2, T])
        bonus, yT = iroom.sb("bonus", [P, T]), iroom.sb("yT", [P, T])
        ph, pl, pv = iroom.ps("ph", [P, 2, T]), iroom.ps("pl", [P, 2, T]), iroom.ps("pv", [P, 2, T])
        py, px = iroom.ps("py", [P, T]), iroom.ps("px", [P, T])
        (lerped, low, tanhed, high, mixed, px_full, px_free, decayed, v_full, v_used, weighted, summed, bonused, y_done) = (
            S["w_" + k] for k in ("lerped", "low", "tanhed", "high", "mixed", "px_full", "px_free", "decayed", "v_full",
                                  "v_used", "weighted", "summed", "bonused", "y_done"))
        PX = 6
        with nc.Block() as block:
            @block.tensor
            def _(pe):
                pe.wait_ge(big.sem, big.at(16 * n_loads))
                with pe.Fori(0, B) as b:
                    def low_rank(p, src, n):
                        nc.tensor.matmul(ph[0:LORA, n % 2, :], la[:, p, :], src, start=True, stop=True).then_inc(low.sem, 1)

                    def back(p, n):
                        pe.wait_ge(tanhed.sem, tanhed.at(b * 6 + n + 1))
                        if n >= 2:
                            pe.wait_ge(mixed.sem, mixed.at(b * 5 + n - 1))
                        nc.tensor.matmul(pl[:, n % 2, :], lb[:, p, :], th[:, n % 2, :], start=True, stop=True).then_inc(high.sem, 1)

                    def project(n, weight, src):
                        pe.wait_ge(px_free.sem, px_free.at(b * PX + n))
                        nc.tensor.matmul(px[:, :], weight, src, start=True, stop=True).then_inc(px_full.sem, 1)

                    pe.wait_ge(lerped.sem, lerped.at(b + 1))
                    low_rank(0, lerp[:, :], 0)
                    low_rank(1, lerp[:, :], 1)
                    for p in range(5):
                        back(p, p)
                        if p + 2 < 5:
                            low_rank(p + 2, lerp[:, :], p + 2)
                        if p >= 1 and p - 1 < 3:
                            pe.wait_ge(mixed.sem, mixed.at(b * 5 + p))
                            project(p - 1, w[:, p - 1, :], mix[:, p - 1, :])
                    pe.wait_ge(mixed.sem, mixed.at(b * 5 + 5))
                    low_rank(DEC, mix[:, DEC, :], 5)
                    back(DEC, 5)
                    pe.wait_ge(px_free.sem, px_free.at(b * PX + 3))
                    for t in range(TPB):
                        ins = nc.tensor.matmul(px[:, t * P:(t + 1) * P], mix[:, G_, t * P:(t + 1) * P], w[:, 3, :], start=True, stop=True)
                    ins.then_inc(px_full.sem, 1)

                    def sum_rows(j):
                        pe.wait_ge(weighted.sem, weighted.at(b * W_HD + j + 1))
                        nc.tensor.matmul(py[:, :], to_j[:, j, :], pr[:, j % 2, :], start=(j == 0), stop=(j == W_HD - 1)).then_inc(summed.sem, 1)

                    for j in range(W_HD):
                        pe.wait_ge(v_used.sem, v_used.at(b * W_HD + j - 1))
                        nc.tensor.matmul(pv[:, j % 2, :], wvj[:, j, :], mix[:, V_, :], start=True, stop=True).then_inc(v_full.sem, 1)
                        if j >= 1:
                            sum_rows(j - 1)
                    sum_rows(W_HD - 1)
                    pe.wait_ge(bonused.sem, bonused.at(b + 1))
                    project(4, same[:, :], bonus[:, :])
                    pe.wait_ge(y_done.sem, y_done.at(b + 1))
                    pe.wait_ge(px_free.sem, px_free.at(b * PX + 5))
                    for t in range(TPB):
                        ins = nc.tensor.transpose(px[:, t * P:(t + 1) * P], yT[:, t * P:(t + 1) * P], ident[:, :])
                    ins.then_inc(px_full.sem, 1)

            @block.scalar
            def _(act):
                act.wait_ge(big.sem, big.at(16 * n_loads))
                with act.Fori(0, B) as b:
                    def tanh(n):
                        act.wait_ge(low.sem, low.at(b * 6 + n + 1))
                        nc.scalar.activation(th[:, n % 2, :], ph[0:LORA, n % 2, :], ACT.Tanh).then_inc(tanhed.sem, 1)

                    def copy_px(n, dst):
                        act.wait_ge(px_full.sem, px_full.at(b * PX + n + 1))
                        if n in (3, 5):
                            stand_alone(act, S["aside"])
                        nc.scalar.activation(dst, px[:, :], ACT.Copy).then_inc(px_free.sem, 1)

                    tanh(0)
                    tanh(1)
                    tanh(2)
                    copy_px(0, rkv[:, 0, :])
                    tanh(3)
                    copy_px(1, rkv[:, 1, :])
                    tanh(4)
                    copy_px(2, rkv[:, 2, :])
                    tanh(5)
                    act.wait_ge(high.sem, high.at(b * 6 + 6))
                    nc.scalar.activation(e1[:, :], pl[:, 1, :], ACT.Exp, bias=cols[:, DEC:DEC + 1]).then_inc(S["w_e1"].sem, 1)
                    act.wait_ge(S["w_e1"].sem, S["w_e1"].at(b + 1))
                    nc.scalar.activation(dec[:, :], e1[:, :], ACT.Exp, scale=-1.0).then_inc(decayed.sem, 1)
                    copy_px(3, G[:, bass.ds(b * TPB, TPB), :].rearrange("p n d -> p (n d)"))
                    copy_px(5, Y[:, bass.ds(b * TPB, TPB), :].rearrange("p n d -> p (n d)"))

            @block.vector
            def _(dve):
                own = Steps(dve, S["dve"])
                dve.wait_ge(big.sem, big.at(16 * n_loads))
                with dve.Fori(0, B) as b:
                    x = xnT[:, bass.ds(b * T, T)]
                    own.enter(b, 2 + 5 + 2 * W_HD + 1 + 1)
                    nc.vector.tensor_tensor(dx[:, 1:T], xnT[:, bass.ds(b * T, T - 1)], xnT[:, bass.ds(b * T + 1, T - 1)], ALU.subtract)
                    own.link(nc.vector.tensor_scalar(dx[:, 0:1], xnT[:, bass.ds(b * T, 1)], -1.0, None, ALU.mult))
                    own.link(nc.vector.scalar_tensor_tensor(lerp[:, :], dx[:, :], cols[:, XW:XW + 1], x, ALU.mult, ALU.add))
                    dve.sem_inc(lerped.sem, 1)
                    for p in range(5):
                        dve.wait_ge(high.sem, high.at(b * 6 + p + 1))
                        own.link(nc.vector.scalar_tensor_tensor(part[:, :], pl[:, p % 2, :], cols[:, p:p + 1], dx[:, :], ALU.add, ALU.mult))
                        nc.vector.tensor_tensor(mix[:, p, :], part[:, :], x, ALU.add).then_inc(mixed.sem, 1)
                        dve.wait_ge(mixed.sem, mixed.at(b * 5 + p + 1))
                    dve.wait_ge(px_free.sem, px_free.at(b * PX + 3))
                    nc.vector.scalar_tensor_tensor(bonus[:, :], rkv[:, R, :], cols[:, U:U + 1], rkv[:, K, :], ALU.mult, ALU.mult).then_inc(bonused.sem, 1)
                    dve.wait_ge(decayed.sem, decayed.at(b + 1))
                    for j in range(W_HD):
                        dve.wait_ge(v_full.sem, v_full.at(b * W_HD + j + 1))
                        nc.vector.tensor_copy(st[:, j % 2, 0:1], init[:, j:j + 1])
                        own.link(nc.vector.tensor_tensor(kv[:, :], rkv[:, K, :], pv[:, j % 2, :], ALU.mult))
                        dve.sem_inc(v_used.sem, 1)
                        own.link(nc.vector.tensor_tensor_scan(st[:, j % 2, 1:T + 1], dec[:, :], kv[:, :], init[:, j:j + 1], ALU.mult, ALU.add))
                        dve.wait_ge(summed.sem, summed.at(b * W_HD + j - 1))
                        nc.vector.tensor_tensor(pr[:, j % 2, :], st[:, j % 2, 0:T], rkv[:, R, :], ALU.mult).then_inc(weighted.sem, 1)
                    dve.wait_ge(px_full.sem, px_full.at(b * PX + 5))
                    own.link(nc.vector.tensor_tensor(part[:, :], px[:, :], rkv[:, 2, :], ALU.mult))
                    dve.sem_inc(px_free.sem, 1)
                    dve.wait_ge(summed.sem, summed.at((b + 1) * W_HD))
                    own.link(nc.vector.tensor_tensor(yT[:, :], py[:, :], part[:, :], ALU.add))
                    dve.sem_inc(y_done.sem, 1)
                own.leave(B)
                own.close()
        for s, n in ((lerped, 1), (low, 6), (tanhed, 6), (high, 6), (mixed, 5), (px_full, PX), (px_free, PX), (decayed, 1),
                     (v_full, W_HD), (v_used, W_HD), (weighted, W_HD), (summed, W_HD), (bonused, 1), (y_done, 1), (S["w_e1"], 1)):
            s.passed(B * n)
        big.passed(16 * n_loads)
        inner.close()
        group_norm_gate(nc, S, Y, G, W_HEADS, W_HD, ln[:, 0:W_HD], ln[:, W_HD:2 * W_HD])
        project_add(nc, S, X, Y, wo, ident, 1)


def rotate(own, nc, dst, plain, partner, cos, sin, t1, t2):
    nc.vector.tensor_tensor(t1, plain, cos, ALU.mult)
    own.link(nc.vector.tensor_tensor(t2, partner, sin, ALU.mult))
    own.link(nc.vector.tensor_tensor(dst, t1, t2, ALU.add))


def mqa_keys(nc, S, xnT, wk, wv, tables, kT, V):
    with ExitStack() as ctx:
        room = Room(nc, ctx)
        t1, t2 = room.sb("t1", [P, T]), room.sb("t2", [P, T])
        kp = room.ps("kp", [P, 2, T])
        vp = room.ps("vp", [P, NT, M_HD])
        qk_ready, rotated, vg_ready = S["qk_ready"], S["rotated"], S["vg_ready"]
        block = ctx.enter_context(nc.Block())

        @block.tensor
        def _(pe):
            for n in range(NT):
                ins = nc.tensor.matmul(vp[:, n, :], xnT[:, n * P:(n + 1) * P], wv[:, :], start=True, stop=True)
            ins.then_inc(vg_ready.sem, 1)
            for b in range(B):
                if b >= 1:
                    pe.wait_ge(rotated.sem, rotated.at(b))
                for i in range(2):
                    ins = nc.tensor.matmul(kp[:, i, :], wk[:, i, :], xnT[:, b * T:(b + 1) * T], start=True, stop=True)
                ins.then_inc(qk_ready.sem, 1)

        @block.scalar
        def _(act):
            act.wait_ge(vg_ready.sem, vg_ready.at(1))
            for h in range(2):
                nc.scalar.activation(V[:, h * 8:(h + 1) * 8, :], vp[:, h * 8:(h + 1) * 8, :], ACT.Copy)

        @block.vector
        def _(dve):
            own = Steps(dve, S["dve"])
            for b in range(B):
                dve.wait_ge(qk_ready.sem, qk_ready.at(b + 1))
                rotate(own, nc, kT[:, b, :], kp[:, 0, :], kp[:, 1, :], tables["k_cos"][:, :], tables["k_sin"][:, :], t1[:, :], t2[:, :])
                dve.sem_inc(rotated.sem, 1)
            own.close()

    qk_ready.passed(B)
    rotated.passed(B)
    vg_ready.passed(1)


def mqa_heads(nc, S, xnT, wq_dram, tables, kT, V, Y, C, ident):
    PAIRS, HPT = M_HEADS // 2, 2 * B
    U = HPT * TPB
    with ExitStack() as ctx:
        room = Room(nc, ctx)
        wq = room.sb("wq", [P, 2, P])
        qT = room.sb("qT", [P, 2, T])
        t1, t2 = room.sb("t1", [P, T]), room.sb("t2", [P, T])
        prob, probT = room.sb("prob", [P, 2, T]), room.sb("probT", [P, 2, T])
        nmax, rsum, inv = room.sb("nmax", [P, 4]), room.sb("rsum", [P, 2, TPB]), room.sb("inv", [P, TPB])
        sc, tp, ob, qp = (room.ps(n, [P, 2, T]) for n in ("sc", "tp", "ob", "qp"))
        weights, projected, rotated, scored, maxed, expd, turned, copied, valued, normed = (
            S["a_" + k] for k in ("weights", "projected", "rotated", "scored", "maxed", "expd", "turned", "copied", "valued", "normed"))
        block = ctx.enter_context(nc.Block())

        @block.sync
        def _(sp):
            with sp.Fori(0, PAIRS) as hp:
                sp.wait_ge(projected.sem, projected.at(hp * B))
                stand_alone(sp, S["aside"])
                sp.dma_start(wq[:, :, :], wq_dram[bass.ds(hp, 1), :, :, :].rearrange("a p i n -> (a p) i n")).then_inc(weights.sem, 16)

        @block.tensor
        def _(pe):
            with pe.Fori(0, PAIRS) as hp:
                u0, j0 = hp * U, hp * HPT

                def project(b):
                    pe.wait_ge(rotated.sem, rotated.at(hp * B + b))
                    for i in range(2):
                        ins = nc.tensor.matmul(qp[:, i, :], wq[:, i, :], xnT[:, b * T:(b + 1) * T], start=True, stop=True)
                    ins.then_inc(projected.sem, 1)

                def scores(u):
                    j, qi = divmod(u, TPB)
                    b, h = divmod(j, 2)
                    if u % (2 * TPB) == 0:
                        pe.wait_ge(rotated.sem, rotated.at(hp * B + b + 1))
                    pe.wait_ge(expd.sem, expd.at(u0 + u - 1))
                    rows = slice(h * M_HD, (h + 1) * M_HD)
                    s = sc[:, u % 2, 0:(qi + 1) * P]
                    nc.tensor.matmul(s, qT[rows, b % 2, qi * P:(qi + 1) * P], kT[rows, b, 0:(qi + 1) * P], start=True, stop=False)
                    nc.tensor.matmul(s[:, qi * P:(qi + 1) * P], C["identb"][:, :], C["above"][:, :], start=False, stop=True).then_inc(scored.sem, 1)

                def transposes(u):
                    pe.wait_ge(expd.sem, expd.at(u0 + u + 1))
                    pe.wait_ge(copied.sem, copied.at(u0 + u - 1))
                    for kj in range(u % TPB + 1):
                        ins = nc.tensor.transpose(tp[:, u % 2, kj * P:(kj + 1) * P], prob[:, u % 2, kj * P:(kj + 1) * P], ident[:, :])
                    ins.then_inc(turned.sem, 1)

                def values(u):
                    j, qi = divmod(u, TPB)
                    if qi == 0:
                        pe.wait_ge(normed.sem, normed.at(j0 + j - 1))
                    pe.wait_ge(copied.sem, copied.at(u0 + u + 1))
                    for kj in range(qi + 1):
                        ins = nc.tensor.matmul(ob[:, j % 2, qi * M_HD:(qi + 1) * M_HD], probT[:, u % 2, kj * P:(kj + 1) * P],
                                               V[:, j // 2 * TPB + kj, :], start=(kj == 0), stop=(kj == qi))
                    ins.then_inc(valued.sem, 1)

                pe.wait_ge(weights.sem, weights.at(16 * hp + 16))
                project(0)
                for u in range(U + 2):
                    if u < U:
                        scores(u)
                        if u % (2 * TPB) == 1 and u // (2 * TPB) + 1 < B:
                            project(u // (2 * TPB) + 1)
                    if 0 <= u - 2:
                        values(u - 2)
                    if 0 <= u - 1 < U:
                        transposes(u - 1)

        @block.scalar
        def _(act):
            with act.Fori(0, PAIRS) as hp:
                u0, j0 = hp * U, hp * HPT
                for u in range(U + 1):
                    if u < U:
                        j, qi = divmod(u, TPB)
                        if qi == 0:
                            act.wait_ge(normed.sem, normed.at(j0 + j - 1))
                        act.wait_ge(turned.sem, turned.at(u0 + u - 1))
                        act.wait_ge(maxed.sem, maxed.at(u0 + u + 1))
                        w = (qi + 1) * P
                        nc.scalar.activation(prob[:, u % 2, 0:w], sc[:, u % 2, 0:w], ACT.Exp, bias=nmax[:, u % 4:u % 4 + 1],
                                             accum_out=rsum[:, j % 2, qi:qi + 1]).then_inc(expd.sem, 1)
                    if u >= 1:
                        v = u - 1
                        w = (v % TPB + 1) * P
                        act.wait_ge(valued.sem, valued.at(u0 + v - 1))
                        act.wait_ge(turned.sem, turned.at(u0 + v + 1))
                        nc.scalar.activation(probT[:, v % 2, 0:w], tp[:, v % 2, 0:w], ACT.Copy).then_inc(copied.sem, 1)

        @block.vector
        def _(dve):
            own = Steps(dve, S["dve"])
            with dve.Fori(0, PAIRS) as hp:
                own.enter(hp, 2 * B + HPT)
                u0, j0 = hp * U, hp * HPT

                def queries(b):
                    dve.wait_ge(projected.sem, projected.at(hp * B + b + 1))
                    dve.wait_ge(scored.sem, scored.at(u0 + max(2 * TPB * (b - 1), 0)))
                    rotate(own, nc, qT[:, b % 2, :], qp[:, 0, :], qp[:, 1, :], tables["cos"][:, :], tables["sin"][:, :], t1[:, :], t2[:, :])
                    dve.sem_inc(rotated.sem, 1)

                def norm(j):
                    dve.wait_ge(valued.sem, valued.at(u0 + (j + 1) * TPB))
                    dve.wait_ge(normed.sem, normed.at(j0 + j))
                    own.link(nc.vector.reciprocal(inv[:, :], rsum[:, j % 2, :]))
                    b, h = divmod(j, 2)
                    dst = Y[:, b * TPB:(b + 1) * TPB, bass.ds(hp * P + h * M_HD, M_HD)]
                    nc.vector.tensor_tensor(dst, ob[:, j % 2, 0:TPB * M_HD].rearrange("p (n c) -> p n c", c=M_HD),
                                            inv[:, :].unsqueeze(2).broadcast_to([P, TPB, M_HD]), ALU.mult).then_inc(normed.sem, 1)

                queries(0)
                for u in range(U):
                    dve.wait_ge(scored.sem, scored.at(u0 + u + 1))
                    w = (u % TPB + 1) * P
                    nc.vector.tensor_reduce(nmax[:, u % 4:u % 4 + 1], sc[:, u % 2, 0:w], AX.X, ALU.max, negate=True).then_inc(maxed.sem, 1)
                    if u % (2 * TPB) == 1 and u // (2 * TPB) + 1 < B:
                        queries(u // (2 * TPB) + 1)
                    if u % TPB == 3 and u > TPB:
                        norm(u // TPB - 1)
                norm(HPT - 1)
            own.leave(PAIRS)
            own.close()

    for s, n in ((weights, 16), (projected, B), (rotated, B), (scored, U), (maxed, U), (expd, U), (turned, U), (copied, U), (valued, U),
                 (normed, HPT)):
        s.passed(PAIRS * n)


def attention_mqa(nc, S, X, C, D, ident):
    KT = M_HEADS * M_HD // P
    with ExitStack() as ctx:
        room = Room(nc, ctx)
        Y = room.sb("Y", [P, NT, KT * P])
        wo = room.sb("wo", [P, KT, P])
        big = S["big"]
        with ExitStack() as inner:
            iroom = Room(nc, inner)
            xnT, kT, V = iroom.sb("xnT", [P, B * T]), iroom.sb("kT", [P, B, T]), iroom.sb("V", [P, NT, M_HD])
            wk, wv = iroom.sb("wk", [P, 2, P]), iroom.sb("wv", [P, M_HD])
            tables = {n: iroom.sb(n, [P, T]) for n in ("cos", "sin", "k_cos", "k_sin")}
            with nc.Block() as block:
                @block.sync
                def _(sp):
                    sp.dma_start(wk[:, :, :], D["mq_wk"]).then_inc(big.sem, 16)
                    sp.dma_start(wv[:, :], D["mq_wv"]).then_inc(big.sem, 16)
                    for n in tables:
                        sp.dma_start(tables[n][:, :], D["rope_" + n]).then_inc(big.sem, 16)
                    sp.dma_start(wo[:, :, :], D["mq_wo"]).then_inc(big.sem, 16)
            norm_transpose(nc, S, X, xnT, ident)
            with nc.Block() as block:
                @block.sync
                def _(sp):
                    sp.wait_ge(big.sem, big.at(7 * 16))
            big.passed(7 * 16)
            mqa_keys(nc, S, xnT, wk, wv, tables, kT, V)
            mqa_heads(nc, S, xnT, D["mq_wq"], tables, kT, V, Y, C, ident)
        project_add(nc, S, X, Y, wo, ident, KT)


CUTS = ((0, 0), (0, 1), (1, 0), (0, 2), (2, 0), (1, 1))


def decay_project(nc, S, xnT, w, drow, log_dist, V1, weight, parts_q, parts_k):
    with ExitStack() as ctx:
        room = Room(nc, ctx)
        dt, sp_ = room.sb("dt", [P, A_HEADS]), room.sb("softplus", [P, A_HEADS])
        qk, rest = room.sb("qk", [P, 2, 2, T]), room.sb("rest", [P, 2, T])
        cut = room.sb("cut", [P, 2, 2, 3, T], BF16)
        qp = room.ps("qp", [P, 2, 2, T])
        vp = room.ps("vp", [P, 2, T])
        (qk_ready, qk_copied, cut_ready, vg_ready, vg_copied, expd) = (
            S[k] for k in ("qk_ready", "qk_copied", "cut_ready", "vg_ready", "vg_copied", "expd"))
        cut_stored = S["cut_stored0"], S["cut_stored1"]
        block = ctx.enter_context(nc.Block())

        @block.tensor
        def _(pe):
            for b in range(B):
                if b >= 2:
                    pe.wait_ge(qk_copied.sem, qk_copied.at(b - 1))
                    pe.wait_ge(vg_copied.sem, vg_copied.at(b - 1))
                for i in range(2):
                    ins = nc.tensor.matmul(qp[:, b % 2, i, :], w[:, i * P:(i + 1) * P], xnT[:, b * T:(b + 1) * T], start=True, stop=True)
                ins.then_inc(qk_ready.sem, 1)
                for t in range(TPB):
                    n = b * TPB + t
                    ins = nc.tensor.matmul(vp[:, b % 2, t * P:(t + 1) * P], xnT[:, n * P:(n + 1) * P], w[:, 2 * P:3 * P], start=True, stop=True)
                ins.then_inc(vg_ready.sem, 1)

        @block.scalar
        def _(act):
            act.wait_ge(expd.sem, expd.at(1))
            nc.scalar.activation(dt[:, :], dt[:, :], ACT.Exp, scale=-1.0).then_inc(expd.sem, 1)
            act.wait_ge(expd.sem, expd.at(2))
            nc.scalar.activation(dt[:, :], dt[:, :], ACT.Ln, bias=1.0).then_inc(expd.sem, 1)
            for b in range(B):
                act.wait_ge(qk_ready.sem, qk_ready.at(b + 1))
                if b >= 2:
                    act.wait_ge(cut_ready.sem, cut_ready.at(b - 1))
                nc.scalar.activation(qk[:, b % 2, 0, :], qp[:, b % 2, 0, :], ACT.Copy, scale=float(A_HD) ** -0.5)
                nc.scalar.activation(qk[:, b % 2, 1, :], qp[:, b % 2, 1, :], ACT.Copy).then_inc(qk_copied.sem, 1)
                act.wait_ge(vg_ready.sem, vg_ready.at(b + 1))
                nc.scalar.activation(V1[:, b * TPB:(b + 1) * TPB, :, 0:A_HD],
                                     vp[:, b % 2, :].rearrange("p (n h c) -> p n h c", h=A_HEADS, c=A_HD), ACT.Copy).then_inc(vg_copied.sem, 1)

        @block.vector
        def _(dve):
            own = Steps(dve, S["dve"])
            own.link(nc.vector.tensor_scalar(dt[:, :], drow[:, :], -1.0, None, ALU.mult))
            nc.vector.tensor_tensor(dt[:, :], dt[:, :], drow[:, :], ALU.max).then_inc(expd.sem, 1)
            own.link(nc.vector.tensor_scalar(sp_[:, :], drow[:, :], 0.0, None, ALU.max))
            for b in range(B):
                dve.wait_ge(qk_copied.sem, qk_copied.at(b + 1))
                if b >= 2:
                    dve.wait_ge(cut_stored[b % 2].sem, cut_stored[b % 2].at(6 * 16 * (b // 2)))
                c = cut[:, b % 2, :, :, :]
                split3(own, nc, qk[:, b % 2, :, :], rest[:, :, :], c[:, :, 0, :], c[:, :, 1, :], c[:, :, 2, :]).then_inc(cut_ready.sem, 1)
                dve.wait_ge(cut_ready.sem, cut_ready.at(b + 1))
            dve.wait_ge(expd.sem, expd.at(3))
            own.link(nc.vector.tensor_tensor(sp_[:, :], sp_[:, :], dt[:, :], ALU.add))
            for h in range(A_HEADS):
                own.link(nc.vector.tensor_scalar(weight[:, h, :], log_dist[:, :], sp_[:, h:h + 1], 1.0, ALU.mult, ALU.add))
                nc.vector.reciprocal(weight[:, h, :], weight[:, h, :])
            own.close()

        @block.gpsimd
        def _(pool):
            nc.gpsimd.memset(V1[:, :, :, A_HD:A_HD + 1], 1.0)

        @block.sync
        def _(sp):
            for b in range(B):
                sp.wait_ge(cut_ready.sem, cut_ready.at(b + 1))
                for i, dram in enumerate((parts_q, parts_k)):
                    for part in range(3):
                        sp.dma_start(dram[part, :, b, :], cut[:, b % 2, i, part, :]).then_inc(cut_stored[b % 2].sem, 16)
            for half in cut_stored:
                sp.wait_ge(half.sem, half.at(6 * 16 * (B // 2)))

    for s in (qk_ready, qk_copied, cut_ready, vg_ready, vg_copied):
        s.passed(B)
    for half in cut_stored:
        half.passed(6 * 16 * (B // 2))
    expd.passed(3)


def decay_heads(nc, S, parts_q, parts_k, V1, weight, Y, C, ident):
    U = A_HEADS * TPB
    with ExitStack() as ctx:
        room = Room(nc, ctx)
        KC = len(CUTS) * A_HD
        qs, ks = (room.sb(n, [KC, 2, A_HEADS, T], BF16) for n in ("qs", "ks"))
        prob, probT = room.sb("prob", [P, TPB, T]), room.sb("probT", [P, 2, T])
        nmax, inv = room.sb("nmax", [P, TPB]), room.sb("inv", [P, TPB, A_HEADS])
        sc, tp = room.ps("sc", [P, 2, T]), room.ps("tp", [P, 2, T])
        ob = room.ps("ob", [P, 2, TPB, A_HEADS, 16])
        loaded = S["loaded0"], S["loaded1"]
        scored, maxed, expd, turned, copied, valued, normed = (
            S["a_" + k] for k in ("scored", "maxed", "expd", "turned", "copied", "valued", "normed"))
        PER_LOAD = 2 * len(CUTS) * 16
        block = ctx.enter_context(nc.Block())

        @block.sync
        def _(sp):
            for b in range(B):
                if b >= 2:
                    sp.wait_ge(scored.sem, scored.at(U * (b - 1)))
                for c, (pq, pk) in enumerate(CUTS):
                    for dst, dram, part in ((qs, parts_q, pq), (ks, parts_k, pk)):
                        sp.dma_start(dst[c * A_HD:(c + 1) * A_HD, b % 2, :, :],
                                     dram[part, :, b, :].rearrange("(h d) t -> d h t", d=A_HD)).then_inc(loaded[b % 2].sem, 16)

        @block.tensor
        def _(pe):
            def scores(half, b, h, qi):
                u = b * U + h * TPB + qi
                pe.wait_ge(expd.sem, expd.at(u - 1))
                head = bass.ds(h, 1)
                s = sc[:, qi % 2, 0:(qi + 1) * P]
                nc.tensor.matmul(s, qs[:, half, head, qi * P:(qi + 1) * P].rearrange("p a t -> p (a t)"),
                                 ks[:, half, head, 0:(qi + 1) * P].rearrange("p a t -> p (a t)"), start=True, stop=False)
                nc.tensor.matmul(s[:, qi * P:(qi + 1) * P], C["identb"][:, :], C["above"][:, :], start=False, stop=True).then_inc(scored.sem, 1)

            def transposes(half, b, h, qi):
                u = b * U + h * TPB + qi
                pe.wait_ge(expd.sem, expd.at(u + 1))
                pe.wait_ge(copied.sem, copied.at(u - 1))
                for kj in range(qi + 1):
                    at = (qi - kj) * P
                    ins = nc.tensor.transpose(tp[:, qi % 2, at:at + P], prob[:, qi, kj * P:(kj + 1) * P], ident[:, :])
                ins.then_inc(turned.sem, 1)

            def values(half, b, h, qi):
                u = b * U + h * TPB + qi
                pe.wait_ge(copied.sem, copied.at(u + 1))
                for kj in range(qi + 1):
                    at = (qi - kj) * P
                    ins = nc.tensor.matmul(ob[:, half, qi, bass.ds(h, 1), 0:A_HD + 1].rearrange("p a c -> p (a c)"),
                                           probT[:, qi % 2, at:at + P],
                                           V1[:, bass.ds(b * TPB + kj, 1), bass.ds(h, 1), :].rearrange("p a e c -> p (a e c)"),
                                           start=(kj == 0), stop=(kj == qi))
                ins.then_inc(valued.sem, 1)

            def head(half, b, h, ahead=True, behind=True, last=True):
                for qi in range(TPB):
                    if ahead:
                        scores(half, b, h, qi)
                    if behind:
                        transposes(half, b, h - 1, qi)
                    if qi == 0 and last:
                        values(half, b, h - 2, TPB - 1)
                    if qi >= 1 and behind:
                        values(half, b, h - 1, qi - 1)

            with pe.Fori(0, B // 2) as pair:
                for half in range(2):
                    b = pair * 2 + half
                    pe.wait_ge(loaded[half].sem, loaded[half].at(PER_LOAD * (pair + 1)))
                    pe.wait_ge(normed.sem, normed.at(b - 1))
                    head(half, b, 0, behind=False, last=False)
                    head(half, b, 1, last=False)
                    with pe.Fori(2, A_HEADS) as h:
                        head(half, b, h)
                    head(half, b, A_HEADS, ahead=False)
                    values(half, b, A_HEADS - 1, TPB - 1)

        @block.scalar
        def _(act):
            with act.Fori(0, B * A_HEADS) as g:
                for qi in range(TPB):
                    u = g * TPB + qi
                    act.wait_ge(turned.sem, turned.at(u - 3))
                    act.wait_ge(maxed.sem, maxed.at(u + 1))
                    w = (qi + 1) * P
                    nc.scalar.activation(prob[:, qi, 0:w], sc[:, qi % 2, 0:w], ACT.Exp, bias=nmax[:, qi:qi + 1]).then_inc(expd.sem, 1)

        @block.vector
        def _(dve):
            own = Steps(dve, S["dve"])

            def largest(b, h, qi):
                u = b * U + h * TPB + qi
                dve.wait_ge(scored.sem, scored.at(u + 1))
                nc.vector.tensor_reduce(nmax[:, qi:qi + 1], sc[:, qi % 2, 0:(qi + 1) * P], AX.X, ALU.max, negate=True).then_inc(maxed.sem, 1)

            def weigh(b, h, qi):
                u = b * U + h * TPB + qi
                w = (qi + 1) * P
                dve.wait_ge(valued.sem, valued.at(u - 1))
                dve.wait_ge(turned.sem, turned.at(u + 1))
                nc.vector.tensor_tensor(probT[:, qi % 2, 0:w], tp[:, qi % 2, 0:w],
                                        weight[:, bass.ds(h, 1), 0:w].rearrange("p a t -> p (a t)"), ALU.mult).then_inc(copied.sem, 1)

            def head(b, h, ahead=True, behind=True):
                for qi in range(TPB):
                    if ahead:
                        largest(b, h, qi)
                    if behind:
                        weigh(b, h - 1, qi)

            with dve.Fori(0, B // 2) as pair:
                own.enter(pair, 2)
                for half in range(2):
                    b = pair * 2 + half
                    head(b, 0, behind=False)
                    with dve.Fori(1, A_HEADS) as h:
                        head(b, h)
                    head(b, A_HEADS, ahead=False)
                    dve.wait_ge(valued.sem, valued.at((b + 1) * U))
                    dve.wait_ge(normed.sem, normed.at(b))
                    own.link(nc.vector.reciprocal(inv[:, :, :], ob[:, half, :, :, A_HD]))
                    dst = Y[:, bass.ds(b * TPB, TPB), :].rearrange("p n (h c) -> p n h c", c=A_HD)
                    nc.vector.tensor_tensor(dst, ob[:, half, :, :, 0:A_HD], inv[:, :, :].unsqueeze(3).broadcast_to([P, TPB, A_HEADS, A_HD]),
                                            ALU.mult).then_inc(normed.sem, 1)
            own.leave(B // 2)
            own.close()

    for half in loaded:
        half.passed(PER_LOAD * (B // 2))
    for s in (scored, maxed, expd, turned, copied, valued):
        s.passed(U * B)
    normed.passed(B)


def attention_decay(nc, S, X, C, D, ident):
    with ExitStack() as ctx:
        room = Room(nc, ctx)
        Y, wo = room.sb("Y", [P, NT, P]), room.sb("wo", [P, 1, P])
        V1, weight = room.sb("V1", [P, NT, A_HEADS, A_HD + 1]), room.sb("weight", [P, A_HEADS, T])
        parts_q, parts_k = (nc.dram_tensor(n, (3, P, B, T), BF16, kind="Internal").ap() for n in ("parts_q", "parts_k"))
        big = S["big"]
        with ExitStack() as inner:
            iroom = Room(nc, inner)
            xnT, w = iroom.sb("xnT", [P, B * T]), iroom.sb("w", [P, 3 * P])
            drow, log_dist = iroom.sb("drow", [P, A_HEADS]), iroom.sb("log_dist", [P, T])
            with nc.Block() as block:
                @block.sync
                def _(sp):
                    sp.dma_start(w[:, :], D["at_w"]).then_inc(big.sem, 16)
                    sp.dma_start(drow[:, :], D["at_decay"].broadcast_to([P, A_HEADS])).then_inc(big.sem, 16)
                    sp.dma_start(log_dist[:, :], D["log_dist"]).then_inc(big.sem, 16)
                    sp.dma_start(wo[:, :, :], D["at_wo"].rearrange("p (a n) -> p a n", a=1)).then_inc(big.sem, 16)
            norm_transpose(nc, S, X, xnT, ident)
            with nc.Block() as block:
                @block.sync
                def _(sp):
                    sp.wait_ge(big.sem, big.at(4 * 16))
            big.passed(4 * 16)
            decay_project(nc, S, xnT, w, drow, log_dist, V1, weight, parts_q, parts_k)
        decay_heads(nc, S, parts_q, parts_k, V1, weight, Y, C, ident)
        project_add(nc, S, X, Y, wo, ident, 1)


def ffn0(nc, S, X, C, D, ident):
    E, F = FF0_EXPERTS, (FF0_EXPERTS + 1) * FF0_DIM
    FT = F // P
    with ExitStack() as ctx:
        room = Room(nc, ctx)
        Wg, Wu, Wd = room.sb("Wg", [P, F]), room.sb("Wu", [P, F]), room.sb("Wd", [P, F // P, P])
        Wr, gb, sel = room.sb("Wr", [P, E]), room.sb("gb", [P, 2]), room.sb("sel", [96, F], BF16)
        xnT, gateT = room.sb("xnT", [P, B * T]), room.sb("gateT", [96, B * T], BF16)
        small, big = S["small"], S["big"]
        with nc.Block() as block:
            @block.sync
            def _(sp):
                sp.dma_start(gb[:, :], D["ff0_gb"]).then_inc(small.sem, 16)
                sp.dma_start(Wr[:, :], D["ff0_wr"]).then_inc(small.sem, 16)
                sp.dma_start(Wg[:, :], D["ff0_wg"]).then_inc(big.sem, 16)
                sp.dma_start(Wu[:, :], D["ff0_wu"]).then_inc(big.sem, 16)
                sp.dma_start(sel[:, :], D["ff0_sel"]).then_inc(big.sem, 16)
                sp.dma_start(Wd[:, :, :], D["ff0_wd"]).then_inc(big.sem, 16)
                sp.wait_ge(small.sem, small.at(32))
        small.passed(32)
        norm_transpose(nc, S, X, xnT, ident, True, gb[:, 0:1], gb[:, 1:2])
        route(nc, S, xnT, Wr, E, False, FF0_CAPACITY, gateT, C)
        experts(nc, S, X, xnT, gateT, sel, Wg, Wu, Wd, FT, ident, big.sem, big.at(64))
        big.passed(64)


def ffn1(nc, S, X, C, D, ident):
    E, F = FF1_EXPERTS, (FF1_EXPERTS + 1) * FF1_DIM
    FT = -(-F // P)
    with ExitStack() as ctx:
        room = Room(nc, ctx)
        Wg, Wu, Wd = room.sb("Wg", [P, FT * P]), room.sb("Wu", [P, FT * P]), room.sb("Wd", [P, FT, P])
        Wr, sel = room.sb("Wr", [P, E + 1]), room.sb("sel", [96, FT * P], BF16)
        xnT, gateT = room.sb("xnT", [P, B * T]), room.sb("gateT", [96, B * T], BF16)
        small, big, padded = S["small"], S["big"], S["wpad"]
        whole = F // P
        with nc.Block() as block:
            @block.sync
            def _(sp):
                sp.dma_start(Wr[:, :], D["ff1_wr"]).then_inc(small.sem, 16)
                sp.wait_ge(padded.sem, padded.at(1))
                sp.dma_start(Wg[:, 0:F], D["ff1_wg"]).then_inc(big.sem, 16)
                sp.dma_start(Wu[:, 0:F], D["ff1_wu"]).then_inc(big.sem, 16)
                sp.dma_start(sel[:, :], D["ff1_sel"]).then_inc(big.sem, 16)
                sp.dma_start(Wd[:, 0:whole, :], D["ff1_wd"][0:whole * P, :].rearrange("(f p) d -> p f d", p=P)).then_inc(big.sem, 16)
                sp.dma_start(Wd[0:F - whole * P, whole, :], D["ff1_wd"][whole * P:F, :]).then_inc(big.sem, 16)
                sp.wait_ge(small.sem, small.at(16))

            @block.gpsimd
            def _(pool):
                nc.gpsimd.memset(Wg[:, F:], 0.0)
                nc.gpsimd.memset(Wu[:, F:], 0.0)
                nc.gpsimd.memset(Wd[:, whole, :], 0.0).then_inc(padded.sem, 1)
        small.passed(16)
        padded.passed(1)
        norm_transpose(nc, S, X, xnT, ident)
        route(nc, S, xnT, Wr, E, True, None, gateT, C)
        experts(nc, S, X, xnT, gateT, sel, Wg, Wu, Wd, FT, ident, big.sem, big.at(80))
        big.passed(80)


SIGNALS = ["dve", "act", "pe", "var", "std", "norm", "turned", "copied", "pready", "padded", "have", "expd", "chosen",
           "counted", "parted", "proj", "silu", "hidden", "down", "small", "big", "wpad",
           "centred", "squared", "gated", "made", "qk_ready", "rotated", "vg_ready", "vg_copied",
           "picked", "scored", "decays", "rsummed", "rcopied", "aside",
           "w_lerped", "w_low", "w_tanhed", "w_high", "w_mixed", "w_px_full", "w_px_free", "w_decayed", "w_v_full",
           "w_v_used", "w_weighted", "w_summed", "w_bonused", "w_y_done", "w_e1",
           "a_weights", "a_projected", "a_rotated", "a_scored", "a_maxed", "a_expd", "a_turned", "a_copied", "a_valued", "a_normed",
           "qk_copied", "cut_ready", "cut_stored0", "cut_stored1", "loaded0", "loaded1"]


def mixed_model(nc, D, out):
    with ExitStack() as ctx:
        room = Room(nc, ctx)
        X = room.sb("X", [P, NT, P])
        ident = room.sb("ident", [P, P])
        C = {name: room.sb(name, shape, dt) for name, shape, dt in (
            ("identb", [P, P], BF16), ("upto", [P, P], BF16), ("ones", [P, P], BF16), ("above", [P, P], BF16),
            ("rank", [P, 8], F32))}
        start = ctx.enter_context(nc.semaphore("start"))
        stored = ctx.enter_context(nc.semaphore("stored"))
        S = {name: Signal(nc, ctx, "s_" + name) for name in SIGNALS}

        with nc.Block() as block:
            @block.sync
            def _(sp):
                for s in S.values():
                    sp.sem_inc(s.sem, LEAD)
                sp.dma_start(X[:, :, :], D["x"].rearrange("(n p) d -> p n d", p=P)).then_inc(start, 16)
                sp.dma_start(ident[:, :], D["ident"]).then_inc(start, 16)
                for name in C:
                    sp.dma_start(C[name][:, :], D[name]).then_inc(start, 16)
                sp.wait_ge(start, 16 * (2 + len(C)))

        steps = {1: attention_decay, 2: ffn0, 3: recurrent, 4: ffn0, 5: attention_mqa, 6: ffn1, 7: retention, 8: ffn1}
        for layer in LAYERS:
            steps[layer](nc, S, X, C, D, ident)

        with nc.Block() as block:
            @block.sync
            def _(sp):
                sp.dma_start(out.rearrange("(n p) d -> p n d", p=P), X[:, :, :]).then_inc(stored, 16)
                sp.wait_ge(stored, 16)


def constants():
    import numpy as np

    def bf(a):
        return (np.ascontiguousarray(a, np.float32).view(np.uint32) >> 16).astype(np.uint16)

    f32 = np.float32
    p = np.arange(P)
    c = {"ident": np.eye(P, dtype=f32), "identb": bf(np.eye(P)),
         "upto": bf(p[:, None] <= p[None, :]), "ones": bf(np.ones((P, P))),
         "above": bf(np.where(p[None, :] > p[:, None], MASKED, 0.0)),
         "rank": np.broadcast_to(8.0 - np.arange(8), (P, 8)).astype(f32)}
    for name, e, d in (("ff0_sel", FF0_EXPERTS + 1, FF0_DIM), ("ff1_sel", FF1_EXPERTS + 1, FF1_DIM)):
        sel = np.zeros((96, -(-e * d // P) * P), f32)
        for part in range(3):
            for k in range(e):
                sel[32 * part + k, k * d:(k + 1) * d] = 1.0
        c[name] = bf(sel)
    i = np.arange(T)
    dist = np.maximum(i[None, :] - p[:, None], 0).astype(f32)
    c["log_dist"] = np.log1p(dist).astype(f32)
    inv = (1.0 / 10000.0 ** (np.arange(0, M_HD, 2, dtype=f32) / f32(M_HD))).astype(f32)
    freq = i.astype(f32)[:, None] * inv[None, :]
    cos, sin = np.cos(freq).astype(f32).T, np.sin(freq).astype(f32).T
    c["rope_cos"] = np.concatenate([cos] * 4, 0)
    c["rope_sin"] = np.concatenate([-sin, sin, -sin, sin], 0)
    c["rope_k_cos"], c["rope_k_sin"] = (c[n] * f32(M_HD ** -0.5) for n in ("rope_cos", "rope_sin"))
    half = P // 2
    sv = ((np.arange(0, P, 2, dtype=f32) + f32(0.4 * P)) / f32(1.4 * P)).astype(f32)
    scale = (sv[None, :] ** (i.astype(f32)[:, None] / f32(512.0))).astype(f32)
    invf = (1.0 / 10000.0 ** (np.arange(half, dtype=f32) / f32(half))).astype(f32)
    sinu = i.astype(f32)[:, None] * invf[None, :]
    si, co = np.sin(sinu).astype(f32), np.cos(sinu).astype(f32)
    sign = np.where(np.arange(P) % 2 == 0, -1.0, 1.0).astype(f32)
    s_, e_ = np.log(1.0 / 32.0), np.log(1.0 / 512.0)
    gamma = (1.0 - np.exp(np.linspace(s_, e_, R_HEADS).astype(f32))).astype(f32)
    ld = np.log(gamma).astype(f32)
    expo = np.maximum(i[:, None] - i[None, :], 0).astype(f32)
    tri = (i[:, None] >= i[None, :]).astype(f32)
    mask = np.exp(ld[:, None, None] * expo) * tri
    row = np.sqrt(mask.sum(-1))
    per = np.repeat(1.0 / row, R_DK, axis=0).T * f32(R_DK) ** -0.5
    for name, sc, extra in (("xq", scale, per), ("xk", 1.0 / scale, np.ones((T, P)))):
        c[name + "_cos"] = np.ascontiguousarray((np.repeat(co * sc, 2, -1) * extra).T.astype(f32))
        c[name + "_sin"] = np.ascontiguousarray((np.repeat(si * sc, 2, -1) * extra * sign[None, :]).T.astype(f32))
    causal = (i[None, :] >= p[:, None]).astype(f32)
    c["decays"] = np.ascontiguousarray((np.exp(ld[:, None, None] * dist[None]) * causal[None]).transpose(1, 0, 2).astype(f32))
    c["head_rows"] = np.ascontiguousarray((p[:, None] // R_DK == np.arange(R_HEADS)[None, :]).astype(f32))
    same = (p[:, None] // W_HD == p[None, :] // W_HD).astype(f32)
    c["head_sum"] = same
    c["head_to"] = np.ascontiguousarray(np.stack([same * (p[None, :] % W_HD == j) for j in range(W_HD)], 1).astype(f32))
    return c


def kernel(**inputs):
    import numpy as _np
    import concourse.bacc as _bacc
    from concourse import mybir as _mybir
    from concourse.bass_utils import run_bass_kernel_spmd as _run

    def a(name):
        return _np.asarray(inputs[name])

    cc = _np.ascontiguousarray
    data = {
        "x": a("L0_attn_a_x").reshape(B * T, P),
        "at_w": a("L0_attn_a_w_attn"), "at_wo": a("L0_attn_a_w_proj"), "at_decay": a("L0_attn_a_decay_raw").reshape(1, A_HEADS),
        "ff0_gb": cc(_np.stack([a("L0_ffn_ln_g"), a("L0_ffn_ln_b")], 1)), "ff0_wr": a("L0_ffn_Wr"),
        "ff0_wg": cc(_np.concatenate([a("L0_ffn_W1"), a("L0_ffn_W1s")[None]]).transpose(1, 0, 2).reshape(P, -1)),
        "ff0_wu": cc(_np.concatenate([a("L0_ffn_W3"), a("L0_ffn_W3s")[None]]).transpose(1, 0, 2).reshape(P, -1)),
        "ff0_wd": cc(_np.concatenate([a("L0_ffn_W2"), a("L0_ffn_W2s")[None]]).reshape(-1, P, P).transpose(1, 0, 2)),
        "ff1_wr": cc(_np.concatenate([a("L1_ffn_gate_w"), a("L1_ffn_shared_gate_w")]).T),
        "ff1_wg": cc(_np.concatenate([a("L1_ffn_w_gate"), a("L1_ffn_sw_gate")[None]]).transpose(1, 0, 2).reshape(P, -1)),
        "ff1_wu": cc(_np.concatenate([a("L1_ffn_w_up"), a("L1_ffn_sw_up")[None]]).transpose(1, 0, 2).reshape(P, -1)),
        "ff1_wd": cc(_np.concatenate([a("L1_ffn_w_down"), a("L1_ffn_sw_down")[None]]).reshape(-1, P)),
    }
    wq = a("L1_attn_a_Wq")
    h64 = _np.arange(M_HD)
    turn = _np.where(h64 < M_HD // 2, h64 + M_HD // 2, h64 - M_HD // 2)
    heads = wq.reshape(P, M_HEADS, M_HD)
    data["mq_wq"] = cc(_np.stack([heads, heads[:, :, turn]], 1).reshape(P, 2, M_HEADS // 2, P).transpose(2, 0, 1, 3))
    wk, wv = a("L1_attn_a_Wkv")[:, :M_HD], a("L1_attn_a_Wkv")[:, M_HD:]
    data["mq_wk"] = cc(_np.stack([_np.concatenate([wk, wk], 1), _np.concatenate([wk[:, turn]] * 2, 1)], 1))
    data["mq_wv"] = cc(wv)
    data["mq_wo"] = cc(a("L1_attn_a_Wo").reshape(M_HEADS * M_HD // P, P, P).transpose(1, 0, 2))
    pair = _np.arange(P) ^ 1
    w = a("L1_attn_b_w_qkv")
    bq = a("L1_attn_b_b_qkv")
    q, k = slice(0, P), slice(P, 2 * P)
    data["re_wqk"] = cc(_np.stack([w[:, q], w[:, q][:, pair], w[:, k], w[:, k][:, pair]], 1))
    data["re_bqk"] = cc(_np.stack([bq[q], bq[q][pair], bq[k], bq[k][pair]], 1))
    data["re_wv"], data["re_bv"] = cc(w[:, 2 * P:]), cc(bq[None, 2 * P:])
    data["re_wg"], data["re_bg"] = a("L1_attn_b_w_g"), a("L1_attn_b_b_g")[None]
    data["re_wp"] = cc(a("L1_attn_b_w_p").reshape(2, P, P).transpose(1, 0, 2))
    data["re_bp"] = a("L1_attn_b_b_p")[None]
    data["rw_la"] = cc(_np.stack([a(f"L0_attn_b_{n}_la").T for n in "rkvgd"], 1))
    data["rw_lb"] = cc(_np.stack([a(f"L0_attn_b_{n}_lb").T for n in "rkvgd"], 1))
    data["rw_cols"] = cc(_np.stack([a(f"L0_attn_b_{n}_ll") for n in "rkvgd"] + [a("L0_attn_b_xw"), a("L0_attn_b_u")], 1))
    data["rw_w"] = cc(_np.stack([a(f"L0_attn_b_{n}W").T for n in "rkvgo"], 1))
    vt = a("L0_attn_b_vW").T.reshape(P, W_HEADS, W_HD)
    data["rw_wvj"] = cc(_np.repeat(vt.transpose(0, 2, 1)[..., None], W_HD, -1).reshape(P, W_HD, P))
    data["rw_init"] = a("L0_attn_b_init_state").reshape(P, W_HD)
    data["rw_ln"] = cc(_np.stack([a("L0_attn_b_ln_w"), a("L0_attn_b_ln_b")]).reshape(1, 2 * W_HD))
    data.update(constants())

    nc = _bacc.Bacc("TRN2", target_bir_lowering=False, num_devices=1)
    arrays, aps = {}, {}
    for name, v in data.items():
        v = cc(v)
        arrays[f"in_{name}"] = v
        aps[name] = nc.dram_tensor(f"in_{name}", v.shape, _mybir.dt.from_np(v.dtype), kind="ExternalInput").ap()
        if v.dtype == _np.uint16:
            aps[name] = aps[name].bitcast(BF16)
    out = nc.dram_tensor("out_x", (B * T, P), F32, kind="ExternalOutput").ap()
    mixed_model(nc, aps, out)
    r = _run(nc, [arrays], core_ids=[0])
    return r.results[0]["out_x"].reshape(B, T, P)
```

```python
from contextlib import ExitStack

import concourse.bass as bass
from concourse import mybir

F32 = mybir.dt.float32
BF16 = mybir.dt.bfloat16
U32 = mybir.dt.uint32
ALU = mybir.AluOpType
ACT = mybir.ActivationFunctionType
AX = mybir.AxisListType

P = 128
B, T = 4, 512
TPB = T // P
NT = B * TPB
EPS = 1e-5
LEAD = 8
LAYERS = (1, 2, 3, 4, 5, 6, 7, 8)

A_HEADS, A_HD = 16, 8
W_HEADS, W_HD, LORA = 16, 8, 64
FF0_EXPERTS, FF0_DIM = 7, 512
FF0_CAPACITY = -(-5 * (B * T // 2) * 2 // (4 * FF0_EXPERTS))
M_HEADS, M_HD = 16, 64
FF1_EXPERTS, FF1_DIM = 8, 176
R_HEADS, R_DK, R_DV = 8, 16, 32
MASKED = -1e30


class Room:

    def __init__(self, nc, ctx):
        self.nc, self.ctx = nc, ctx

    def sb(self, name, shape, dt=F32):
        return self.ctx.enter_context(self.nc.sbuf_tensor(name, shape, dt, allow_name_mangling=True))

    def ps(self, name, shape, dt=F32):
        return self.ctx.enter_context(self.nc.psum_tensor(name, shape, dt, allow_name_mangling=True))


class Signal:

    def __init__(self, nc, ctx, name, lead=LEAD):
        self.sem = ctx.enter_context(nc.semaphore(name))
        self.lead = self.base = lead

    def at(self, n):
        return self.base + n

    def passed(self, n):
        self.base += n


class Steps:

    def __init__(self, engine, signal):
        self.engine, self.own_count, self.n = engine, signal, 0
        self.turn, self.per = None, 0

    def link(self, ins):
        self.n += 1
        ins.then_inc(self.own_count.sem, 1)
        n = self.n if self.turn is None else self.turn * self.per + self.n
        self.engine.wait_ge(self.own_count.sem, self.own_count.base + n)

    def enter(self, turn, per):
        self.turn, self.per, self.entered = turn, per, self.n

    def leave(self, turns):
        assert self.n - self.entered == self.per, (self.n - self.entered, self.per)
        self.n = self.entered + self.per * turns
        self.turn = None

    def close(self):
        self.own_count.passed(self.n)


def stand_alone(engine, signal):
    engine.sem_inc(signal.sem, 1)


def norm_transpose(nc, S, X, xnT, ident, twice=False, gain=None, shift=None, xn=None):
    rounds = 2 if twice else 1
    with ExitStack() as ctx:
        room = Room(nc, ctx)
        if xn is None:
            xn = room.sb("xn", [P, NT, P], F32)
        stats = room.sb("stats", [P, TPB, 6], F32)
        mv = room.sb("mv", [P, TPB, 2], F32)
        ve = room.sb("ve", [P, TPB], F32)
        sd = room.sb("sd", [P, TPB], F32)
        rs = room.sb("rs", [P, TPB], F32)
        tp = room.ps("tp", [P, B, T], F32)
        var_ready, std_ready, norm_ready, turned = S["var"], S["std"], S["norm"], S["turned"]
        block = ctx.enter_context(nc.Block())

        @block.vector
        def _(dve):
            own = Steps(dve, S["dve"])
            for r in range(rounds):
                src = X if r == 0 else xn
                if r:
                    dve.wait_ge(norm_ready.sem, norm_ready.at(r * B))
                for b in range(B):
                    for t in range(TPB):
                        ins = nc.vector.bn_stats(stats[:, t, :], src[:, b * TPB + t, :])
                    own.link(ins)
                    for t in range(TPB):
                        ins = nc.vector.bn_aggr(mv[:, t, :], stats[:, t, :])
                    own.link(ins)
                    nc.vector.tensor_scalar(ve[:, :], mv[:, :, 1], EPS, None, ALU.add).then_inc(var_ready.sem, 1)
                    dve.wait_ge(std_ready.sem, std_ready.at(r * B + b + 1))
                    own.link(nc.vector.reciprocal(rs[:, :], sd[:, :]))
                    for t in range(TPB):
                        ins = nc.vector.tensor_scalar(xn[:, b * TPB + t, :], src[:, b * TPB + t, :],
                                                      mv[:, t, 0:1], rs[:, t:t + 1], ALU.subtract, ALU.mult)
                    ins.then_inc(norm_ready.sem, 1)
            own.close()

        @block.scalar
        def _(act):
            for r in range(rounds):
                for b in range(B):
                    act.wait_ge(var_ready.sem, var_ready.at(r * B + b + 1))
                    nc.scalar.activation(sd[:, :], ve[:, :], ACT.Sqrt).then_inc(std_ready.sem, 1)
            for b in range(B):
                act.wait_ge(turned.sem, turned.at(b + 1))
                dst = xnT[:, b * T:(b + 1) * T]
                if gain is None:
                    nc.scalar.activation(dst, tp[:, b, :], ACT.Copy)
                else:
                    nc.scalar.activation(dst, tp[:, b, :], ACT.Identity, bias=shift, scale=gain)

        @block.tensor
        def _(pe):
            for b in range(B):
                pe.wait_ge(norm_ready.sem, norm_ready.at((rounds - 1) * B + b + 1))
                for t in range(TPB):
                    ins = nc.tensor.transpose(tp[:, b, t * P:(t + 1) * P], xn[:, b * TPB + t, :], ident[:, :])
                ins.then_inc(turned.sem, 1)

    for s in (var_ready, std_ready, norm_ready):
        s.passed(rounds * B)
    turned.passed(B)


def project_add(nc, S, X, Y, W, ident, KT, bias_row=None, ones_row=None):
    with ExitStack() as ctx:
        room = Room(nc, ctx)
        yT = room.sb("yT", [P, 2, KT * P], F32)
        tp = room.ps("tp", [P, 2, max(KT * P, 512)], F32)
        op = room.ps("op", [P, 2, 512], F32)
        turned, copied, ready, added = S["turned"], S["copied"], S["pready"], S["padded"]
        block = ctx.enter_context(nc.Block())

        @block.tensor
        def _(pe):
            def transposes(n):
                if n >= 2:
                    pe.wait_ge(copied.sem, copied.at(n - 1))
                for k in range(KT):
                    ins = nc.tensor.transpose(tp[:, n % 2, k * P:(k + 1) * P], Y[:, n, k * P:(k + 1) * P], ident[:, :])
                ins.then_inc(turned.sem, 1)

            transposes(0)
            for n in range(NT):
                if n + 1 < NT:
                    transposes(n + 1)
                pe.wait_ge(copied.sem, copied.at(n + 1))
                if n >= 2:
                    pe.wait_ge(added.sem, added.at(n - 1))
                for k in range(KT):
                    ins = nc.tensor.matmul(op[:, n % 2, 0:P], yT[:, n % 2, k * P:(k + 1) * P], W[:, k, :],
                                           start=(k == 0), stop=(k == KT - 1 and bias_row is None))
                if bias_row is not None:
                    ins = nc.tensor.matmul(op[:, n % 2, 0:P], ones_row, bias_row, start=False, stop=True)
                ins.then_inc(ready.sem, 1)

        @block.scalar
        def _(act):
            for n in range(NT):
                act.wait_ge(turned.sem, turned.at(n + 1))
                if n >= 2:
                    act.wait_ge(ready.sem, ready.at(n - 1))
                for half in range(-(-KT * P // 512)):
                    lo, hi = half * 512, min(KT * P, half * 512 + 512)
                    ins = nc.scalar.activation(yT[:, n % 2, lo:hi], tp[:, n % 2, lo:hi], ACT.Copy)
                ins.then_inc(copied.sem, 1)

        @block.vector
        def _(dve):
            for n in range(NT):
                dve.wait_ge(ready.sem, ready.at(n + 1))
                nc.vector.tensor_tensor(X[:, n, :], X[:, n, :], op[:, n % 2, 0:P], ALU.add).then_inc(added.sem, 1)

    for s in (turned, copied, ready, added):
        s.passed(NT)


def split3(own, nc, value, rest, hi, mid, lo):
    own.link(nc.vector.tensor_copy(hi, value))
    own.link(nc.vector.tensor_tensor(rest, value, hi, ALU.subtract))
    own.link(nc.vector.tensor_copy(mid, rest))
    return nc.vector.tensor_tensor(lo, rest, mid, ALU.subtract)


def route(nc, S, xnT, Wr, E, extra, capacity, gateT, C):
    EX = E + 1
    with ExitStack() as ctx:
        room = Room(nc, ctx)
        lg, l2 = room.sb("lg", [P, NT, 8]), room.sb("l2", [P, NT, 8])
        cand, m1 = room.sb("cand", [P, NT, 8]), room.sb("m1", [P, NT])
        v1, v2, ex, den, sg = room.sb("v1", [P, NT]), room.sb("v2", [P, NT]), room.sb("ex", [P, NT]), room.sb("den", [P, NT]), room.sb("sg", [P, NT])
        o = room.sb("o", [P, 2 * NT, 8])
        g = room.sb("g", [P, 2 * NT])
        ob = room.sb("ob", [P, 2 * NT, 8], BF16)
        run_a, run_b, pos = room.sb("run_a", [P, 2 * NT, 8]), room.sb("run_b", [P, 2 * NT, 8]), room.sb("pos", [P, 2 * NT, 8])
        comb = room.sb("comb", [P, NT, 9])
        rest = room.sb("rest", [P, NT, 9])
        parts = room.sb("parts", [P, NT, 96], BF16)
        lp = room.ps("lp", [P, 512], F32)
        cp = room.ps("cp", [P, 2, 512], F32)
        gp = room.ps("gp", [P, NT, P], BF16)
        logits = lp[:, 0:NT * 16].rearrange("p (n e) -> p n e", e=16)
        up_to = cp[:, 0, 0:2 * NT * 8].rearrange("p (n e) -> p n e", e=8)
        total = cp[:, 1, 0:2 * NT * 8].rearrange("p (n e) -> p n e", e=8)
        have, expd, chosen, counted, parted, turned = S["have"], S["expd"], S["chosen"], S["counted"], S["parted"], S["turned"]
        block = ctx.enter_context(nc.Block())

        @block.tensor
        def _(pe):
            ncol = EX if extra else E
            for n in range(NT):
                ins = nc.tensor.matmul(logits[:, n, 0:ncol], xnT[:, n * P:(n + 1) * P], Wr[:, 0:ncol], start=True, stop=True)
            ins.then_inc(have.sem, 1)
            if capacity:
                pe.wait_ge(chosen.sem, chosen.at(1))
                flat = ob[:, :, :].rearrange("p n e -> p (n e)")
                nc.tensor.matmul(cp[:, 0, 0:2 * NT * 8], C["upto"][:, :], flat, start=True, stop=True)
                nc.tensor.matmul(cp[:, 1, 0:2 * NT * 8], C["ones"][:, :], flat, start=True, stop=True).then_inc(counted.sem, 1)
            pe.wait_ge(parted.sem, parted.at(1))
            for n in range(NT):
                ins = nc.tensor.transpose(gp[0:96, n, :], parts[:, n, :], C["identb"][:, :])
            ins.then_inc(turned.sem, 1)

        @block.scalar
        def _(act):
            act.wait_ge(expd.sem, expd.at(1))
            nc.scalar.activation(ex[:, :], ex[:, :], ACT.Exp)
            if extra:
                nc.scalar.activation(sg[:, :], sg[:, :], ACT.Exp, scale=-1.0)
            nc.scalar.activation(m1[:, 0:1], m1[:, 0:1], ACT.Copy).then_inc(expd.sem, 1)
            act.wait_ge(turned.sem, turned.at(1))
            for h in range(2):
                nc.scalar.activation(gateT[:, h * 1024:(h + 1) * 1024],
                                     gp[0:96, h * 8:(h + 1) * 8, :].rearrange("p n t -> p (n t)"), ACT.Copy)

        @block.vector
        def _(dve):
            own = Steps(dve, S["dve"])
            link = own.link

            def bc(a, w=8):
                return a.unsqueeze(2).broadcast_to([P, a.shape[1], w])

            rank = C["rank"][:, 0:8].unsqueeze(1).broadcast_to([P, NT, 8])
            nc.vector.memset(parts[:, :, :], 0.0)
            nc.vector.memset(comb[:, :, :], 1.0)
            link(nc.vector.memset(lg[:, :, :], -3e38))
            dve.wait_ge(have.sem, have.at(1))
            link(nc.vector.tensor_copy(lg[:, :, 0:E], logits[:, :, 0:E]))
            if extra:
                link(nc.vector.tensor_copy(sg[:, :], logits[:, :, E]))
            for k, (src, v) in enumerate(((lg, v1), (l2, v2))):
                link(nc.vector.tensor_reduce(v[:, :], src[:, :, :], AX.X, ALU.max))
                link(nc.vector.tensor_tensor(cand[:, :, :], src[:, :, :], bc(v[:, :]), ALU.is_equal))
                link(nc.vector.tensor_tensor(cand[:, :, :], cand[:, :, :], rank, ALU.mult))
                link(nc.vector.tensor_reduce(m1[:, :], cand[:, :, :], AX.X, ALU.max))
                link(nc.vector.tensor_tensor(o[:, k * NT:(k + 1) * NT, :], cand[:, :, :], bc(m1[:, :]), ALU.is_equal))
                if k == 0:
                    link(nc.vector.scalar_tensor_tensor(l2[:, :, :], o[:, 0:NT, :], MASKED, lg[:, :, :], ALU.mult, ALU.add))
            nc.vector.tensor_tensor(ex[:, :], v2[:, :], v1[:, :], ALU.subtract).then_inc(expd.sem, 1)
            if capacity:
                nc.vector.tensor_copy(ob[:, :, :], o[:, :, :]).then_inc(chosen.sem, 1)
                dve.wait_ge(counted.sem, counted.at(1))
                link(nc.vector.tensor_copy(run_a[:, :, :], total))
                a, b_ = run_a, run_b
                for sh in (1, 2, 4, 8, 16):
                    nc.vector.tensor_copy(b_[:, 0:sh, :], a[:, 0:sh, :])
                    link(nc.vector.tensor_tensor(b_[:, sh:, :], a[:, sh:, :], a[:, 0:2 * NT - sh, :], ALU.add))
                    a, b_ = b_, a
                link(nc.vector.tensor_tensor(pos[:, :, :], a[:, :, :], total, ALU.subtract))
                link(nc.vector.tensor_tensor(pos[:, :, :], pos[:, :, :], up_to, ALU.add))
                link(nc.vector.scalar_tensor_tensor(o[:, :, :], pos[:, :, :], capacity + 0.5, o[:, :, :], ALU.is_lt, ALU.mult))
            dve.wait_ge(expd.sem, expd.at(2))
            link(nc.vector.tensor_scalar(den[:, :], ex[:, :], 1.0, None, ALU.add))
            link(nc.vector.reciprocal(g[:, 0:NT], den[:, :]))
            link(nc.vector.tensor_tensor(g[:, NT:2 * NT], ex[:, :], g[:, 0:NT], ALU.mult))
            link(nc.vector.tensor_tensor(o[:, :, :], o[:, :, :], bc(g[:, :]), ALU.mult))
            link(nc.vector.tensor_tensor(comb[:, :, 0:E], o[:, 0:NT, 0:E], o[:, NT:2 * NT, 0:E], ALU.add))
            if extra:
                link(nc.vector.tensor_scalar(sg[:, :], sg[:, :], 1.0, None, ALU.add))
                link(nc.vector.reciprocal(comb[:, :, E], sg[:, :]))
            pv = [parts[:, :, 32 * i:32 * i + EX] for i in range(3)]
            split3(own, nc, comb[:, :, 0:EX], rest[:, :, 0:EX], *pv).then_inc(parted.sem, 1)
            own.close()

    for s in (have, parted, turned):
        s.passed(1)
    expd.passed(2)
    if capacity:
        chosen.passed(1)
        counted.passed(1)


def experts(nc, S, X, xnT, gateT, sel, Wg, Wu, Wd, FT, ident, loaded, loaded_at):
    with ExitStack() as ctx:
        room = Room(nc, ctx)
        sg = room.sb("sg", [P, 2, T], F32)
        su = room.sb("su", [P, 2, T], F32)
        hid = room.sb("hid", [P, 2, T], F32)
        oT = room.sb("oT", [P, T], F32)
        pa = room.ps("pa", [P, 2, T], F32)
        pu = room.ps("pu", [P, 2, T], F32)
        pg = room.ps("pg", [P, 2, T], F32)
        po = room.ps("po", [P, T], F32)
        py = room.ps("py", [P, T], F32)
        proj, silu, hidden, down, copied, turned, added = (
            S[k] for k in ("proj", "silu", "hidden", "down", "copied", "turned", "padded"))
        block = ctx.enter_context(nc.Block())

        @block.tensor
        def _(pe):
            pe.wait_ge(loaded, loaded_at)
            with pe.Fori(0, B) as c:
                tok = bass.ds(c * T, T)

                def down_product(f):
                    if f == 0:
                        pe.wait_ge(copied.sem, copied.at(c))
                    pe.wait_ge(hidden.sem, hidden.at(c * FT + f + 1))
                    ins = nc.tensor.matmul(po[:, :], Wd[:, f, :], hid[:, f % 2, :],
                                           start=(f == 0), stop=(f == FT - 1))
                    ins.then_inc(down.sem, 1)

                for f in range(FT):
                    if f != 1:
                        pe.wait_ge(hidden.sem, hidden.at(c * FT + max(f - 1, 0)))
                    cols = slice(f * P, f * P + P)
                    nc.tensor.matmul(pa[:, f % 2, :], Wg[:, cols], xnT[:, tok], start=True, stop=True)
                    nc.tensor.matmul(pu[:, f % 2, :], Wu[:, cols], xnT[:, tok], start=True, stop=True)
                    nc.tensor.matmul(pg[:, f % 2, :], sel[0:96, cols], gateT[0:96, tok],
                                     start=True, stop=True).then_inc(proj.sem, 1)
                    if f >= 1:
                        down_product(f - 1)
                down_product(FT - 1)
                pe.wait_ge(copied.sem, copied.at(c + 1))
                pe.wait_ge(added.sem, added.at(c))
                for t in range(TPB):
                    ins = nc.tensor.transpose(py[:, t * P:(t + 1) * P], oT[:, t * P:(t + 1) * P], ident[:, :])
                ins.then_inc(turned.sem, 1)

        @block.scalar
        def _(act):
            nc.scalar.preload_act_table(ACT.Silu)
            with act.Fori(0, B) as c:
                for f in range(FT):
                    act.wait_ge(proj.sem, proj.at(c * FT + f + 1))
                    nc.scalar.activation(sg[:, f % 2, :], pa[:, f % 2, :], ACT.Silu).then_inc(silu.sem, 1)
                act.wait_ge(down.sem, down.at(c * FT + FT))
                act.wait_ge(turned.sem, turned.at(c))
                nc.scalar.activation(oT[:, :], po[:, :], ACT.Copy).then_inc(copied.sem, 1)

        @block.vector
        def _(dve):
            own = Steps(dve, S["dve"])
            with dve.Fori(0, B) as c:
                own.enter(c, FT)
                for f in range(FT):
                    dve.wait_ge(silu.sem, silu.at(c * FT + f + 1))
                    own.link(nc.vector.tensor_tensor(su[:, f % 2, :], sg[:, f % 2, :], pu[:, f % 2, :], ALU.mult))
                    if f != 1:
                        dve.wait_ge(down.sem, down.at(c * FT + max(f - 1, 0)))
                    nc.vector.tensor_tensor(hid[:, f % 2, :], su[:, f % 2, :], pg[:, f % 2, :],
                                            ALU.mult).then_inc(hidden.sem, 1)
                dve.wait_ge(turned.sem, turned.at(c + 1))
                xs = X[:, bass.ds(c * TPB, TPB), :].rearrange("p n d -> p (n d)")
                nc.vector.tensor_tensor(xs, xs, py[:, :], ALU.add).then_inc(added.sem, 1)
            own.leave(B)
            own.close()

    for s in (proj, silu, hidden, down):
        s.passed(B * FT)
    for s in (copied, turned, added):
        s.passed(B)


def dispatch(nc, S, xnT, Wr, C, row_in, row_out, gates):
    E = FF0_EXPERTS
    with ExitStack() as ctx:
        room = Room(nc, ctx)
        lg, l2, cand = room.sb("lg", [P, NT, 8]), room.sb("l2", [P, NT, 8]), room.sb("cand", [P, NT, 8])
        m1, v1, v2, ex = room.sb("m1", [P, NT]), room.sb("v1", [P, NT]), room.sb("v2", [P, NT]), room.sb("ex", [P, NT])
        ob = room.sb("ob", [P, 2 * NT, 8], BF16)
        o, run_a, run_b, pos = (room.sb(n, [P, 2 * NT, 8]) for n in ("o", "run_a", "run_b", "pos"))
        kept, place, late = room.sb("kept", [P, 2 * NT]), room.sb("place", [P, 2 * NT]), room.sb("late", [P, 2 * NT])
        lp = room.ps("lp", [P, 512])
        cp = room.ps("cp", [P, 2, 512])
        logits = lp[:, 0:NT * 16].rearrange("p (n e) -> p n e", e=16)
        up_to = cp[:, 0, 0:2 * NT * 8].rearrange("p (n e) -> p n e", e=8)
        total = cp[:, 1, 0:2 * NT * 8].rearrange("p (n e) -> p n e", e=8)
        have, expd, chosen, counted = S["have"], S["expd"], S["chosen"], S["counted"]
        block = ctx.enter_context(nc.Block())

        @block.tensor
        def _(pe):
            for n in range(NT):
                ins = nc.tensor.matmul(logits[:, n, 0:E], xnT[:, n * P:(n + 1) * P], Wr[:, :], start=True, stop=True)
            ins.then_inc(have.sem, 1)
            pe.wait_ge(chosen.sem, chosen.at(1))
            flat = ob[:, :, :].rearrange("p n e -> p (n e)")
            nc.tensor.matmul(cp[:, 0, 0:2 * NT * 8], C["upto"][:, :], flat, start=True, stop=True)
            nc.tensor.matmul(cp[:, 1, 0:2 * NT * 8], C["ones"][:, :], flat, start=True, stop=True).then_inc(counted.sem, 1)

        @block.scalar
        def _(act):
            act.wait_ge(expd.sem, expd.at(1))
            nc.scalar.activation(ex[:, :], ex[:, :], ACT.Exp).then_inc(expd.sem, 1)

        @block.vector
        def _(dve):
            own = Steps(dve, S["dve"])
            link = own.link

            def bc(a):
                return a.unsqueeze(2).broadcast_to([P, a.shape[1], 8])

            rank = C["rank"][:, 0:8].unsqueeze(1).broadcast_to([P, NT, 8])
            first_row = C["first_row"][:, 0:8].unsqueeze(1).broadcast_to([P, 2 * NT, 8])
            link(nc.vector.memset(lg[:, :, :], -3e38))
            dve.wait_ge(have.sem, have.at(1))
            link(nc.vector.tensor_copy(lg[:, :, 0:E], logits[:, :, 0:E]))
            for k, (src, v) in enumerate(((lg, v1), (l2, v2))):
                link(nc.vector.tensor_reduce(v[:, :], src[:, :, :], AX.X, ALU.max))
                link(nc.vector.tensor_tensor(cand[:, :, :], src[:, :, :], bc(v[:, :]), ALU.is_equal))
                link(nc.vector.tensor_tensor(cand[:, :, :], cand[:, :, :], rank, ALU.mult))
                link(nc.vector.tensor_reduce(m1[:, :], cand[:, :, :], AX.X, ALU.max))
                link(nc.vector.tensor_tensor(o[:, k * NT:(k + 1) * NT, :], cand[:, :, :], bc(m1[:, :]), ALU.is_equal))
                if k == 0:
                    link(nc.vector.scalar_tensor_tensor(l2[:, :, :], o[:, 0:NT, :], MASKED, lg[:, :, :], ALU.mult, ALU.add))
            nc.vector.tensor_copy(ob[:, :, :], o[:, :, :]).then_inc(chosen.sem, 1)
            nc.vector.tensor_tensor(ex[:, :], v2[:, :], v1[:, :], ALU.subtract).then_inc(expd.sem, 1)
            dve.wait_ge(counted.sem, counted.at(1))
            link(nc.vector.tensor_copy(run_a[:, :, :], total))
            a, b_ = run_a, run_b
            for sh in (1, 2, 4, 8, 16):
                nc.vector.tensor_copy(b_[:, 0:sh, :], a[:, 0:sh, :])
                link(nc.vector.tensor_tensor(b_[:, sh:, :], a[:, sh:, :], a[:, 0:2 * NT - sh, :], ALU.add))
                a, b_ = b_, a
            link(nc.vector.tensor_tensor(pos[:, :, :], a[:, :, :], total, ALU.subtract))
            link(nc.vector.tensor_tensor(pos[:, :, :], pos[:, :, :], up_to, ALU.add))
            link(nc.vector.scalar_tensor_tensor(run_a[:, :, :], pos[:, :, :], FF0_CAPACITY + 0.5, o[:, :, :], ALU.is_lt, ALU.mult))
            link(nc.vector.tensor_reduce(kept[:, :], run_a[:, :, :], AX.X, ALU.add))
            link(nc.vector.scalar_tensor_tensor(pos[:, :, :], pos[:, :, :], float(FF0_CAPACITY), first_row, ALU.min, ALU.add))
            link(nc.vector.tensor_tensor(pos[:, :, :], pos[:, :, :], o[:, :, :], ALU.mult))
            link(nc.vector.tensor_reduce(place[:, :], pos[:, :, :], AX.X, ALU.add))
            link(nc.vector.tensor_copy(row_out[:, :], place[:, :]))
            link(nc.vector.tensor_scalar(late[:, :], kept[:, :], -1e6, 1e6, ALU.mult, ALU.add))
            link(nc.vector.tensor_tensor(place[:, :], place[:, :], late[:, :], ALU.add))
            link(nc.vector.tensor_copy(row_in[:, :], place[:, :]))
            dve.wait_ge(expd.sem, expd.at(2))
            link(nc.vector.tensor_scalar(v1[:, :], ex[:, :], 1.0, None, ALU.add))
            link(nc.vector.reciprocal(gates[:, 0:NT], v1[:, :]))
            link(nc.vector.tensor_tensor(gates[:, NT:2 * NT], ex[:, :], gates[:, 0:NT], ALU.mult))
            link(nc.vector.tensor_tensor(gates[:, :], gates[:, :], kept[:, :], ALU.mult))
            own.close()

    for s in (have, chosen, counted):
        s.passed(1)
    expd.passed(2)


def capacity_experts(nc, S, X, xn, xnT, Wg, Wu, Wd, gb, row_in, row_out, gates, inbox, outbox, ident, loaded, loaded_at):
    E, FT, CAP = FF0_EXPERTS, FF0_DIM // P, FF0_CAPACITY
    SLOTS = CAP // 3
    assert SLOTS * 3 == CAP
    EARLY = 3
    jobs = [("shared", c) for c in range(EARLY)] + [("expert", e) for e in range(E)] + [("shared", c) for c in range(EARLY, B)]
    width = {"shared": T, "expert": CAP}
    with ExitStack() as ctx:
        room = Room(nc, ctx)
        sg, hid = room.sb("sg", [P, 2, T]), room.sb("hid", [P, 2, FT, T])
        xs, xsT = room.sb("xs", [SLOTS, E, 3, P]), room.sb("xsT", [P, 2, CAP])
        ys, back = room.sb("ys", [SLOTS, 2, 3, P]), room.sb("back", [P, 2 * NT, P])
        pa, pu, po = (room.ps(n, [P, 2, T]) for n in ("pa", "pu", "po"))
        tp = room.ps("tp", [P, T])
        sent, fetched, turned, entered, proj, silu, hidden, down, taken = (
            S["m_" + k] for k in ("sent", "fetched", "turned", "entered", "proj", "silu", "hidden", "down", "taken"))
        stored = S["m_stored0"], S["m_stored1"]
        returned = S["m_returned0"], S["m_returned1"]
        block = ctx.enter_context(nc.Block())

        @block.gpsimd
        def _(pool):
            for k in range(2 * NT):
                nc.gpsimd.indirect_dma_start(inbox, bass.IndirectOffsetOnAxis(ap=row_in[:, k:k + 1], axis=0), xn[:, k % NT, :], None,
                                             bounds_check=E * CAP - 1, oob_is_err=False).then_inc(sent.sem, 16)
            for half in range(2):
                n = sum(1 for j, (kind, _) in enumerate(jobs) if kind == "expert" and j % 2 == half)
                pool.wait_ge(stored[half].sem, stored[half].at(16 * n))
            for k in range(2 * NT):
                nc.gpsimd.indirect_dma_start(back[:, k, :], None, outbox, bass.IndirectOffsetOnAxis(ap=row_out[:, k:k + 1], axis=0),
                                             bounds_check=E * CAP - 1, oob_is_err=False).then_inc(returned[k // NT].sem, 16)

        @block.sync
        def _(sp):
            sp.wait_ge(sent.sem, sent.at(16 * 2 * NT))
            sp.dma_start(xs[:, :, :, :], inbox.rearrange("(e c p) d -> p e c d", p=SLOTS, c=3)).then_inc(fetched.sem, 16)
            for j, (kind, e) in enumerate(jobs):
                if kind == "expert":
                    sp.wait_ge(taken.sem, taken.at(j + 1))
                    sp.dma_start(outbox[e * CAP:(e + 1) * CAP, :].rearrange("(c p) d -> p c d", p=SLOTS), ys[:, j % 2, :, :])\
                      .then_inc(stored[j % 2].sem, 16)

        @block.tensor
        def _(pe):
            pe.wait_ge(loaded, loaded_at)

            def turn(e):
                if e == 0:
                    pe.wait_ge(fetched.sem, fetched.at(16))
                else:
                    pe.wait_ge(entered.sem, entered.at(e))
                for c in range(3):
                    ins = nc.tensor.transpose(tp[:, c * SLOTS:(c + 1) * SLOTS], xs[:, e, c, :], ident[0:SLOTS, 0:SLOTS])
                ins.then_inc(turned.sem, 1)

            def up(j, f):
                kind, i = jobs[j]
                u = j * FT + f
                if u >= 2:
                    pe.wait_ge(hidden.sem, hidden.at(u - 1))
                if kind == "expert" and f == 0:
                    pe.wait_ge(entered.sem, entered.at(i + 1))
                x = xnT[:, i * T:(i + 1) * T] if kind == "shared" else xsT[:, j % 2, :]
                at = ((E if kind == "shared" else i) * FT + f) * P
                nc.tensor.matmul(pa[:, u % 2, 0:width[kind]], Wg[:, at:at + P], x, start=True, stop=True)
                nc.tensor.matmul(pu[:, u % 2, 0:width[kind]], Wu[:, at:at + P], x, start=True, stop=True).then_inc(proj.sem, 1)

            def down_products(j):
                kind, i = jobs[j]
                pe.wait_ge(hidden.sem, hidden.at((j + 1) * FT))
                if j >= 2:
                    pe.wait_ge(taken.sem, taken.at(j - 1))
                tiles, m = (TPB, P) if kind == "shared" else (3, SLOTS)
                at = (E if kind == "shared" else i) * FT
                for c in range(tiles):
                    for f in range(FT):
                        ins = nc.tensor.matmul(po[0:m, j % 2, c * P:(c + 1) * P], hid[:, j % 2, f, c * m:(c + 1) * m], Wd[:, at + f, :],
                                               start=(f == 0), stop=(f == FT - 1))
                ins.then_inc(down.sem, 1)

            for j in range(len(jobs)):
                for f in range(FT):
                    up(j, f)
                    if f == 1 and j >= 1:
                        down_products(j - 1)
                    if f == 2 and j + 1 < len(jobs) and jobs[j + 1][0] == "expert":
                        turn(jobs[j + 1][1])
            down_products(len(jobs) - 1)

        @block.scalar
        def _(act):
            for j, (kind, i) in enumerate(jobs):
                for f in range(FT):
                    u = j * FT + f
                    act.wait_ge(proj.sem, proj.at(u + 1))
                    w = width[kind]
                    nc.scalar.activation(sg[:, u % 2, 0:w], pa[:, u % 2, 0:w], ACT.Silu).then_inc(silu.sem, 1)
                    if f == 2 and j + 1 < len(jobs) and jobs[j + 1][0] == "expert":
                        e = jobs[j + 1][1]
                        act.wait_ge(turned.sem, turned.at(e + 1))
                        nc.scalar.activation(xsT[:, (j + 1) % 2, :], tp[:, 0:CAP], ACT.Identity, bias=gb[:, 1:2],
                                             scale=gb[:, 0:1]).then_inc(entered.sem, 1)

        @block.vector
        def _(dve):
            own = Steps(dve, S["dve"])

            def take(j):
                kind, i = jobs[j]
                dve.wait_ge(down.sem, down.at(j + 1))
                if kind == "shared":
                    xc = X[:, i * TPB:(i + 1) * TPB, :].rearrange("p n d -> p (n d)")
                    nc.vector.tensor_tensor(xc, xc, po[:, j % 2, :], ALU.add).then_inc(taken.sem, 1)
                else:
                    before = sum(1 for q in range(j) if jobs[q][0] == "expert" and q % 2 == j % 2)
                    if before:
                        dve.wait_ge(stored[j % 2].sem, stored[j % 2].at(16 * before))
                    nc.vector.tensor_copy(ys[:, j % 2, :, :].rearrange("p c d -> p (c d)"), po[0:SLOTS, j % 2, 0:3 * P]).then_inc(taken.sem, 1)

            for j, (kind, i) in enumerate(jobs):
                for f in range(FT):
                    u = j * FT + f
                    w = width[kind]
                    if f == 0 and j >= 2:
                        dve.wait_ge(down.sem, down.at(j - 1))
                    dve.wait_ge(silu.sem, silu.at(u + 1))
                    nc.vector.tensor_tensor(hid[:, j % 2, f, 0:w], sg[:, u % 2, 0:w], pu[:, u % 2, 0:w], ALU.mult).then_inc(hidden.sem, 1)
                    if f == 1 and j >= 1:
                        take(j - 1)
            take(len(jobs) - 1)
            dve.wait_ge(taken.sem, taken.at(len(jobs)))
            for s in range(2):
                dve.wait_ge(returned[s].sem, returned[s].at(16 * NT))
                for n in range(NT):
                    k = s * NT + n
                    ins = nc.vector.scalar_tensor_tensor(X[:, n, :], back[:, k, :], gates[:, k:k + 1], X[:, n, :], ALU.mult, ALU.add)
                own.link(ins)
            own.close()

    for s, n in ((sent, 32 * NT), (fetched, 16), (turned, E), (entered, E), (proj, FT * len(jobs)), (silu, FT * len(jobs)),
                 (hidden, FT * len(jobs)), (down, len(jobs)), (taken, len(jobs)), (returned[0], 16 * NT), (returned[1], 16 * NT)):
        s.passed(n)
    for half in range(2):
        stored[half].passed(16 * sum(1 for j, (kind, _) in enumerate(jobs) if kind == "expert" and j % 2 == half))


def group_norm_gate(nc, S, Y, G, groups, width, gain=None, shift=None):
    GC = TPB * groups
    with ExitStack() as ctx:
        room = Room(nc, ctx)
        sq = room.sb("sq", [P, GC, width])
        total, mean, ve = room.sb("total", [P, GC]), room.sb("mean", [P, GC]), room.sb("ve", [P, GC])
        sd, rs = room.sb("sd", [P, GC]), room.sb("rs", [P, GC])
        centred, squared, var_ready, std_ready, gated = (S[k] for k in ("centred", "squared", "var", "std", "gated"))
        block = ctx.enter_context(nc.Block())

        @block.vector
        def _(dve):
            own = Steps(dve, S["dve"])

            def bc(a):
                return a.unsqueeze(2).broadcast_to([P, GC, width])

            for b in range(B):
                y = Y[:, b * TPB:(b + 1) * TPB, :].rearrange("p n (g w) -> p (n g) w", w=width)
                gate = G[:, b * TPB:(b + 1) * TPB, :].rearrange("p n (g w) -> p (n g) w", w=width)
                own.link(nc.vector.tensor_reduce(total[:, :], y, AX.X, ALU.add))
                own.link(nc.vector.tensor_scalar(mean[:, :], total[:, :], -1.0 / width, None, ALU.mult))
                nc.vector.tensor_tensor(y, y, bc(mean[:, :]), ALU.add).then_inc(centred.sem, 1)
                dve.wait_ge(squared.sem, squared.at(b + 1))
                own.link(nc.vector.tensor_reduce(total[:, :], sq[:, :, :], AX.X, ALU.add))
                nc.vector.tensor_scalar(ve[:, :], total[:, :], 1.0 / width, EPS, ALU.mult, ALU.add).then_inc(var_ready.sem, 1)
                dve.wait_ge(std_ready.sem, std_ready.at(b + 1))
                own.link(nc.vector.reciprocal(rs[:, :], sd[:, :]))
                own.link(nc.vector.tensor_tensor(y, y, bc(rs[:, :]), ALU.mult))
                if gain is not None:
                    own.link(nc.vector.tensor_tensor(y, y, gain.unsqueeze(1).broadcast_to([P, GC, width]), ALU.mult))
                    own.link(nc.vector.tensor_tensor(y, y, shift.unsqueeze(1).broadcast_to([P, GC, width]), ALU.add))
                if b == 0:
                    dve.wait_ge(gated.sem, gated.at(B))
                nc.vector.tensor_tensor(y, y, gate, ALU.mult)
            own.close()

        @block.scalar
        def _(act):
            for b in range(B):
                g = G[:, b * TPB:(b + 1) * TPB, :]
                nc.scalar.activation(g, g, ACT.Silu).then_inc(gated.sem, 1)
            for b in range(B):
                y = Y[:, b * TPB:(b + 1) * TPB, :].rearrange("p n (g w) -> p (n g) w", w=width)
                act.wait_ge(centred.sem, centred.at(b + 1))
                nc.scalar.activation(sq[:, :, :], y, ACT.Square).then_inc(squared.sem, 1)
                act.wait_ge(var_ready.sem, var_ready.at(b + 1))
                nc.scalar.activation(sd[:, :], ve[:, :], ACT.Sqrt).then_inc(std_ready.sem, 1)

    for s in (centred, squared, var_ready, std_ready, gated):
        s.passed(B)


def retention_project(nc, S, xnT, W, qT, kT, V, G):
    with ExitStack() as ctx:
        room = Room(nc, ctx)
        t1, t2 = room.sb("t1", [P, T]), room.sb("t2", [P, T])
        qk = room.ps("qk", [P, 4, T])
        vg = room.ps("vg", [P, 2, 2, 256])
        qk_ready, rotated, vg_ready, vg_copied = (S[k] for k in ("qk_ready", "rotated", "vg_ready", "vg_copied"))
        block = ctx.enter_context(nc.Block())

        @block.tensor
        def _(pe):
            for b in range(B):
                x = xnT[:, b * T:(b + 1) * T]
                if b >= 1:
                    pe.wait_ge(rotated.sem, rotated.at(b))
                for i in range(4):
                    ins = nc.tensor.matmul(qk[:, i, :], W["wqk"][:, i, :], x, start=True, stop=True)
                ins.then_inc(qk_ready.sem, 1)
                for t in range(TPB):
                    n = b * TPB + t
                    if n >= 2:
                        pe.wait_ge(vg_copied.sem, vg_copied.at(n - 1))
                    xt = xnT[:, n * P:(n + 1) * P]
                    for i, (w, bias) in enumerate((("wv", "bv"), ("wg", "bg"))):
                        nc.tensor.matmul(vg[:, n % 2, i, :], xt, W[w][:, :], start=True, stop=False)
                        ins = nc.tensor.matmul(vg[:, n % 2, i, :], W["one"][0:1, :], W[bias][0:1, :], start=False, stop=True)
                    ins.then_inc(vg_ready.sem, 1)

        @block.scalar
        def _(act):
            for n in range(NT):
                act.wait_ge(vg_ready.sem, vg_ready.at(n + 1))
                nc.scalar.activation(V[:, n, :], vg[:, n % 2, 0, :], ACT.Copy)
                nc.scalar.activation(G[:, n, :], vg[:, n % 2, 1, :], ACT.Copy).then_inc(vg_copied.sem, 1)

        @block.vector
        def _(dve):
            own = Steps(dve, S["dve"])
            for b in range(B):
                dve.wait_ge(qk_ready.sem, qk_ready.at(b + 1))
                for i, (dst, tab) in enumerate(((qT, "xq"), (kT, "xk"))):
                    nc.vector.scalar_tensor_tensor(t1[:, :], qk[:, 2 * i, :], W["bqk"][:, 2 * i:2 * i + 1],
                                                   W[tab + "_cos"][:, :], ALU.add, ALU.mult)
                    own.link(nc.vector.scalar_tensor_tensor(t2[:, :], qk[:, 2 * i + 1, :], W["bqk"][:, 2 * i + 1:2 * i + 2],
                                                            W[tab + "_sin"][:, :], ALU.add, ALU.mult))
                    own.link(nc.vector.tensor_tensor(dst[:, b, :], t1[:, :], t2[:, :], ALU.add))
                dve.sem_inc(rotated.sem, 1)
            own.close()

    qk_ready.passed(B)
    rotated.passed(B)
    vg_ready.passed(NT)
    vg_copied.passed(NT)


def retention_heads(nc, S, W, qT, kT, V, Y):
    U = R_HEADS * B
    start_of = [0, T, 2 * T - P, 3 * T - 3 * P]
    with ExitStack() as ctx:
        room = Room(nc, ctx)
        qh = room.sb("qh", [P, 2, T])
        decayed = room.sb("decayed", [P, 2, 10 * P])
        sc = room.ps("sc", [P, 4, T])
        ob = room.ps("ob", [P, 2, 512])
        picked, scored, decays, summed, copied = (S[k] for k in ("picked", "scored", "decays", "rsummed", "rcopied"))
        block = ctx.enter_context(nc.Block())

        @block.scalar
        def _(act):
            def pick(h, b, u):
                act.wait_ge(scored.sem, scored.at(TPB * (u - 1)))
                stand_alone(act, S["aside"])
                nc.scalar.activation(qh[:, b % 2, :], qT[:, b, :], ACT.Copy, scale=W["head_rows"][:, h]).then_inc(picked.sem, 1)

            def put(h, b, u):
                act.wait_ge(summed.sem, summed.at(u + 1))
                stand_alone(act, S["aside"])
                dst = Y[:, b * TPB:(b + 1) * TPB, h]
                nc.scalar.activation(dst, ob[:, b % 2, 0:TPB * R_DV].rearrange("p (n c) -> p n c", c=R_DV),
                                     ACT.Copy).then_inc(copied.sem, 1)

            with act.Fori(0, R_HEADS) as h:
                head = bass.ds(h, 1)
                cols = bass.ds(h * R_DV, R_DV)
                for b in range(B):
                    pick(head, b, h * B + b)
                    if b >= 1:
                        put(cols, b - 1, h * B + b - 1)
                put(cols, B - 1, h * B + B - 1)

        @block.tensor
        def _(pe):
            with pe.Fori(0, R_HEADS) as h:
                def scores(b):
                    u = h * B + b
                    pe.wait_ge(picked.sem, picked.at(u + 1))
                    for kj in range(TPB):
                        pe.wait_ge(decays.sem, decays.at((u - 1) * TPB + kj + 1))
                        w = T - kj * P
                        nc.tensor.matmul(sc[:, kj, 0:w], kT[:, b, kj * P:(kj + 1) * P], qh[:, b % 2, kj * P:T],
                                         start=True, stop=True).then_inc(scored.sem, 1)

                def values(b):
                    u = h * B + b
                    pe.wait_ge(decays.sem, decays.at((u + 1) * TPB))
                    pe.wait_ge(copied.sem, copied.at(u - 1))
                    for qi in range(TPB):
                        for kj in range(qi + 1):
                            at = start_of[kj] + (qi - kj) * P
                            ins = nc.tensor.matmul(ob[:, b % 2, qi * R_DV:(qi + 1) * R_DV], decayed[:, b % 2, at:at + P],
                                                   V[:, b * TPB + kj, bass.ds(h * R_DV, R_DV)],
                                                   start=(kj == 0), stop=(kj == qi))
                    ins.then_inc(summed.sem, 1)

                for b in range(B):
                    scores(b)
                    if b >= 1:
                        values(b - 1)
                values(B - 1)

        @block.vector
        def _(dve):
            with dve.Fori(0, R_HEADS) as h:
                for b in range(B):
                    u = h * B + b
                    dve.wait_ge(summed.sem, summed.at(u - 1))
                    for kj in range(TPB):
                        w = T - kj * P
                        dve.wait_ge(scored.sem, scored.at(u * TPB + kj + 1))
                        nc.vector.tensor_tensor(decayed[:, b % 2, start_of[kj]:start_of[kj] + w], sc[:, kj, 0:w],
                                                W["decays"][:, bass.ds(h, 1), 0:w].rearrange("p a c -> p (a c)"),
                                                ALU.mult).then_inc(decays.sem, 1)

    picked.passed(U)
    scored.passed(TPB * U)
    decays.passed(TPB * U)
    summed.passed(U)
    copied.passed(U)


def retention(nc, S, X, C, D, ident):
    with ExitStack() as ctx:
        room = Room(nc, ctx)
        qT, kT = room.sb("qT", [P, B, T]), room.sb("kT", [P, B, T])
        V, G = room.sb("V", [P, NT, 256]), room.sb("G", [P, NT, 256])
        W = {n: room.sb(n, s) for n, s in (
            ("wqk", [P, 4, P]), ("bqk", [P, 4]), ("wv", [P, 256]), ("bv", [1, 256]), ("wg", [P, 256]), ("bg", [1, 256]),
            ("wp", [P, 2, P]), ("bp", [1, P]), ("one", [1, P]), ("decays", [P, R_HEADS, T]), ("head_rows", [P, R_HEADS]),
            ("xq_cos", [P, T]), ("xq_sin", [P, T]), ("xk_cos", [P, T]), ("xk_sin", [P, T]))}
        big, made = S["big"], S["made"]
        with nc.Block() as block:
            @block.sync
            def _(sp):
                for n, key in (("wqk", "re_wqk"), ("bqk", "re_bqk"), ("wv", "re_wv"), ("bv", "re_bv"), ("wg", "re_wg"), ("bg", "re_bg"),
                               ("wp", "re_wp"), ("bp", "re_bp"), ("xq_cos", "xq_cos"), ("xq_sin", "xq_sin"), ("xk_cos", "xk_cos"),
                               ("xk_sin", "xk_sin"), ("head_rows", "head_rows"), ("decays", "decays")):
                    sp.dma_start(W[n][:, :] if len(W[n].shape) == 2 else W[n][:, :, :], D[key]).then_inc(big.sem, 16)

            @block.gpsimd
            def _(pool):
                nc.gpsimd.memset(W["one"][0:1, :], 1.0).then_inc(made.sem, 1)
                pool.wait_ge(made.sem, made.at(1))
        made.passed(1)
        with ExitStack() as inner:
            xnT = Room(nc, inner).sb("xnT", [P, B * T])
            norm_transpose(nc, S, X, xnT, ident)
            with nc.Block() as block:
                @block.sync
                def _(sp):
                    sp.wait_ge(big.sem, big.at(14 * 16))
            big.passed(14 * 16)
            retention_project(nc, S, xnT, W, qT, kT, V, G)
        Y = room.sb("Y", [P, NT, 256])
        retention_heads(nc, S, W, qT, kT, V, Y)
        group_norm_gate(nc, S, Y, G, R_HEADS, R_DV)
        project_add(nc, S, X, Y, W["wp"], ident, 2, W["bp"][0:1, :], W["one"][0:1, :])


def recurrent(nc, S, X, C, D, ident):
    R, K, V_, G_, DEC = range(5)
    XW, U = 5, 6
    with ExitStack() as ctx:
        room = Room(nc, ctx)
        Y, G = room.sb("Y", [P, NT, P]), room.sb("G", [P, NT, P])
        wo, ln = room.sb("wo", [P, 1, P]), room.sb("ln", [P, 2 * W_HD])
        big = S["big"]
        inner = ExitStack()
        iroom = Room(nc, inner)
        xnT = iroom.sb("xnT", [P, B * T])
        la, lb = iroom.sb("la", [P, 5, LORA]), iroom.sb("lb", [LORA, 5, P])
        cols, w = iroom.sb("cols", [P, 7]), iroom.sb("w", [P, 5, P])
        wvj, to_j = iroom.sb("wvj", [P, W_HD, P]), iroom.sb("to_j", [P, W_HD, P])
        same, init = iroom.sb("same", [P, P]), iroom.sb("init", [P, W_HD])
        loads = ((la, "rw_la"), (lb, "rw_lb"), (cols, "rw_cols"), (w, "rw_w"), (wvj, "rw_wvj"), (to_j, "head_to"), (same, "head_sum"),
                 (init, "rw_init"))
        with nc.Block() as block:
            @block.sync
            def _(sp):
                for dst, key in loads:
                    src = D[key]
                    d = dst[:, :] if len(dst.shape) == 2 else dst[:, :, :] if key != "rw_w" else dst[:, 0:5, :]
                    sp.dma_start(d, src).then_inc(big.sem, 16)
                sp.dma_start(wo[:, :, :], D["rw_w"][:, 4:5, :]).then_inc(big.sem, 16)
                sp.dma_start(ln[:, :], D["rw_ln"].broadcast_to([P, 2 * W_HD])).then_inc(big.sem, 16)
        n_loads = len(loads) + 2
        norm_transpose(nc, S, X, xnT, ident)

        dx, lerp = iroom.sb("dx", [P, T]), iroom.sb("lerp", [P, T])
        th, mix, part = iroom.sb("th", [LORA, 2, T]), iroom.sb("mix", [P, 5, T]), iroom.sb("part", [P, T])
        rkv, e1, dec = iroom.sb("rkv", [P, 3, T]), iroom.sb("e1", [P, T]), iroom.sb("dec", [P, T])
        kv, st, pr = iroom.sb("kv", [P, T]), iroom.sb("st", [P, 2, T + 1]), iroom.sb("pr", [P, 2, T])
        bonus, yT = iroom.sb("bonus", [P, T]), iroom.sb("yT", [P, T])
        ph, pl, pv = iroom.ps("ph", [P, 2, T]), iroom.ps("pl", [P, 2, T]), iroom.ps("pv", [P, 2, T])
        py, px = iroom.ps("py", [P, T]), iroom.ps("px", [P, T])
        (lerped, low, tanhed, high, mixed, px_full, px_free, decayed, v_full, v_used, weighted, summed, bonused, y_done) = (
            S["w_" + k] for k in ("lerped", "low", "tanhed", "high", "mixed", "px_full", "px_free", "decayed", "v_full",
                                  "v_used", "weighted", "summed", "bonused", "y_done"))
        PX = 6
        with nc.Block() as block:
            @block.tensor
            def _(pe):
                pe.wait_ge(big.sem, big.at(16 * n_loads))
                with pe.Fori(0, B) as b:
                    def low_rank(p, src, n):
                        nc.tensor.matmul(ph[0:LORA, n % 2, :], la[:, p, :], src, start=True, stop=True).then_inc(low.sem, 1)

                    def back(p, n):
                        pe.wait_ge(tanhed.sem, tanhed.at(b * 6 + n + 1))
                        if n >= 2:
                            pe.wait_ge(mixed.sem, mixed.at(b * 5 + n - 1))
                        nc.tensor.matmul(pl[:, n % 2, :], lb[:, p, :], th[:, n % 2, :], start=True, stop=True).then_inc(high.sem, 1)

                    def project(n, weight, src):
                        pe.wait_ge(px_free.sem, px_free.at(b * PX + n))
                        nc.tensor.matmul(px[:, :], weight, src, start=True, stop=True).then_inc(px_full.sem, 1)

                    pe.wait_ge(lerped.sem, lerped.at(b + 1))
                    low_rank(0, lerp[:, :], 0)
                    low_rank(1, lerp[:, :], 1)
                    for p in range(5):
                        back(p, p)
                        if p + 2 < 5:
                            low_rank(p + 2, lerp[:, :], p + 2)
                        if p >= 1 and p - 1 < 3:
                            pe.wait_ge(mixed.sem, mixed.at(b * 5 + p))
                            project(p - 1, w[:, p - 1, :], mix[:, p - 1, :])
                    pe.wait_ge(mixed.sem, mixed.at(b * 5 + 5))
                    low_rank(DEC, mix[:, DEC, :], 5)
                    back(DEC, 5)
                    pe.wait_ge(px_free.sem, px_free.at(b * PX + 3))
                    for t in range(TPB):
                        ins = nc.tensor.matmul(px[:, t * P:(t + 1) * P], mix[:, G_, t * P:(t + 1) * P], w[:, 3, :], start=True, stop=True)
                    ins.then_inc(px_full.sem, 1)

                    def sum_rows(j):
                        pe.wait_ge(weighted.sem, weighted.at(b * W_HD + j + 1))
                        nc.tensor.matmul(py[:, :], to_j[:, j, :], pr[:, j % 2, :], start=(j == 0), stop=(j == W_HD - 1)).then_inc(summed.sem, 1)

                    for j in range(W_HD):
                        pe.wait_ge(v_used.sem, v_used.at(b * W_HD + j - 1))
                        nc.tensor.matmul(pv[:, j % 2, :], wvj[:, j, :], mix[:, V_, :], start=True, stop=True).then_inc(v_full.sem, 1)
                        if j >= 1:
                            sum_rows(j - 1)
                    sum_rows(W_HD - 1)
                    pe.wait_ge(bonused.sem, bonused.at(b + 1))
                    project(4, same[:, :], bonus[:, :])
                    pe.wait_ge(y_done.sem, y_done.at(b + 1))
                    pe.wait_ge(px_free.sem, px_free.at(b * PX + 5))
                    for t in range(TPB):
                        ins = nc.tensor.transpose(px[:, t * P:(t + 1) * P], yT[:, t * P:(t + 1) * P], ident[:, :])
                    ins.then_inc(px_full.sem, 1)

            @block.scalar
            def _(act):
                act.wait_ge(big.sem, big.at(16 * n_loads))
                nc.scalar.preload_act_table(ACT.Exp)
                with act.Fori(0, B) as b:
                    def tanh(n):
                        act.wait_ge(low.sem, low.at(b * 6 + n + 1))
                        nc.scalar.activation(th[:, n % 2, :], ph[0:LORA, n % 2, :], ACT.Tanh).then_inc(tanhed.sem, 1)

                    def copy_px(n, dst):
                        act.wait_ge(px_full.sem, px_full.at(b * PX + n + 1))
                        if n in (3, 5):
                            stand_alone(act, S["aside"])
                        nc.scalar.activation(dst, px[:, :], ACT.Copy).then_inc(px_free.sem, 1)

                    tanh(0)
                    tanh(1)
                    tanh(2)
                    copy_px(0, rkv[:, 0, :])
                    tanh(3)
                    copy_px(1, rkv[:, 1, :])
                    tanh(4)
                    copy_px(2, rkv[:, 2, :])
                    tanh(5)
                    act.wait_ge(high.sem, high.at(b * 6 + 6))
                    nc.scalar.activation(e1[:, :], pl[:, 1, :], ACT.Exp, bias=cols[:, DEC:DEC + 1]).then_inc(S["w_e1"].sem, 1)
                    act.wait_ge(S["w_e1"].sem, S["w_e1"].at(b + 1))
                    nc.scalar.activation(dec[:, :], e1[:, :], ACT.Exp, scale=-1.0).then_inc(decayed.sem, 1)
                    copy_px(3, G[:, bass.ds(b * TPB, TPB), :].rearrange("p n d -> p (n d)"))
                    copy_px(5, Y[:, bass.ds(b * TPB, TPB), :].rearrange("p n d -> p (n d)"))

            @block.vector
            def _(dve):
                own = Steps(dve, S["dve"])
                dve.wait_ge(big.sem, big.at(16 * n_loads))
                with dve.Fori(0, B) as b:
                    x = xnT[:, bass.ds(b * T, T)]
                    own.enter(b, 2 + 5 + 2 * W_HD + 1 + 1)
                    nc.vector.tensor_tensor(dx[:, 1:T], xnT[:, bass.ds(b * T, T - 1)], xnT[:, bass.ds(b * T + 1, T - 1)], ALU.subtract)
                    own.link(nc.vector.tensor_scalar(dx[:, 0:1], xnT[:, bass.ds(b * T, 1)], -1.0, None, ALU.mult))
                    own.link(nc.vector.scalar_tensor_tensor(lerp[:, :], dx[:, :], cols[:, XW:XW + 1], x, ALU.mult, ALU.add))
                    dve.sem_inc(lerped.sem, 1)
                    for p in range(5):
                        dve.wait_ge(high.sem, high.at(b * 6 + p + 1))
                        own.link(nc.vector.scalar_tensor_tensor(part[:, :], pl[:, p % 2, :], cols[:, p:p + 1], dx[:, :], ALU.add, ALU.mult))
                        nc.vector.tensor_tensor(mix[:, p, :], part[:, :], x, ALU.add).then_inc(mixed.sem, 1)
                        dve.wait_ge(mixed.sem, mixed.at(b * 5 + p + 1))
                    dve.wait_ge(px_free.sem, px_free.at(b * PX + 3))
                    nc.vector.scalar_tensor_tensor(bonus[:, :], rkv[:, R, :], cols[:, U:U + 1], rkv[:, K, :], ALU.mult, ALU.mult).then_inc(bonused.sem, 1)
                    dve.wait_ge(decayed.sem, decayed.at(b + 1))
                    for j in range(W_HD):
                        dve.wait_ge(v_full.sem, v_full.at(b * W_HD + j + 1))
                        nc.vector.tensor_copy(st[:, j % 2, 0:1], init[:, j:j + 1])
                        own.link(nc.vector.tensor_tensor(kv[:, :], rkv[:, K, :], pv[:, j % 2, :], ALU.mult))
                        dve.sem_inc(v_used.sem, 1)
                        own.link(nc.vector.tensor_tensor_scan(st[:, j % 2, 1:T + 1], dec[:, :], kv[:, :], init[:, j:j + 1], ALU.mult, ALU.add))
                        dve.wait_ge(summed.sem, summed.at(b * W_HD + j - 1))
                        nc.vector.tensor_tensor(pr[:, j % 2, :], st[:, j % 2, 0:T], rkv[:, R, :], ALU.mult).then_inc(weighted.sem, 1)
                    dve.wait_ge(px_full.sem, px_full.at(b * PX + 5))
                    own.link(nc.vector.tensor_tensor(part[:, :], px[:, :], rkv[:, 2, :], ALU.mult))
                    dve.sem_inc(px_free.sem, 1)
                    dve.wait_ge(summed.sem, summed.at((b + 1) * W_HD))
                    own.link(nc.vector.tensor_tensor(yT[:, :], py[:, :], part[:, :], ALU.add))
                    dve.sem_inc(y_done.sem, 1)
                own.leave(B)
                own.close()
        for s, n in ((lerped, 1), (low, 6), (tanhed, 6), (high, 6), (mixed, 5), (px_full, PX), (px_free, PX), (decayed, 1),
                     (v_full, W_HD), (v_used, W_HD), (weighted, W_HD), (summed, W_HD), (bonused, 1), (y_done, 1), (S["w_e1"], 1)):
            s.passed(B * n)
        big.passed(16 * n_loads)
        inner.close()
        group_norm_gate(nc, S, Y, G, W_HEADS, W_HD, ln[:, 0:W_HD], ln[:, W_HD:2 * W_HD])
        project_add(nc, S, X, Y, wo, ident, 1)


def rotate(own, nc, dst, plain, partner, cos, sin, t1, t2):
    nc.vector.tensor_tensor(t1, plain, cos, ALU.mult)
    own.link(nc.vector.tensor_tensor(t2, partner, sin, ALU.mult))
    own.link(nc.vector.tensor_tensor(dst, t1, t2, ALU.add))


def mqa_keys(nc, S, xnT, wk, wv, tables, kT, V):
    with ExitStack() as ctx:
        room = Room(nc, ctx)
        t1, t2 = room.sb("t1", [P, T]), room.sb("t2", [P, T])
        kp = room.ps("kp", [P, 2, T])
        vp = room.ps("vp", [P, NT, M_HD])
        qk_ready, rotated, vg_ready = S["qk_ready"], S["rotated"], S["vg_ready"]
        block = ctx.enter_context(nc.Block())

        @block.tensor
        def _(pe):
            for n in range(NT):
                ins = nc.tensor.matmul(vp[:, n, :], xnT[:, n * P:(n + 1) * P], wv[:, :], start=True, stop=True)
            ins.then_inc(vg_ready.sem, 1)
            for b in range(B):
                if b >= 1:
                    pe.wait_ge(rotated.sem, rotated.at(b))
                for i in range(2):
                    ins = nc.tensor.matmul(kp[:, i, :], wk[:, i, :], xnT[:, b * T:(b + 1) * T], start=True, stop=True)
                ins.then_inc(qk_ready.sem, 1)

        @block.scalar
        def _(act):
            act.wait_ge(vg_ready.sem, vg_ready.at(1))
            for h in range(2):
                nc.scalar.activation(V[:, h * 8:(h + 1) * 8, :], vp[:, h * 8:(h + 1) * 8, :], ACT.Copy)

        @block.vector
        def _(dve):
            own = Steps(dve, S["dve"])
            for b in range(B):
                dve.wait_ge(qk_ready.sem, qk_ready.at(b + 1))
                rotate(own, nc, kT[:, b, :], kp[:, 0, :], kp[:, 1, :], tables["k_cos"][:, :], tables["k_sin"][:, :], t1[:, :], t2[:, :])
                dve.sem_inc(rotated.sem, 1)
            own.close()

    qk_ready.passed(B)
    rotated.passed(B)
    vg_ready.passed(1)


def mqa_heads(nc, S, xnT, wq_dram, tables, kT, V, YT, C, ident):
    PAIRS, U = M_HEADS // 2, 2 * B * TPB
    UB = 2 * TPB
    with ExitStack() as ctx:
        room = Room(nc, ctx)
        wq = room.sb("wq", [P, 2, P])
        qT = room.sb("qT", [P, 2, T])
        t1, t2 = room.sb("t1", [P, T]), room.sb("t2", [P, T])
        prob, probT = room.sb("prob", [P, 3, T]), room.sb("probT", [P, 2, T])
        nmax, rsum, inv = room.sb("nmax", [P, 4]), room.sb("rsum", [P, 4]), room.sb("inv", [P, 4])
        sc = room.ps("sc", [P, 3, T])
        tp, ob = room.ps("tp", [P, 2, T]), room.ps("ob", [P, 2, T])
        qp = room.ps("qp", [P, T])
        weights, projected, rotated, scored, maxed, expd, scaled, turned, copied, valued, stored = (
            S["a_" + k] for k in ("weights", "projected", "rotated", "scored", "maxed", "expd", "scaled", "turned", "copied", "valued", "normed"))
        half_rotated = S["a_half"]
        block = ctx.enter_context(nc.Block())

        def sync_turn(sp, hp):
            sp.wait_ge(projected.sem, projected.at(hp * 2 * B))
            stand_alone(sp, S["aside"])
            sp.dma_start(wq[:, :, :], wq_dram[bass.ds(hp, 1), :, :, :].rearrange("a p i n -> (a p) i n")).then_inc(weights.sem, 16)

        @block.sync
        def _(sp):
            with sp.Fori(0, PAIRS) as hp:
                sync_turn(sp, hp)

        def before(u, hp, back):
            return (hp, u - back) if u >= back else (hp - 1, U + u - back)

        @block.tensor
        def _(pe):
            def project(hp, b, i):
                if i == 0:
                    if b == 0:
                        pe.wait_ge(weights.sem, weights.at(16 * hp + 16))
                    pe.wait_ge(rotated.sem, rotated.at(hp * B + b))
                else:
                    pe.wait_ge(half_rotated.sem, half_rotated.at(hp * B + b + 1))
                nc.tensor.matmul(qp[:, :], wq[:, i, :], xnT[:, b * T:(b + 1) * T], start=True, stop=True).then_inc(projected.sem, 1)

            def scores(hp, u):
                j, qi = divmod(u, TPB)
                b, h = divmod(j, 2)
                if u % UB == 0:
                    pe.wait_ge(rotated.sem, rotated.at(hp * B + b + 1))
                pe.wait_ge(expd.sem, expd.at(hp * U + u - (1 if u < 2 else 2)))
                rows = slice(h * M_HD, (h + 1) * M_HD)
                s = sc[:, u % 3, 0:(qi + 1) * P]
                nc.tensor.matmul(s, qT[rows, b % 2, qi * P:(qi + 1) * P], kT[rows, b, 0:(qi + 1) * P], start=True, stop=False)
                nc.tensor.matmul(s[:, qi * P:(qi + 1) * P], C["identb"][:, :], C["above"][:, :], start=False, stop=True).then_inc(scored.sem, 1)

            def transposes(hp, u):
                pe.wait_ge(scaled.sem, scaled.at(hp * U + u + 1))
                pe.wait_ge(copied.sem, copied.at(hp * U + u - 1))
                for kj in range(u % TPB + 1):
                    ins = nc.tensor.transpose(tp[:, u % 2, kj * P:(kj + 1) * P], prob[:, u % 3, kj * P:(kj + 1) * P], ident[:, :])
                ins.then_inc(turned.sem, 1)

            def values(hp, u):
                j, qi = divmod(u, TPB)
                b, h = divmod(j, 2)
                if u % UB == 0:
                    pe.wait_ge(stored.sem, stored.at(hp * B + b - 1))
                pe.wait_ge(copied.sem, copied.at(hp * U + u + 1))
                for kj in range(qi + 1):
                    ins = nc.tensor.matmul(ob[h * M_HD:(h + 1) * M_HD, b % 2, qi * P:(qi + 1) * P], V[:, b * TPB + kj, :],
                                           probT[:, u % 2, kj * P:(kj + 1) * P], start=(kj == 0), stop=(kj == qi))
                ins.then_inc(valued.sem, 1)

            def turn(hp, first=False, last=False):
                for u in range(U + 3 if last else U):
                    if u < U:
                        scores(hp, u)
                        b = (u // UB + 1) % B
                        if u % UB in (1, 5) and not (last and b == 0):
                            project(hp if b else hp + 1, b, (u % UB) // 4)
                    if u >= 3 or not first:
                        values(*before(u, hp, 3))
                    if (u >= 2 or not first) and u - 2 < U:
                        transposes(*before(u, hp, 2))

            project(0, 0, 0)
            project(0, 0, 1)
            turn(0, first=True)
            with pe.Fori(1, PAIRS - 1) as hp:
                turn(hp)
            turn(PAIRS - 1, last=True)

        @block.scalar
        def _(act):
            def exponentials(hp, u):
                act.wait_ge(turned.sem, turned.at(hp * U + u - (1 if u < 2 else 2)))
                act.wait_ge(maxed.sem, maxed.at(hp * U + u + 1))
                w = (u % TPB + 1) * P
                nc.scalar.activation(prob[:, u % 3, 0:w], sc[:, u % 3, 0:w], ACT.Exp, bias=nmax[:, u % 4:u % 4 + 1],
                                     accum_out=rsum[:, u % 4:u % 4 + 1]).then_inc(expd.sem, 1)

            def store(hp, b):
                act.wait_ge(valued.sem, valued.at(hp * U + (b + 1) * UB))
                stand_alone(act, S["aside"])
                nc.scalar.activation(YT[:, bass.ds(hp, 1), b * T:(b + 1) * T].rearrange("p a t -> p (a t)"), ob[:, b % 2, :],
                                     ACT.Copy).then_inc(stored.sem, 1)

            def copy(hp, u):
                w = (u % TPB + 1) * P
                act.wait_ge(valued.sem, valued.at(hp * U + u - 1))
                act.wait_ge(turned.sem, turned.at(hp * U + u + 1))
                nc.scalar.activation(probT[:, u % 2, 0:w], tp[:, u % 2, 0:w], ACT.Copy).then_inc(copied.sem, 1)

            def turn(hp, first=False, last=False):
                for u in range(U + 3 if last else U):
                    if u < U:
                        exponentials(hp, u)
                    if u >= 3 or not first:
                        turn_, v = before(u, hp, 3)
                        if v % UB == UB - 1:
                            store(turn_, v // UB)
                    if (u >= 2 or not first) and u - 2 < U:
                        copy(*before(u, hp, 2))

            nc.scalar.preload_act_table(ACT.Exp)
            turn(0, first=True)
            with act.Fori(1, PAIRS - 1) as hp:
                turn(hp)
            turn(PAIRS - 1, last=True)

        @block.vector
        def _(dve):
            own = Steps(dve, S["dve"])

            def rotate_plain(hp, b):
                dve.wait_ge(projected.sem, projected.at((hp * B + b) * 2 + 1))
                own.link(nc.vector.tensor_tensor(t1[:, :], qp[:, :], tables["cos"][:, :], ALU.mult))
                dve.sem_inc(half_rotated.sem, 1)

            def rotate_partner(hp, b):
                dve.wait_ge(projected.sem, projected.at((hp * B + b) * 2 + 2))
                if not (isinstance(hp, int) and hp == 0 and b < 2):
                    dve.wait_ge(scored.sem, scored.at(hp * U + UB * (b - 1)) if b else scored.at((hp - 1) * U + UB * (B - 1)))
                own.link(nc.vector.tensor_tensor(t2[:, :], qp[:, :], tables["sin"][:, :], ALU.mult))
                nc.vector.tensor_tensor(qT[:, b % 2, :], t1[:, :], t2[:, :], ALU.add).then_inc(rotated.sem, 1)
                dve.wait_ge(rotated.sem, rotated.at(hp * B + b + 1))

            def largest(hp, u):
                w = (u % TPB + 1) * P
                dve.wait_ge(scored.sem, scored.at(hp * U + u + 1))
                nc.vector.tensor_reduce(nmax[:, u % 4:u % 4 + 1], sc[:, u % 3, 0:w], AX.X, ALU.max, negate=True).then_inc(maxed.sem, 1)

            def scale(hp, u):
                w = (u % TPB + 1) * P
                dve.wait_ge(expd.sem, expd.at(hp * U + u + 1))
                own.link(nc.vector.reciprocal(inv[:, u % 4:u % 4 + 1], rsum[:, u % 4:u % 4 + 1]))
                p = prob[:, u % 3, 0:w]
                nc.vector.tensor_scalar(p, p, inv[:, u % 4:u % 4 + 1], None, ALU.mult).then_inc(scaled.sem, 1)

            def turn(hp, first=False, last=False):
                for u in range(U + 1 if last else U):
                    if u < U:
                        largest(hp, u)
                        b = (u // UB + 1) % B
                        if not (last and b == 0):
                            if u % UB == 2:
                                rotate_plain(hp if b else hp + 1, b)
                            if u % UB == 6:
                                rotate_partner(hp if b else hp + 1, b)
                    if u >= 1 or not first:
                        scale(*before(u, hp, 1))

            rotate_plain(0, 0)
            rotate_partner(0, 0)
            turn(0, first=True)
            with dve.Fori(1, PAIRS - 1) as hp:
                own.enter(hp - 1, 2 * B + U)
                turn(hp)
            own.leave(PAIRS - 2)
            turn(PAIRS - 1, last=True)
            own.close()

    for s, n in ((weights, 16), (projected, 2 * B), (rotated, B), (half_rotated, B), (scored, U), (maxed, U), (expd, U), (scaled, U),
                 (turned, U), (copied, U), (valued, U), (stored, B)):
        s.passed(PAIRS * n)


def project_turned(nc, S, X, YT, W, KT):
    with ExitStack() as ctx:
        room = Room(nc, ctx)
        op = room.ps("op", [P, B, T])
        ready = S["pready"]
        block = ctx.enter_context(nc.Block())

        @block.tensor
        def _(pe):
            for n in range(NT):
                b, t = divmod(n, TPB)
                for k in range(KT):
                    ins = nc.tensor.matmul(op[:, b, t * P:(t + 1) * P], YT[:, k, n * P:(n + 1) * P], W[:, k, :],
                                           start=(k == 0), stop=(k == KT - 1))
                if t == TPB - 1:
                    ins.then_inc(ready.sem, 1)

        @block.vector
        def _(dve):
            for b in range(B):
                dve.wait_ge(ready.sem, ready.at(b + 1))
                xb = X[:, b * TPB:(b + 1) * TPB, :].rearrange("p n d -> p (n d)")
                nc.vector.tensor_tensor(xb, xb, op[:, b, :], ALU.add)

    ready.passed(B)


def attention_mqa(nc, S, X, C, D, ident):
    KT = M_HEADS * M_HD // P
    with ExitStack() as ctx:
        room = Room(nc, ctx)
        YT = room.sb("YT", [P, KT, B * T])
        wo = room.sb("wo", [P, KT, P])
        big = S["big"]
        with ExitStack() as inner:
            iroom = Room(nc, inner)
            xnT, kT, V = iroom.sb("xnT", [P, B * T]), iroom.sb("kT", [P, B, T]), iroom.sb("V", [P, NT, M_HD])
            wk, wv = iroom.sb("wk", [P, 2, P]), iroom.sb("wv", [P, M_HD])
            tables = {n: iroom.sb(n, [P, T]) for n in ("cos", "sin", "k_cos", "k_sin")}
            with nc.Block() as block:
                @block.sync
                def _(sp):
                    sp.dma_start(wk[:, :, :], D["mq_wk"]).then_inc(big.sem, 16)
                    sp.dma_start(wv[:, :], D["mq_wv"]).then_inc(big.sem, 16)
                    for n in tables:
                        sp.dma_start(tables[n][:, :], D["rope_" + n]).then_inc(big.sem, 16)
                    sp.dma_start(wo[:, :, :], D["mq_wo"]).then_inc(big.sem, 16)
            norm_transpose(nc, S, X, xnT, ident)
            with nc.Block() as block:
                @block.sync
                def _(sp):
                    sp.wait_ge(big.sem, big.at(7 * 16))
            big.passed(7 * 16)
            mqa_keys(nc, S, xnT, wk, wv, tables, kT, V)
            mqa_heads(nc, S, xnT, D["mq_wq"], tables, kT, V, YT, C, ident)
        project_turned(nc, S, X, YT, wo, KT)


CUTS = ((0, 0), (0, 1), (1, 0), (0, 2), (2, 0), (1, 1))


def decay_project(nc, S, xnT, w, drow, log_dist, V1, weight, parts_q, parts_k):
    with ExitStack() as ctx:
        room = Room(nc, ctx)
        dt, sp_ = room.sb("dt", [P, A_HEADS]), room.sb("softplus", [P, A_HEADS])
        qk, rest = room.sb("qk", [P, 2, 2, T]), room.sb("rest", [P, 2, T])
        cut = room.sb("cut", [P, 2, 2, 3, T], BF16)
        qp = room.ps("qp", [P, 2, 2, T])
        vp = room.ps("vp", [P, 2, T])
        (qk_ready, qk_copied, cut_ready, vg_ready, vg_copied, expd) = (
            S[k] for k in ("qk_ready", "qk_copied", "cut_ready", "vg_ready", "vg_copied", "expd"))
        weighed = S["weighed"]
        cut_stored = S["cut_stored0"], S["cut_stored1"]
        block = ctx.enter_context(nc.Block())

        @block.tensor
        def _(pe):
            for b in range(B):
                if b >= 2:
                    pe.wait_ge(qk_copied.sem, qk_copied.at(b - 1))
                    pe.wait_ge(vg_copied.sem, vg_copied.at(b - 1))
                for i in range(2):
                    ins = nc.tensor.matmul(qp[:, b % 2, i, :], w[:, i * P:(i + 1) * P], xnT[:, b * T:(b + 1) * T], start=True, stop=True)
                ins.then_inc(qk_ready.sem, 1)
                for t in range(TPB):
                    n = b * TPB + t
                    ins = nc.tensor.matmul(vp[:, b % 2, t * P:(t + 1) * P], xnT[:, n * P:(n + 1) * P], w[:, 2 * P:3 * P], start=True, stop=True)
                ins.then_inc(vg_ready.sem, 1)

        @block.scalar
        def _(act):
            act.wait_ge(expd.sem, expd.at(1))
            nc.scalar.activation(dt[:, :], dt[:, :], ACT.Exp, scale=-1.0).then_inc(expd.sem, 1)
            act.wait_ge(expd.sem, expd.at(2))
            nc.scalar.activation(dt[:, :], dt[:, :], ACT.Ln, bias=1.0).then_inc(expd.sem, 1)
            act.wait_ge(expd.sem, expd.at(4))
            for h in range(A_HEADS):
                nc.scalar.activation(weight[:, h, :], log_dist[:, :], ACT.Ln, scale=sp_[:, h:h + 1], bias=1.0).then_inc(weighed.sem, 1)
            for b in range(B):
                act.wait_ge(qk_ready.sem, qk_ready.at(b + 1))
                if b >= 2:
                    act.wait_ge(cut_ready.sem, cut_ready.at(b - 1))
                nc.scalar.activation(qk[:, b % 2, 0, :], qp[:, b % 2, 0, :], ACT.Copy, scale=float(A_HD) ** -0.5)
                nc.scalar.activation(qk[:, b % 2, 1, :], qp[:, b % 2, 1, :], ACT.Copy).then_inc(qk_copied.sem, 1)
                act.wait_ge(vg_ready.sem, vg_ready.at(b + 1))
                nc.scalar.activation(V1[:, b * TPB:(b + 1) * TPB, :, 0:A_HD],
                                     vp[:, b % 2, :].rearrange("p (n h c) -> p n h c", h=A_HEADS, c=A_HD), ACT.Copy).then_inc(vg_copied.sem, 1)
            act.wait_ge(weighed.sem, weighed.at(A_HEADS))
            for h in range(A_HEADS // 4):
                w4 = weight[:, 4 * h:4 * h + 4, :]
                nc.scalar.activation(w4, w4, ACT.Exp, scale=-1.0)

        @block.vector
        def _(dve):
            own = Steps(dve, S["dve"])
            own.link(nc.vector.tensor_scalar(dt[:, :], drow[:, :], -1.0, None, ALU.mult))
            nc.vector.tensor_tensor(dt[:, :], dt[:, :], drow[:, :], ALU.max).then_inc(expd.sem, 1)
            own.link(nc.vector.tensor_scalar(sp_[:, :], drow[:, :], 0.0, None, ALU.max))
            dve.wait_ge(expd.sem, expd.at(3))
            nc.vector.tensor_tensor(sp_[:, :], sp_[:, :], dt[:, :], ALU.add).then_inc(expd.sem, 1)
            for b in range(B):
                dve.wait_ge(qk_copied.sem, qk_copied.at(b + 1))
                if b >= 2:
                    dve.wait_ge(cut_stored[b % 2].sem, cut_stored[b % 2].at(6 * 16 * (b // 2)))
                c = cut[:, b % 2, :, :, :]
                split3(own, nc, qk[:, b % 2, :, :], rest[:, :, :], c[:, :, 0, :], c[:, :, 1, :], c[:, :, 2, :]).then_inc(cut_ready.sem, 1)
                dve.wait_ge(cut_ready.sem, cut_ready.at(b + 1))
            own.close()

        @block.gpsimd
        def _(pool):
            nc.gpsimd.memset(V1[:, :, :, A_HD:A_HD + 1], 1.0)

        @block.sync
        def _(sp):
            for b in range(B):
                sp.wait_ge(cut_ready.sem, cut_ready.at(b + 1))
                for i, dram in enumerate((parts_q, parts_k)):
                    for part in range(3):
                        sp.dma_start(dram[part, :, b, :], cut[:, b % 2, i, part, :]).then_inc(cut_stored[b % 2].sem, 16)
            for half in cut_stored:
                sp.wait_ge(half.sem, half.at(6 * 16 * (B // 2)))

    for s in (qk_ready, qk_copied, cut_ready, vg_ready, vg_copied):
        s.passed(B)
    for half in cut_stored:
        half.passed(6 * 16 * (B // 2))
    expd.passed(4)
    weighed.passed(A_HEADS)


def decay_heads(nc, S, parts_q, parts_k, V1, weight, Y, C, ident):
    U = A_HEADS * TPB
    with ExitStack() as ctx:
        room = Room(nc, ctx)
        KC = len(CUTS) * A_HD
        qs, ks = (room.sb(n, [KC, 2, A_HEADS, T], BF16) for n in ("qs", "ks"))
        prob, probT = room.sb("prob", [P, TPB, T]), room.sb("probT", [P, 2, T])
        nmax, inv = room.sb("nmax", [P, TPB]), room.sb("inv", [P, TPB, A_HEADS])
        sc, tp = room.ps("sc", [P, 2, T]), room.ps("tp", [P, 2, T])
        ob = room.ps("ob", [P, 2, TPB, A_HEADS, 16])
        loaded = S["loaded0"], S["loaded1"]
        scored, maxed, expd, turned, copied, valued, normed = (
            S["a_" + k] for k in ("scored", "maxed", "expd", "turned", "copied", "valued", "normed"))
        PER_LOAD = 2 * len(CUTS) * 16
        block = ctx.enter_context(nc.Block())

        @block.sync
        def _(sp):
            for b in range(B):
                if b >= 2:
                    sp.wait_ge(scored.sem, scored.at(U * (b - 1)))
                for c, (pq, pk) in enumerate(CUTS):
                    for dst, dram, part in ((qs, parts_q, pq), (ks, parts_k, pk)):
                        sp.dma_start(dst[c * A_HD:(c + 1) * A_HD, b % 2, :, :],
                                     dram[part, :, b, :].rearrange("(h d) t -> d h t", d=A_HD)).then_inc(loaded[b % 2].sem, 16)

        @block.tensor
        def _(pe):
            def scores(half, b, h, qi):
                u = b * U + h * TPB + qi
                pe.wait_ge(expd.sem, expd.at(u - 1))
                head = bass.ds(h, 1)
                s = sc[:, qi % 2, 0:(qi + 1) * P]
                nc.tensor.matmul(s, qs[:, half, head, qi * P:(qi + 1) * P].rearrange("p a t -> p (a t)"),
                                 ks[:, half, head, 0:(qi + 1) * P].rearrange("p a t -> p (a t)"), start=True, stop=False)
                nc.tensor.matmul(s[:, qi * P:(qi + 1) * P], C["identb"][:, :], C["above"][:, :], start=False, stop=True).then_inc(scored.sem, 1)

            def transposes(half, b, h, qi):
                u = b * U + h * TPB + qi
                pe.wait_ge(expd.sem, expd.at(u + 1))
                pe.wait_ge(copied.sem, copied.at(u - 1))
                for kj in range(qi + 1):
                    at = (qi - kj) * P
                    ins = nc.tensor.transpose(tp[:, qi % 2, at:at + P], prob[:, qi, kj * P:(kj + 1) * P], ident[:, :])
                ins.then_inc(turned.sem, 1)

            def values(half, b, h, qi):
                u = b * U + h * TPB + qi
                pe.wait_ge(copied.sem, copied.at(u + 1))
                for kj in range(qi + 1):
                    at = (qi - kj) * P
                    ins = nc.tensor.matmul(ob[:, half, qi, bass.ds(h, 1), 0:A_HD + 1].rearrange("p a c -> p (a c)"),
                                           probT[:, qi % 2, at:at + P],
                                           V1[:, bass.ds(b * TPB + kj, 1), bass.ds(h, 1), :].rearrange("p a e c -> p (a e c)"),
                                           start=(kj == 0), stop=(kj == qi))
                ins.then_inc(valued.sem, 1)

            def head(half, b, h, ahead=True, behind=True, last=True):
                for qi in range(TPB):
                    if ahead:
                        scores(half, b, h, qi)
                    if behind:
                        transposes(half, b, h - 1, qi)
                    if qi == 0 and last:
                        values(half, b, h - 2, TPB - 1)
                    if qi >= 1 and behind:
                        values(half, b, h - 1, qi - 1)

            with pe.Fori(0, B // 2) as pair:
                for half in range(2):
                    b = pair * 2 + half
                    pe.wait_ge(loaded[half].sem, loaded[half].at(PER_LOAD * (pair + 1)))
                    pe.wait_ge(normed.sem, normed.at(b - 1))
                    head(half, b, 0, behind=False, last=False)
                    head(half, b, 1, last=False)
                    with pe.Fori(2, A_HEADS) as h:
                        head(half, b, h)
                    head(half, b, A_HEADS, ahead=False)
                    values(half, b, A_HEADS - 1, TPB - 1)

        @block.scalar
        def _(act):
            nc.scalar.preload_act_table(ACT.Exp)
            with act.Fori(0, B * A_HEADS) as g:
                for qi in range(TPB):
                    u = g * TPB + qi
                    act.wait_ge(turned.sem, turned.at(u - 3))
                    act.wait_ge(maxed.sem, maxed.at(u + 1))
                    w = (qi + 1) * P
                    nc.scalar.activation(prob[:, qi, 0:w], sc[:, qi % 2, 0:w], ACT.Exp, bias=nmax[:, qi:qi + 1]).then_inc(expd.sem, 1)

        @block.vector
        def _(dve):
            own = Steps(dve, S["dve"])

            def largest(b, h, qi):
                u = b * U + h * TPB + qi
                dve.wait_ge(scored.sem, scored.at(u + 1))
                nc.vector.tensor_reduce(nmax[:, qi:qi + 1], sc[:, qi % 2, 0:(qi + 1) * P], AX.X, ALU.max, negate=True).then_inc(maxed.sem, 1)

            def weigh(b, h, qi):
                u = b * U + h * TPB + qi
                w = (qi + 1) * P
                dve.wait_ge(valued.sem, valued.at(u - 1))
                dve.wait_ge(turned.sem, turned.at(u + 1))
                nc.vector.tensor_tensor(probT[:, qi % 2, 0:w], tp[:, qi % 2, 0:w],
                                        weight[:, bass.ds(h, 1), 0:w].rearrange("p a t -> p (a t)"), ALU.mult).then_inc(copied.sem, 1)

            def head(b, h, ahead=True, behind=True):
                for qi in range(TPB):
                    if ahead:
                        largest(b, h, qi)
                    if behind:
                        weigh(b, h - 1, qi)

            with dve.Fori(0, B // 2) as pair:
                own.enter(pair, 2)
                for half in range(2):
                    b = pair * 2 + half
                    head(b, 0, behind=False)
                    with dve.Fori(1, A_HEADS) as h:
                        head(b, h)
                    head(b, A_HEADS, ahead=False)
                    dve.wait_ge(valued.sem, valued.at((b + 1) * U))
                    dve.wait_ge(normed.sem, normed.at(b))
                    own.link(nc.vector.reciprocal(inv[:, :, :], ob[:, half, :, :, A_HD]))
                    dst = Y[:, bass.ds(b * TPB, TPB), :].rearrange("p n (h c) -> p n h c", c=A_HD)
                    nc.vector.tensor_tensor(dst, ob[:, half, :, :, 0:A_HD], inv[:, :, :].unsqueeze(3).broadcast_to([P, TPB, A_HEADS, A_HD]),
                                            ALU.mult).then_inc(normed.sem, 1)
            own.leave(B // 2)
            own.close()

    for half in loaded:
        half.passed(PER_LOAD * (B // 2))
    for s in (scored, maxed, expd, turned, copied, valued):
        s.passed(U * B)
    normed.passed(B)


def attention_decay(nc, S, X, C, D, ident):
    with ExitStack() as ctx:
        room = Room(nc, ctx)
        Y, wo = room.sb("Y", [P, NT, P]), room.sb("wo", [P, 1, P])
        V1, weight = room.sb("V1", [P, NT, A_HEADS, A_HD + 1]), room.sb("weight", [P, A_HEADS, T])
        parts_q, parts_k = (nc.dram_tensor(n, (3, P, B, T), BF16, kind="Internal").ap() for n in ("parts_q", "parts_k"))
        big = S["big"]
        with ExitStack() as inner:
            iroom = Room(nc, inner)
            xnT, w = iroom.sb("xnT", [P, B * T]), iroom.sb("w", [P, 3 * P])
            drow, log_dist = iroom.sb("drow", [P, A_HEADS]), iroom.sb("log_dist", [P, T])
            with nc.Block() as block:
                @block.sync
                def _(sp):
                    sp.dma_start(w[:, :], D["at_w"]).then_inc(big.sem, 16)
                    sp.dma_start(drow[:, :], D["at_decay"].broadcast_to([P, A_HEADS])).then_inc(big.sem, 16)
                    sp.dma_start(log_dist[:, :], D["log_dist"]).then_inc(big.sem, 16)
                    sp.dma_start(wo[:, :, :], D["at_wo"].rearrange("p (a n) -> p a n", a=1)).then_inc(big.sem, 16)
            norm_transpose(nc, S, X, xnT, ident)
            with nc.Block() as block:
                @block.sync
                def _(sp):
                    sp.wait_ge(big.sem, big.at(4 * 16))
            big.passed(4 * 16)
            decay_project(nc, S, xnT, w, drow, log_dist, V1, weight, parts_q, parts_k)
        decay_heads(nc, S, parts_q, parts_k, V1, weight, Y, C, ident)
        project_add(nc, S, X, Y, wo, ident, 1)


def ffn0(nc, S, X, C, D, ident):
    E, F = FF0_EXPERTS, (FF0_EXPERTS + 1) * FF0_DIM
    with ExitStack() as ctx:
        room = Room(nc, ctx)
        Wg, Wu, Wd = room.sb("Wg", [P, F]), room.sb("Wu", [P, F]), room.sb("Wd", [P, F // P, P])
        Wr, gb = room.sb("Wr", [P, E]), room.sb("gb", [P, 2])
        xn, xnT = room.sb("xn", [P, NT, P]), room.sb("xnT", [P, B * T])
        row_in, row_out = room.sb("row_in", [P, 2 * NT], U32), room.sb("row_out", [P, 2 * NT], U32)
        gates = room.sb("gates", [P, 2 * NT])
        small, big = S["small"], S["big"]
        with nc.Block() as block:
            @block.sync
            def _(sp):
                sp.dma_start(gb[:, :], D["ff0_gb"]).then_inc(small.sem, 16)
                sp.dma_start(Wr[:, :], D["ff0_wr"]).then_inc(small.sem, 16)
                for dst, src in ((Wg, D["ff0_wg"]), (Wu, D["ff0_wu"])):
                    sp.dma_start(dst[:, :], src).then_inc(big.sem, 16)
                sp.dma_start(Wd[:, :, :], D["ff0_wd"]).then_inc(big.sem, 16)
                sp.wait_ge(small.sem, small.at(32))
        small.passed(32)
        norm_transpose(nc, S, X, xnT, ident, True, gb[:, 0:1], gb[:, 1:2], xn)
        dispatch(nc, S, xnT, Wr, C, row_in, row_out, gates)
        capacity_experts(nc, S, X, xn, xnT, Wg, Wu, Wd, gb, row_in, row_out, gates, D["inbox"], D["outbox"], ident, big.sem, big.at(48))
        big.passed(48)


def ffn1(nc, S, X, C, D, ident):
    E, F = FF1_EXPERTS, (FF1_EXPERTS + 1) * FF1_DIM
    FT = -(-F // P)
    with ExitStack() as ctx:
        room = Room(nc, ctx)
        Wg, Wu, Wd = room.sb("Wg", [P, FT * P]), room.sb("Wu", [P, FT * P]), room.sb("Wd", [P, FT, P])
        Wr, sel = room.sb("Wr", [P, E + 1]), room.sb("sel", [96, FT * P], BF16)
        xnT, gateT = room.sb("xnT", [P, B * T]), room.sb("gateT", [96, B * T], BF16)
        small, big, padded = S["small"], S["big"], S["wpad"]
        whole = F // P
        with nc.Block() as block:
            @block.sync
            def _(sp):
                sp.dma_start(Wr[:, :], D["ff1_wr"]).then_inc(small.sem, 16)
                sp.wait_ge(padded.sem, padded.at(1))
                sp.dma_start(Wg[:, 0:F], D["ff1_wg"]).then_inc(big.sem, 16)
                sp.dma_start(Wu[:, 0:F], D["ff1_wu"]).then_inc(big.sem, 16)
                sp.dma_start(sel[:, :], D["ff1_sel"]).then_inc(big.sem, 16)
                sp.dma_start(Wd[:, 0:whole, :], D["ff1_wd"][0:whole * P, :].rearrange("(f p) d -> p f d", p=P)).then_inc(big.sem, 16)
                sp.dma_start(Wd[0:F - whole * P, whole, :], D["ff1_wd"][whole * P:F, :]).then_inc(big.sem, 16)
                sp.wait_ge(small.sem, small.at(16))

            @block.gpsimd
            def _(pool):
                nc.gpsimd.memset(Wg[:, F:], 0.0)
                nc.gpsimd.memset(Wu[:, F:], 0.0)
                nc.gpsimd.memset(Wd[:, whole, :], 0.0).then_inc(padded.sem, 1)
        small.passed(16)
        padded.passed(1)
        norm_transpose(nc, S, X, xnT, ident)
        route(nc, S, xnT, Wr, E, True, None, gateT, C)
        experts(nc, S, X, xnT, gateT, sel, Wg, Wu, Wd, FT, ident, big.sem, big.at(80))
        big.passed(80)


SIGNALS = ["dve", "act", "pe", "var", "std", "norm", "turned", "copied", "pready", "padded", "have", "expd", "chosen",
           "counted", "parted", "proj", "silu", "hidden", "down", "small", "big", "wpad",
           "centred", "squared", "gated", "made", "qk_ready", "rotated", "vg_ready", "vg_copied",
           "picked", "scored", "decays", "rsummed", "rcopied", "aside",
           "w_lerped", "w_low", "w_tanhed", "w_high", "w_mixed", "w_px_full", "w_px_free", "w_decayed", "w_v_full",
           "w_v_used", "w_weighted", "w_summed", "w_bonused", "w_y_done", "w_e1",
           "a_weights", "a_projected", "a_rotated", "a_scored", "a_maxed", "a_expd", "a_turned", "a_copied", "a_valued", "a_normed",
           "qk_copied", "cut_ready", "cut_stored0", "cut_stored1", "loaded0", "loaded1",
           "m_fetched", "m_turned", "m_entered", "m_proj", "m_silu", "m_hidden", "m_down", "m_taken",
           "m_stored0", "m_stored1", "weighed", "a_scaled", "a_half"]


def mixed_model(nc, D, out):
    with ExitStack() as ctx:
        room = Room(nc, ctx)
        X = room.sb("X", [P, NT, P])
        ident = room.sb("ident", [P, P])
        C = {name: room.sb(name, shape, dt) for name, shape, dt in (
            ("identb", [P, P], BF16), ("upto", [P, P], BF16), ("ones", [P, P], BF16), ("above", [P, P], BF16),
            ("rank", [P, 8], F32), ("first_row", [P, 8], F32))}
        D = dict(D)
        for name in ("inbox", "outbox"):
            D[name] = nc.dram_tensor(name, (FF0_EXPERTS * FF0_CAPACITY, P), F32, kind="Internal").ap()
        cleared = ctx.enter_context(nc.semaphore("cleared"))
        start = ctx.enter_context(nc.semaphore("start"))
        stored = ctx.enter_context(nc.semaphore("stored"))
        S = {name: Signal(nc, ctx, "s_" + name) for name in SIGNALS}
        S.update({name: Signal(nc, ctx, "s_" + name, 0) for name in ("m_sent", "m_returned0", "m_returned1")})

        with nc.sbuf_tensor("zeros", [FF0_CAPACITY // 3, 3 * P], F32) as zeros, nc.Block() as block:
            @block.gpsimd
            def _(pool):
                nc.gpsimd.memset(zeros[:, :], 0.0).then_inc(cleared, 1)

            @block.sync
            def _(sp):
                for s in S.values():
                    if s.lead:
                        sp.sem_inc(s.sem, s.lead)
                sp.dma_start(X[:, :, :], D["x"].rearrange("(n p) d -> p n d", p=P)).then_inc(start, 16)
                sp.dma_start(ident[:, :], D["ident"]).then_inc(start, 16)
                for name in C:
                    sp.dma_start(C[name][:, :], D[name]).then_inc(start, 16)
                sp.wait_ge(cleared, 1)
                for k in range(FF0_EXPERTS):
                    sp.dma_start(D["inbox"][k * FF0_CAPACITY:(k + 1) * FF0_CAPACITY, :].rearrange("(p c) d -> p (c d)", c=3),
                                 zeros[:, :]).then_inc(start, 16)
                sp.wait_ge(start, 16 * (2 + len(C) + FF0_EXPERTS))

        steps = {1: attention_decay, 2: ffn0, 3: recurrent, 4: ffn0, 5: attention_mqa, 6: ffn1, 7: retention, 8: ffn1}
        for layer in LAYERS:
            steps[layer](nc, S, X, C, D, ident)

        with nc.Block() as block:
            @block.sync
            def _(sp):
                sp.dma_start(out.rearrange("(n p) d -> p n d", p=P), X[:, :, :]).then_inc(stored, 16)
                sp.wait_ge(stored, 16)


def constants():
    import numpy as np

    def bf(a):
        return (np.ascontiguousarray(a, np.float32).view(np.uint32) >> 16).astype(np.uint16)

    f32 = np.float32
    p = np.arange(P)
    c = {"ident": np.eye(P, dtype=f32), "identb": bf(np.eye(P)),
         "upto": bf(p[:, None] <= p[None, :]), "ones": bf(np.ones((P, P))),
         "above": bf(np.where(p[None, :] > p[:, None], MASKED, 0.0)),
         "first_row": np.broadcast_to(np.arange(8) * float(FF0_CAPACITY) - 1.0, (P, 8)).astype(f32),
         "rank": np.broadcast_to(8.0 - np.arange(8), (P, 8)).astype(f32)}
    for name, e, d in (("ff1_sel", FF1_EXPERTS + 1, FF1_DIM),):
        sel = np.zeros((96, -(-e * d // P) * P), f32)
        for part in range(3):
            for k in range(e):
                sel[32 * part + k, k * d:(k + 1) * d] = 1.0
        c[name] = bf(sel)
    i = np.arange(T)
    dist = np.maximum(i[None, :] - p[:, None], 0).astype(f32)
    c["log_dist"] = np.log1p(dist).astype(f32)
    inv = (1.0 / 10000.0 ** (np.arange(0, M_HD, 2, dtype=f32) / f32(M_HD))).astype(f32)
    freq = i.astype(f32)[:, None] * inv[None, :]
    cos, sin = np.cos(freq).astype(f32).T, np.sin(freq).astype(f32).T
    c["rope_cos"] = np.concatenate([cos] * 4, 0)
    c["rope_sin"] = np.concatenate([-sin, sin, -sin, sin], 0)
    c["rope_k_cos"], c["rope_k_sin"] = (c[n] * f32(M_HD ** -0.5) for n in ("rope_cos", "rope_sin"))
    half = P // 2
    sv = ((np.arange(0, P, 2, dtype=f32) + f32(0.4 * P)) / f32(1.4 * P)).astype(f32)
    scale = (sv[None, :] ** (i.astype(f32)[:, None] / f32(512.0))).astype(f32)
    invf = (1.0 / 10000.0 ** (np.arange(half, dtype=f32) / f32(half))).astype(f32)
    sinu = i.astype(f32)[:, None] * invf[None, :]
    si, co = np.sin(sinu).astype(f32), np.cos(sinu).astype(f32)
    sign = np.where(np.arange(P) % 2 == 0, -1.0, 1.0).astype(f32)
    s_, e_ = np.log(1.0 / 32.0), np.log(1.0 / 512.0)
    gamma = (1.0 - np.exp(np.linspace(s_, e_, R_HEADS).astype(f32))).astype(f32)
    ld = np.log(gamma).astype(f32)
    expo = np.maximum(i[:, None] - i[None, :], 0).astype(f32)
    tri = (i[:, None] >= i[None, :]).astype(f32)
    mask = np.exp(ld[:, None, None] * expo) * tri
    row = np.sqrt(mask.sum(-1))
    per = np.repeat(1.0 / row, R_DK, axis=0).T * f32(R_DK) ** -0.5
    for name, sc, extra in (("xq", scale, per), ("xk", 1.0 / scale, np.ones((T, P)))):
        c[name + "_cos"] = np.ascontiguousarray((np.repeat(co * sc, 2, -1) * extra).T.astype(f32))
        c[name + "_sin"] = np.ascontiguousarray((np.repeat(si * sc, 2, -1) * extra * sign[None, :]).T.astype(f32))
    causal = (i[None, :] >= p[:, None]).astype(f32)
    c["decays"] = np.ascontiguousarray((np.exp(ld[:, None, None] * dist[None]) * causal[None]).transpose(1, 0, 2).astype(f32))
    c["head_rows"] = np.ascontiguousarray((p[:, None] // R_DK == np.arange(R_HEADS)[None, :]).astype(f32))
    same = (p[:, None] // W_HD == p[None, :] // W_HD).astype(f32)
    c["head_sum"] = same
    c["head_to"] = np.ascontiguousarray(np.stack([same * (p[None, :] % W_HD == j) for j in range(W_HD)], 1).astype(f32))
    return c


def kernel(**inputs):
    import numpy as _np
    import concourse.bacc as _bacc
    from concourse import mybir as _mybir
    from concourse.bass_utils import run_bass_kernel_spmd as _run

    def a(name):
        return _np.asarray(inputs[name])

    cc = _np.ascontiguousarray
    data = {
        "x": a("L0_attn_a_x").reshape(B * T, P),
        "at_w": a("L0_attn_a_w_attn"), "at_wo": a("L0_attn_a_w_proj"), "at_decay": a("L0_attn_a_decay_raw").reshape(1, A_HEADS),
        "ff0_gb": cc(_np.stack([a("L0_ffn_ln_g"), a("L0_ffn_ln_b")], 1)), "ff0_wr": a("L0_ffn_Wr"),
        "ff0_wg": cc(_np.concatenate([a("L0_ffn_W1"), a("L0_ffn_W1s")[None]]).transpose(1, 0, 2).reshape(P, -1)),
        "ff0_wu": cc(_np.concatenate([a("L0_ffn_W3"), a("L0_ffn_W3s")[None]]).transpose(1, 0, 2).reshape(P, -1)),
        "ff0_wd": cc(_np.concatenate([a("L0_ffn_W2"), a("L0_ffn_W2s")[None]]).reshape(-1, P, P).transpose(1, 0, 2)),
        "ff1_wr": cc(_np.concatenate([a("L1_ffn_gate_w"), a("L1_ffn_shared_gate_w")]).T),
        "ff1_wg": cc(_np.concatenate([a("L1_ffn_w_gate"), a("L1_ffn_sw_gate")[None]]).transpose(1, 0, 2).reshape(P, -1)),
        "ff1_wu": cc(_np.concatenate([a("L1_ffn_w_up"), a("L1_ffn_sw_up")[None]]).transpose(1, 0, 2).reshape(P, -1)),
        "ff1_wd": cc(_np.concatenate([a("L1_ffn_w_down"), a("L1_ffn_sw_down")[None]]).reshape(-1, P)),
    }
    wq = a("L1_attn_a_Wq")
    h64 = _np.arange(M_HD)
    turn = _np.where(h64 < M_HD // 2, h64 + M_HD // 2, h64 - M_HD // 2)
    heads = wq.reshape(P, M_HEADS, M_HD)
    data["mq_wq"] = cc(_np.stack([heads, heads[:, :, turn]], 1).reshape(P, 2, M_HEADS // 2, P).transpose(2, 0, 1, 3))
    wk, wv = a("L1_attn_a_Wkv")[:, :M_HD], a("L1_attn_a_Wkv")[:, M_HD:]
    data["mq_wk"] = cc(_np.stack([_np.concatenate([wk, wk], 1), _np.concatenate([wk[:, turn]] * 2, 1)], 1))
    data["mq_wv"] = cc(wv)
    data["mq_wo"] = cc(a("L1_attn_a_Wo").reshape(M_HEADS * M_HD // P, P, P).transpose(1, 0, 2))
    pair = _np.arange(P) ^ 1
    w = a("L1_attn_b_w_qkv")
    bq = a("L1_attn_b_b_qkv")
    q, k = slice(0, P), slice(P, 2 * P)
    data["re_wqk"] = cc(_np.stack([w[:, q], w[:, q][:, pair], w[:, k], w[:, k][:, pair]], 1))
    data["re_bqk"] = cc(_np.stack([bq[q], bq[q][pair], bq[k], bq[k][pair]], 1))
    data["re_wv"], data["re_bv"] = cc(w[:, 2 * P:]), cc(bq[None, 2 * P:])
    data["re_wg"], data["re_bg"] = a("L1_attn_b_w_g"), a("L1_attn_b_b_g")[None]
    data["re_wp"] = cc(a("L1_attn_b_w_p").reshape(2, P, P).transpose(1, 0, 2))
    data["re_bp"] = a("L1_attn_b_b_p")[None]
    data["rw_la"] = cc(_np.stack([a(f"L0_attn_b_{n}_la").T for n in "rkvgd"], 1))
    data["rw_lb"] = cc(_np.stack([a(f"L0_attn_b_{n}_lb").T for n in "rkvgd"], 1))
    data["rw_cols"] = cc(_np.stack([a(f"L0_attn_b_{n}_ll") for n in "rkvgd"] + [a("L0_attn_b_xw"), a("L0_attn_b_u")], 1))
    data["rw_w"] = cc(_np.stack([a(f"L0_attn_b_{n}W").T for n in "rkvgo"], 1))
    vt = a("L0_attn_b_vW").T.reshape(P, W_HEADS, W_HD)
    data["rw_wvj"] = cc(_np.repeat(vt.transpose(0, 2, 1)[..., None], W_HD, -1).reshape(P, W_HD, P))
    data["rw_init"] = a("L0_attn_b_init_state").reshape(P, W_HD)
    data["rw_ln"] = cc(_np.stack([a("L0_attn_b_ln_w"), a("L0_attn_b_ln_b")]).reshape(1, 2 * W_HD))
    data.update(constants())

    nc = _bacc.Bacc("TRN2", target_bir_lowering=False, num_devices=1)
    arrays, aps = {}, {}
    for name, v in data.items():
        v = cc(v)
        arrays[f"in_{name}"] = v
        aps[name] = nc.dram_tensor(f"in_{name}", v.shape, _mybir.dt.from_np(v.dtype), kind="ExternalInput").ap()
        if v.dtype == _np.uint16:
            aps[name] = aps[name].bitcast(BF16)
    out = nc.dram_tensor("out_x", (B * T, P), F32, kind="ExternalOutput").ap()
    mixed_model(nc, aps, out)
    r = _run(nc, [arrays], core_ids=[0])
    return r.results[0]["out_x"].reshape(B, T, P)
```
